# Optimizing a Trainium2 kernel written in Bass

```python
import numpy as np
import jax
import jax.numpy as jnp

def _softmax(x, axis=-1):
    return jax.nn.softmax(x, axis=axis)

def _gelu(x):
    return jax.nn.gelu(x, approximate=True)

def _silu(x):
    return jax.nn.silu(x)

def _sigmoid(x):
    return jax.nn.sigmoid(x)

def _layernorm(x, axis=-1, eps=1e-05):
    m = jnp.mean(x, axis=axis, keepdims=True)
    v = jnp.var(x, axis=axis, keepdims=True)
    return (x - m) / jnp.sqrt(v + eps)

def _scatter_add(tgt, idx, src, axis=0):
    return tgt.at[idx].add(src)

def _segment_sum(src, seg, n):
    return jax.ops.segment_sum(src, seg, n)
kernel_name = 'mk_lm_tower_d1_tok_ids256_r4_71a524'

def setup_inputs(seed: int=0):
    np.random.seed(seed)
    _w = jnp.asarray

    def _rec_inputs():
        import jax
        import jax.numpy as jnp
        _rk = jax.random.key(seed)
        x = jax.random.randint(jax.random.fold_in(_rk, 1), (32, 512), 0, 75, jnp.int32)
        mask_BS_i0_1 = jnp.where(jnp.ones((32, 512), dtype=bool), 0, 1).astype(jnp.int32)
        itok_BS_0_299 = jax.random.randint(jax.random.fold_in(_rk, 22), (32, 512), 0, 75, jnp.int32)
        return (x, mask_BS_i0_1, itok_BS_0_299)
    x, mask_BS_i0_1, itok_BS_0_299 = _rec_inputs()

    def _L0_tok_setup():
        import jax, jax.numpy as jnp
        import numpy as np
        NUM_SKILLS = 75
        EMB_SIZE = 64
        CURVE_DIM = 64
        B, S = (128, 200)

        def _running_counts(q, r):
            b, s = q.shape
            rows = jnp.arange(b)
            valid = (q >= 0) & (q < NUM_SKILLS)
            idx = jnp.clip(q, 0, NUM_SKILLS - 1)

            def step(carry, xs):
                att, cor = carry
                it, rt, vt = xs
                att = att.at[rows, it].add(vt.astype(jnp.int32))
                cor = cor.at[rows, it].add((rt * vt).astype(jnp.int32))
                return ((att, cor), (att[rows, it], cor[rows, it]))
            init = (jnp.zeros((b, NUM_SKILLS), jnp.int32), jnp.zeros((b, NUM_SKILLS), jnp.int32))
            xs = (idx.T, r.T, valid.T)
            _, (a_t, c_t) = jax.lax.scan(step, init, xs)
            return (a_t.T.astype(jnp.float32), c_t.T.astype(jnp.float32), valid)
        key = jax.random.key(seed)
        ks = jax.random.split(key, 11)
        d3 = CURVE_DIM // 3
        dm = d3 + CURVE_DIM % 3
        return {'q': jax.random.randint(ks[0], (B, S), 0, NUM_SKILLS, dtype=jnp.int32), 'r': jax.random.randint(ks[1], (B, S), 0, 2, dtype=jnp.int32), 'qry': jax.random.randint(ks[2], (B, S), 0, NUM_SKILLS, dtype=jnp.int32), 'skill_w': jax.random.normal(ks[3], (d3,), jnp.float32), 'skill_b': jax.random.normal(ks[4], (d3,), jnp.float32), 'att_w': jax.random.normal(ks[5], (d3,), jnp.float32), 'att_b': jax.random.normal(ks[6], (d3,), jnp.float32), 'mast_w': jax.random.normal(ks[7], (dm,), jnp.float32), 'mast_b': jax.random.normal(ks[8], (dm,), jnp.float32), 'proj_w': jax.random.normal(ks[9], (EMB_SIZE, CURVE_DIM), jnp.float32) * 0.05, 'proj_b': jax.random.normal(ks[10], (EMB_SIZE,), jnp.float32)}
    _L0_tok_all = _L0_tok_setup()
    _L0_tok_in = {k: v for k, v in _L0_tok_all.items() if k in ('skill_w', 'skill_b', 'att_w', 'att_b', 'mast_w', 'mast_b', 'proj_w', 'proj_b')}
    del _L0_tok_all

    def _L0_attn_setup():
        import jax, jax.numpy as jnp
        import numpy as np
        U_DECAY = 0.97
        X_DECAY = 0.97
        LN_EPS = 1e-05
        L1_EPS = 1e-12

        def _ln(x):
            m = jnp.mean(x, axis=-1, keepdims=True)
            v = jnp.mean((x - m) ** 2, axis=-1, keepdims=True)
            return (x - m) * jax.lax.rsqrt(v + LN_EPS)
        key = jax.random.key(seed)
        k0, k1, k2, k3 = jax.random.split(key, 4)
        B, T, d, n = (8, 64, 64, 256)
        embeddings = jax.random.normal(k0, (B, T, d), dtype=jnp.float32)
        E = jax.random.normal(k1, (d, n), dtype=jnp.float32) / n ** 0.5
        Dx = jax.random.normal(k2, (n, d), dtype=jnp.float32) / d ** 0.5
        Dy = jax.random.normal(k3, (n, d), dtype=jnp.float32) / d ** 0.5
        return {'embeddings': embeddings, 'E': E, 'Dx': Dx, 'Dy': Dy}
    _L0_attn_all = _L0_attn_setup()
    _L0_attn_in = {k: v for k, v in _L0_attn_all.items() if k in ('E', 'Dx', 'Dy')}
    del _L0_attn_all

    def _L0_ffn_setup():
        import jax, jax.numpy as jnp
        import numpy as np
        E = 8
        K = 2
        D = 64
        H = 128
        DOUT = 64
        EPS = 1e-05
        key = jax.random.key(seed)
        ks = jax.random.split(key, 9)
        s = 0.02
        return {'x': jax.random.normal(ks[0], (4, 2048, D), jnp.float32), 'gamma': 1.0 + 0.05 * jax.random.normal(ks[1], (D,), jnp.float32), 'beta': 0.05 * jax.random.normal(ks[2], (D,), jnp.float32), 'Wr': 0.01 * jax.random.normal(ks[3], (D, E), jnp.float32), 'br': jnp.zeros((E,), jnp.float32), 'W1': s * jax.random.normal(ks[4], (E, D, H), jnp.float32), 'b1': s * jax.random.normal(ks[5], (E, H), jnp.float32), 'W2': s * jax.random.normal(ks[6], (E, H, DOUT), jnp.float32), 'b2': s * jax.random.normal(ks[7], (E, DOUT), jnp.float32)}
    _L0_ffn_all = _L0_ffn_setup()
    _L0_ffn_in = {k: v for k, v in _L0_ffn_all.items() if k in ('gamma', 'beta', 'Wr', 'br', 'W1', 'b1', 'W2', 'b2')}
    del _L0_ffn_all
    return {'x': x, 'mask_BS_i0_1': mask_BS_i0_1, 'itok_BS_0_299': itok_BS_0_299, 'L0_tok_skill_w': _L0_tok_in['skill_w'], 'L0_tok_skill_b': _L0_tok_in['skill_b'], 'L0_tok_att_w': _L0_tok_in['att_w'], 'L0_tok_att_b': _L0_tok_in['att_b'], 'L0_tok_mast_w': _L0_tok_in['mast_w'], 'L0_tok_mast_b': _L0_tok_in['mast_b'], 'L0_tok_proj_w': _L0_tok_in['proj_w'], 'L0_tok_proj_b': _L0_tok_in['proj_b'], 'L0_attn_E': _L0_attn_in['E'], 'L0_attn_Dx': _L0_attn_in['Dx'], 'L0_attn_Dy': _L0_attn_in['Dy'], 'L0_ffn_gamma': _L0_ffn_in['gamma'], 'L0_ffn_beta': _L0_ffn_in['beta'], 'L0_ffn_Wr': _L0_ffn_in['Wr'], 'L0_ffn_br': _L0_ffn_in['br'], 'L0_ffn_W1': _L0_ffn_in['W1'], 'L0_ffn_b1': _L0_ffn_in['b1'], 'L0_ffn_W2': _L0_ffn_in['W2'], 'L0_ffn_b2': _L0_ffn_in['b2']}

def reference(x, mask_BS_i0_1, itok_BS_0_299, L0_tok_skill_w, L0_tok_skill_b, L0_tok_att_w, L0_tok_att_b, L0_tok_mast_w, L0_tok_mast_b, L0_tok_proj_w, L0_tok_proj_b, L0_attn_E, L0_attn_Dx, L0_attn_Dy, L0_ffn_gamma, L0_ffn_beta, L0_ffn_Wr, L0_ffn_br, L0_ffn_W1, L0_ffn_b1, L0_ffn_W2, L0_ffn_b2):
    import jax
    import jax.numpy as jnp

    def _L0_tok_ref(q, r, qry, skill_w, skill_b, att_w, att_b, mast_w, mast_b, proj_w, proj_b):
        import jax, jax.numpy as jnp
        import numpy as np
        NUM_SKILLS = 75
        EMB_SIZE = 64
        CURVE_DIM = 64
        B, S = (128, 200)

        def _running_counts(q, r):
            b, s = q.shape
            rows = jnp.arange(b)
            valid = (q >= 0) & (q < NUM_SKILLS)
            idx = jnp.clip(q, 0, NUM_SKILLS - 1)

            def step(carry, xs):
                att, cor = carry
                it, rt, vt = xs
                att = att.at[rows, it].add(vt.astype(jnp.int32))
                cor = cor.at[rows, it].add((rt * vt).astype(jnp.int32))
                return ((att, cor), (att[rows, it], cor[rows, it]))
            init = (jnp.zeros((b, NUM_SKILLS), jnp.int32), jnp.zeros((b, NUM_SKILLS), jnp.int32))
            xs = (idx.T, r.T, valid.T)
            _, (a_t, c_t) = jax.lax.scan(step, init, xs)
            return (a_t.T.astype(jnp.float32), c_t.T.astype(jnp.float32), valid)
        attempts, correct, valid = _running_counts(q, r)
        mastery = correct / jnp.maximum(attempts, 1.0)
        skill_f = q.astype(jnp.float32)
        s_enc = skill_f[..., None] * skill_w + skill_b
        n_enc = attempts[..., None] * att_w + att_b
        m_enc = mastery[..., None] * mast_w + mast_b
        tup = jnp.concatenate([s_enc, n_enc, m_enc], axis=-1)
        traj = jnp.einsum('bsc,ec->bse', tup, proj_w) + proj_b
        return jnp.where(valid[..., None], traj, 0.0)

    def _L0_attn_ref(embeddings, E, Dx, Dy):
        import jax, jax.numpy as jnp
        import numpy as np
        U_DECAY = 0.97
        X_DECAY = 0.97
        LN_EPS = 1e-05
        L1_EPS = 1e-12

        def _ln(x):
            m = jnp.mean(x, axis=-1, keepdims=True)
            v = jnp.mean((x - m) ** 2, axis=-1, keepdims=True)
            return (x - m) * jax.lax.rsqrt(v + LN_EPS)
        B, T, d = embeddings.shape
        n = E.shape[1]

        def step(carry, v_prev):
            x_state, rho = carry
            x_update = jax.nn.relu(v_prev @ Dx.T)
            x_t = X_DECAY * x_state + x_update
            x_t = x_t / jnp.maximum(jnp.sum(jnp.abs(x_t), axis=-1, keepdims=True), L1_EPS)
            a_star = jnp.einsum('bdn,bn->bd', rho, x_t)
            y_core = _ln(a_star) @ Dy.T
            y_t = jax.nn.relu(y_core) * jax.nn.relu(x_t)
            v_star = _ln(y_t @ E.T)
            rho_t = U_DECAY * rho + _ln(v_prev)[:, :, None] * x_t[:, None, :]
            return ((x_t, rho_t), v_star)
        x0 = jnp.zeros((B, n), dtype=embeddings.dtype)
        rho0 = jnp.zeros((B, d, n), dtype=embeddings.dtype)
        _, vs = jax.lax.scan(step, (x0, rho0), jnp.swapaxes(embeddings, 0, 1))
        return jnp.swapaxes(vs, 0, 1)

    def _L0_ffn_ref(x, gamma, beta, Wr, br, W1, b1, W2, b2):
        import jax, jax.numpy as jnp
        import numpy as np
        E = 8
        K = 2
        D = 64
        H = 128
        DOUT = 64
        EPS = 1e-05
        mu = jnp.mean(x, axis=-1, keepdims=True)
        var = jnp.mean(jnp.square(x - mu), axis=-1, keepdims=True)
        xn = (x - mu) * jax.lax.rsqrt(var + EPS) * gamma + beta
        logits = jnp.einsum('bsd,de->bse', xn, Wr) + br
        top_vals, top_idx = jax.lax.top_k(logits, K)
        w = jax.nn.softmax(top_vals, axis=-1)
        w_full = jnp.einsum('bsk,bske->bse', w, jax.nn.one_hot(top_idx, E, dtype=w.dtype))
        y = jnp.zeros(x.shape[:-1] + (DOUT,), x.dtype)
        for e in range(E):
            h = jax.nn.gelu(jnp.einsum('bsd,dh->bsh', xn, W1[e]) + b1[e], approximate=False)
            y_e = jnp.einsum('bsh,hd->bsd', h, W2[e]) + b2[e]
            y = y + y_e * w_full[..., e, None]
        return y
    h = _L0_tok_ref(x, mask_BS_i0_1, itok_BS_0_299, L0_tok_skill_w, L0_tok_skill_b, L0_tok_att_w, L0_tok_att_b, L0_tok_mast_w, L0_tok_mast_b, L0_tok_proj_w, L0_tok_proj_b)
    h = h + _L0_attn_ref(_layernorm(h, axis=-1), L0_attn_E, L0_attn_Dx, L0_attn_Dy)
    h = h + _L0_ffn_ref(_layernorm(h, axis=-1), L0_ffn_gamma, L0_ffn_beta, L0_ffn_Wr, L0_ffn_br, L0_ffn_W1, L0_ffn_b1, L0_ffn_W2, L0_ffn_b2)
    return h

_drawn_inputs = setup_inputs


def setup_inputs(seed=0):
    import zlib

    import numpy as np

    out = dict(_drawn_inputs(seed))
    spreads = {'L0_ffn_br': (0.0, 0.8)}
    factors = {'L0_tok_skill_b': 3.047,
     'L0_tok_att_b': 3.597,
     'L0_tok_mast_b': 3.197,
     'L0_ffn_gamma': 8.0,
     'L0_ffn_beta': 8.0,
     'L0_ffn_Wr': 8.0,
     'L0_ffn_W1': 8.0,
     'L0_ffn_b1': 47.839,
     'L0_ffn_W2': 8.0,
     'L0_ffn_b2': 56.629}
    for name, (base, spread) in spreads.items():
        noise = np.random.default_rng([zlib.crc32(name.encode()), seed]).standard_normal(out[name].shape)
        drawn = base * np.exp(spread * noise) if base else spread * noise
        out[name] = jnp.asarray(drawn.astype(out[name].dtype))
    for name, factor in factors.items():
        out[name] = (out[name] * factor).astype(out[name].dtype)
    return out
```

```python
from contextlib import ExitStack

import numpy as np

import concourse.bass as bass
from concourse import mybir

F32 = mybir.dt.float32
F16 = mybir.dt.float16
BF16 = mybir.dt.bfloat16
I32 = mybir.dt.int32
U32 = mybir.dt.uint32
ALU = mybir.AluOpType
ACT = mybir.ActivationFunctionType
AX_X = mybir.AxisListType.X

P = 128
B, S = 32, 512
C = S // P
J = B * C
D = 64
NS = 256
NK = NS // P
E = 8
HID = 128
NP = E // 2
SKILLS = 75
D3 = 21
NF = 4
PIECES = 3
KF = NF * PIECES * PIECES
DECAY = 0.97
EPS = 1e-5
L1_EPS = 1e-12
RSQRT_SEED = float(0x5F3759DF)
OFF = [0, 512, 896, 1152]
WIDE = [S - P * sc for sc in range(C)]
CAUSAL = OFF[-1] + WIDE[-1]
GROUP = 8
NG = J // GROUP
EXP_MASK = 0x7F800000

N_ATT = 56
N_MLP = 16


class Steps:

    def __init__(self, eng, sem, base=0):
        self.eng, self.sem, self.base, self.n = eng, sem, base, 0

    def done(self, instruction):
        instruction.then_inc(self.sem, 1)
        self.n += 1

    def last(self):
        self.eng.wait_ge(self.sem, self.base + self.n)


def wait(eng, sem, value):
    if not isinstance(value, int) or value > 0:
        eng.wait_ge(sem, value)


def program(nc, x, r, skill_w, skill_b, att_w, att_b, mast_w, mast_b, proj_w, proj_b, Ea, Dx, Dy, gamma, beta,
            Wr, br, W1, b1, W2, b2, ident, masks, decays, out):
    with ExitStack() as ctx:
        def sb(name, shape, dt=F32):
            return ctx.enter_context(nc.sbuf_tensor(name, shape, dt))

        def sem(name):
            return ctx.enter_context(nc.semaphore(name))

        def scratch(name, shape, dt):
            return nc.dram_tensor(name, shape, dt, kind="Internal").ap()

        bank = [ctx.enter_context(nc.psum_tensor(f"bank{n}", [P, 512], F32)) for n in range(8)]

        skill_row_d = scratch("skill_row_d", (J, P), BF16)
        upd_sum_d = scratch("upd_sum_d", (J, P), F32)
        recip_d = scratch("recip_d", (B, S), F32)
        factor_d = scratch("factor_d", (B, S), F32)
        table_d = scratch("table_d", (NF, PIECES, D + NS), BF16)

        xi, ri = sb("xi", [J, P], I32), sb("ri", [J, P], I32)
        xf, rf = sb("xf", [J, P]), sb("rf", [J, P])
        ident_f, mask_sb = sb("ident_f", [P, P]), sb("mask_sb", [P, 2 * P])
        causal_f = mask_sb[:, P:2 * P]
        ident_h, ident_b = sb("ident_h", [P, P], F16), sb("ident_b", [P, P], BF16)
        upto_b = sb("upto_b", [P, P], BF16)
        dec = sb("dec", [P, 2 * C + E])
        fold_f = sb("fold_f", [P, D])
        skill_T, right_T = sb("skill_T", [P, J]), sb("right_T", [P, J])
        skill_row = sb("skill_row", [J, P], BF16)
        right_parts = sb("right_parts", [P, J, 4], BF16)
        ones_row = sb("ones_row", [1, NF])
        s4, proj_sb, projT = sb("s4", [D, NF]), sb("proj_sb", [D, D]), sb("projT", [D, D])
        projb = sb("projb", [1, D])
        table = sb("table", [NF, D + NS])
        table_c, table_cT = sb("table_c", [NF, D]), sb("table_cT", [D, NF])
        table_m = sb("table_m", [NF, 1])
        table_p = sb("table_p", [NF, PIECES, D + NS], BF16)
        table_r = sb("table_r", [NF, D + NS])
        table_k = sb("table_k", [P, D + NS], BF16)
        dx_sb, dxT = sb("dx_sb", [P, NK, D]), sb("dxT", [D, NS])
        dy_sb, dy_scale = sb("dy_sb", [P, NK, D]), sb("dy_scale", [P, 2 * NK])
        dy_p = sb("dy_p", [P, 2, NK, 2, D], F16)
        dyT = sb("dyT", [P, 2, NS], F16)
        e_sb, eT, e_mean = sb("e_sb", [D, NS]), sb("eT", [P, NK, D]), sb("e_mean", [P, NK])
        gam2, bet = sb("gam2", [P, 1]), sb("bet", [D, 1])
        bet_wide = sb("bet_wide", [D, P])
        w1_sb, w1g = sb("w1_sb", [D, E, HID]), sb("w1g", [D, E, HID])
        w1T = sb("w1T", [HID, E, D])
        w1_scale, w1_inv = sb("w1_scale", [HID, E]), sb("w1_inv", [HID, E])
        w1_p = sb("w1_p", [HID, 2, E, 2, D], F16)
        w1k = sb("w1k", [P, 2, E, HID], F16)
        b1_sb, b1T = sb("b1_sb", [E, HID]), sb("b1T", [HID, E])
        w2_sb = sb("w2_sb", [HID, E, D])
        b2_sb, b2_pair = sb("b2_sb", [NP, P]), sb("b2_pair", [P, NP])
        wr_sb, wr_g, wr_r = sb("wr_sb", [P, E]), sb("wr_g", [P, E]), sb("wr_r", [P, E])
        wr_p = sb("wr_p", [P, PIECES, E], BF16)
        br_sb = sb("br_sb", [P, E])
        sel = sb("sel", [2 * E, NP, P], F16)

        attempts = sb("attempts", [P, J])
        valid, feat_t = sb("valid", [P, J]), sb("feat_t", [P, J])
        feat = sb("feat", [P, NF, J])
        feat_r = sb("feat_r", [P, NF, J])
        stat_h0 = sb("stat_h0", [P, J, 6])
        mean_h0, var_h0 = sb("mean_h0", [P, J]), sb("var_h0", [P, J])
        rstd, u_scale = sb("rstd", [P, J]), sb("u_scale", [P, J])
        newton = sb("newton", [P, J])
        upd_sum, recip_T = sb("upd_sum", [P, J]), sb("recip_T", [P, J])
        upd_sum_T, recip_j = sb("upd_sum_T", [J, P]), sb("recip_j", [J, P])

        h_all = sb("h_all", [P, J * D])
        rows_or_scaled = sb("rows_or_scaled", [P, J * P], BF16)
        feat_parts = sb("feat_parts", [P, J, P], BF16)
        feat_k = sb("feat_k", [P, J * P], BF16)
        same = sb("same", [P, 2, CAUSAL], BF16)

        def over(array, at, *shape):
            n = int(np.prod(shape))
            flat = array.bitcast(F32)[:, at:at + n]
            return flat.rearrange("p (a b) -> p a b", a=shape[0]) if len(shape) == 2 else flat

        row_u, row_w, row_nz, row_any, row_one, row_d = [over(feat_k[0:B, :], n * S, S) for n in range(6)]
        parts_flat = feat_parts[:].rearrange("p j n -> p (j n)")
        relu_b = over(parts_flat, 0, NK, S)
        factor = sb("factor", [P, S])
        xs = over(parts_flat, 2 * S, NK, S)
        pm = over(parts_flat, 9 * S, CAUSAL)
        ub, ub_t = sb("ub", [P, C, D]), sb("ub_t", [P, C, D])
        st_a, t_a = sb("st_a", [P, C, 6]), sb("t_a", [P, 8, C])
        an = sb("an", [P, C, D])
        a_p, aT = sb("a_p", [P, C, 2 * D], F16), sb("aT", [P, S], F16)
        ys = over(parts_flat, 4 * S, NK, S)
        st_z, t_z = sb("st_z", [P, C, 6]), sb("t_z", [P, 6, C])
        st_h, t_h = sb("st_h", [P, C, 6]), sb("t_h", [P, 6, C])
        h_mean, h_scale = sb("h_mean", [P, C]), sb("h_scale", [P, C])
        xc, xc_t = sb("xc", [P, C, D]), sb("xc_t", [P, C, D])
        x_p, xT = sb("x_p", [P, C, 2 * D], F16), sb("xT", [P, S], F16)
        lg, top, top_i = sb("lg", [P, C, E]), sb("top", [P, C, E]), sb("top_i", [P, C, E], U32)
        gap, tanh_g, wgt = sb("gap", [P, C]), sb("tanh_g", [P, C]), sb("wgt", [P, 2, C])
        pick = sb("pick", [P, 2, C, E])
        w_p, wT = sb("w_p", [P, C, 2 * E], F16), sb("wT", [2 * E, S], F16)
        wb = over(feat_k[:], E * S, NP, S)
        hid = over(feat_k[:], 0, E, S)
        tm = over(feat_k[:], (E + NP) * S, NP, S)
        half, acc = over(parts_flat, 6 * S, 2, S), over(parts_flat, 8 * S, S)
        o_sb = sb("o_sb", [P, C, D])

        ld_x, ld_c, ld_w, ld_w2 = sem("ld_x"), sem("ld_c"), sem("ld_w"), sem("ld_w2")
        ld_rows = [sem(f"ld_rows{n}") for n in range(4)]
        ld_table, ld_row_u, ld_recip, ld_factor = sem("ld_table"), sem("ld_row_u"), sem("ld_recip"), sem("ld_factor")
        st_rows, st_table, st_upd, st_recip, st_out = (sem("st_rows"), sem("st_table"), sem("st_upd"),
                                                       sem("st_recip"), sem("st_out"))
        zeroed, table_zeroed = sem("zeroed"), sem("table_zeroed")
        ints_f, rows_ready, sel_ready = sem("ints_f"), sem("rows_ready"), sem("sel_ready")
        ids_ready, gammas_in, wide_beta = sem("ids_ready"), sem("gammas_in"), sem("wide_beta")
        pe_tok_T, pe_wT, pe_bias = sem("pe_tok_T"), sem("pe_wT"), sem("pe_bias")
        projT_in, pe_tab, tab_c_in, pe_tabT, tabT_in, pe_g, table_ready = (
            sem("projT_in"), sem("pe_tab"), sem("tab_c_in"), sem("pe_tabT"), sem("tabT_in"), sem("pe_g"),
            sem("table_ready"))
        parts_in, pe_parts, weights_in = sem("parts_in"), sem("pe_parts"), sem("weights_in")
        dve_set = sem("dve_set")
        tok_in = sem("tok_in")
        same_in, pe_counts = sem("same_in"), sem("pe_counts")
        feats_in, pe_featT, featT_in = sem("feats_in"), sem("pe_featT"), sem("featT_in")
        pe_h0, pe_g2 = sem("pe_h0"), sem("pe_g2")
        h0_in, sum_a, sum_v, h0_stats = sem("h0_in"), sem("sum_a"), sem("sum_v"), sem("h0_stats")
        upd_in, pe_updT, updT_in, pe_recT = sem("upd_in"), sem("pe_updT"), sem("updT_in"), sem("pe_recT")
        scalars_in, recip_ready = sem("scalars_in"), sem("recip_ready")
        scaled_in, pe_scT, scT_in = sem("scaled_in"), sem("pe_scT"), sem("scT_in")
        pe_pre, pe_s, pe_a, pe_aT, pe_y, pe_z = (sem("pe_pre"), sem("pe_s"), sem("pe_a"), sem("pe_aT"), sem("pe_y"),
                                                 sem("pe_z"))
        pe_xT, pe_lg, pe_hid, pe_zz, pe_wT2, pe_wb, pe_fold = (
            sem("pe_xT"), sem("pe_lg"), sem("pe_hid"), sem("pe_zz"), sem("pe_wT2"), sem("pe_wb"), sem("pe_fold"))
        ac_relu, ac_off, ac_ah, ac_aT, ac_xh, ac_xT = (sem("ac_relu"), sem("ac_off"), sem("ac_ah"), sem("ac_aT"),
                                                       sem("ac_xh"), sem("ac_xT"))
        ac_gelu, ac_tanh, ac_wT, ac_wb = sem("ac_gelu"), sem("ac_tanh"), sem("ac_wT"), sem("ac_wb")
        dv_x, dv_diag, dv_an, dv_y, dv_h = sem("dv_x"), sem("dv_diag"), sem("dv_an"), sem("dv_y"), sem("dv_h")
        dv_gap, dv_w, dv_tm, dv_out, dv_lg = sem("dv_gap"), sem("dv_w"), sem("dv_tm"), sem("dv_out"), sem("dv_lg")
        att_steps, mlp_steps, pool_steps = sem("att_steps"), sem("mlp_steps"), sem("pool_steps")
        dv_passed = sem("dv_passed")
        po_in, po_ub, po_al, po_xt, po_xc = sem("po_in"), sem("po_ub"), sem("po_al"), sem("po_xt"), sem("po_xc")
        po_xl, po_half, po_acc = sem("po_xl"), sem("po_half"), sem("po_acc")

        mA, mB, tp, az, hA, hB, zb, ly = bank
        n_bank, h_bank = [mA, mB], [hA, hB]
        tp_h = tp[:, :].bitcast(F16)
        ly_lg = ly[:, 0:C * PIECES * E]
        ly_w = ly[:, 256:512].bitcast(F16)
        ly_y = ly[:, 256:512]
        az_a = az[:, 0:C * D].rearrange("p (c d) -> p c d", c=C)
        az_z = az[:, C * D:2 * C * D].rearrange("p (c d) -> p c d", c=C)
        counts = bank[0][:, :].rearrange("p (j k) -> p j k", k=4)

        def wide(ap, n):
            return ap.unsqueeze(2).to_broadcast([ap.shape[0], ap.shape[1], n])

        def h_of(b):
            return h_all[:, bass.ds(b * C * D, C * D)].rearrange("p (c d) -> p c d", c=C)

        block = ctx.enter_context(nc.Block())

        @block.sync
        def _(sp):
            sp.dma_start(xi[:], x.rearrange("b (c p) -> (b c) p", p=P)).then_inc(ld_x, 16)
            sp.dma_start(ri[:], r.rearrange("b (c p) -> (b c) p", p=P)).then_inc(ld_x, 16)
            sp.dma_start(ident_f[:], ident).then_inc(ld_c, 16)
            sp.dma_start(mask_sb[:], masks).then_inc(ld_c, 16)
            sp.dma_start(dec[:], decays).then_inc(ld_c, 16)
            sp.dma_start(proj_sb[:], proj_w).then_inc(ld_w, 16)
            sp.dma_start(projb[:], proj_b.unsqueeze(0)).then_inc(ld_w, 16)
            sp.wait_ge(zeroed, 1)
            sp.dma_start(s4[0:D3, 0:1], skill_w.unsqueeze(1)).then_inc(ld_w, 16)
            sp.dma_start(s4[D3:2 * D3, 1:2], att_w.unsqueeze(1)).then_inc(ld_w, 16)
            sp.dma_start(s4[2 * D3:D, 2:3], mast_w.unsqueeze(1)).then_inc(ld_w, 16)
            sp.dma_start(s4[0:D3, 3:4], skill_b.unsqueeze(1)).then_inc(ld_w, 16)
            sp.dma_start(s4[D3:2 * D3, 3:4], att_b.unsqueeze(1)).then_inc(ld_w, 16)
            sp.dma_start(s4[2 * D3:D, 3:4], mast_b.unsqueeze(1)).then_inc(ld_w, 16)
            sp.dma_start(dx_sb[:], Dx.rearrange("(k p) d -> p k d", p=P)).then_inc(ld_w, 16)
            sp.wait_ge(rows_ready, 1)
            sp.dma_start(skill_row_d, skill_row[:]).then_inc(st_rows, 16)
            sp.wait_ge(st_rows, 16)
            rows = skill_row_d.rearrange("j p -> (j p)").unsqueeze(0)
            n = J * P // 4
            for q in range(4):
                sp.dma_start(rows_or_scaled[:, q * n:(q + 1) * n],
                             rows[:, q * n:(q + 1) * n].to_broadcast([P, n])).then_inc(ld_rows[q], 16)
            sp.wait_ge(table_ready, 1)
            sp.dma_start(table_d, table_p[:]).then_inc(st_table, 16)
            sp.wait_ge(st_table, 16)
            sp.wait_ge(table_zeroed, 1)
            for g in range(PIECES):
                for piece in range(PIECES):
                    row = NF * (PIECES * g + piece)
                    sp.dma_start(table_k[row:row + NF, :], table_d[:, g, :]).then_inc(ld_table, 16)
            sp.wait_ge(updT_in, 1)
            sp.dma_start(upd_sum_d, upd_sum_T[:]).then_inc(st_upd, 16)
            sp.wait_ge(st_upd, 16)
            sp.dma_start(row_u, upd_sum_d.rearrange("(b c) p -> b (c p)", c=C)).then_inc(ld_row_u, 16)
            sp.wait_ge(scalars_in, 1)
            sp.dma_start(recip_d, row_w).then_inc(st_recip, 16)
            sp.dma_start(factor_d, row_nz).then_inc(st_recip, 16)
            sp.wait_ge(st_recip, 32)
            sp.dma_start(recip_j[:], recip_d.rearrange("b (c p) -> (b c) p", p=P)).then_inc(ld_recip, 16)

            def load_factor(b):
                wait(sp, dv_x, 2 * b)
                sp.dma_start(factor[:], factor_d[bass.ds(b, 1), :].to_broadcast([P, S])).then_inc(ld_factor, 16)

            def store(b):
                sp.wait_ge(dv_out, b + 1)
                sp.dma_start(out[bass.ds(b, 1)].rearrange("o (c p) d -> p (o c) d", p=P), o_sb[:]).then_inc(st_out, 16)

            load_factor(0)
            load_factor(1)
            load_factor(2)
            with sp.Fori(2, B - 1) as i:
                store(i - 2)
                load_factor(i + 1)
            for b in range(B - 3, B):
                store(b)
            sp.wait_ge(st_out, 16 * B)

        @block.gpsimd
        def _(pool):
            pool.memset(s4[:], 0.0).then_inc(zeroed, 1)
            pool.dma_start(gam2[0:D, :], gamma.unsqueeze(1)).then_inc(ld_w2, 16)
            pool.dma_start(gam2[D:P, :], gamma.unsqueeze(1)).then_inc(ld_w2, 16)
            pool.dma_start(bet[:], beta.unsqueeze(1)).then_inc(ld_w2, 16)
            pool.dma_start(w1_sb[:], W1.rearrange("e d h -> d e h")).then_inc(ld_w2, 16)
            pool.dma_start(b1_sb[:], b1).then_inc(ld_w2, 16)
            pool.dma_start(dy_sb[:], Dy.rearrange("(k p) d -> p k d", p=P)).then_inc(ld_w2, 16)
            pool.dma_start(e_sb[:], Ea).then_inc(ld_w2, 16)
            pool.dma_start(wr_sb[0:D, :], Wr).then_inc(ld_w2, 16)
            pool.dma_start(wr_sb[D:P, :], Wr).then_inc(ld_w2, 16)
            pool.dma_start(br_sb[:], br.unsqueeze(0).to_broadcast([P, E])).then_inc(ld_w2, 16)
            pool.dma_start(w2_sb[:], W2.rearrange("e h d -> h e d")).then_inc(ld_w2, 16)
            pool.dma_start(b2_sb[:], b2.rearrange("(q two) d -> q (two d)", two=2)).then_inc(ld_w2, 16)
            pool.memset(sel[:], 1.0).then_inc(pool_steps, 1)
            pool.wait_ge(pool_steps, 1)
            low = sel[:, :, :].rearrange("k q (two m) -> k q two m", two=2)
            pool.affine_select(out=low, in_=low, compare_op=ALU.is_ge, fill=0.0, base=0,
                               pattern=[[-2, NP], [-1, 2], [0, D]], channel_multiplier=1).then_inc(pool_steps, 1)
            pool.wait_ge(pool_steps, 2)
            for n, d in enumerate(list(range(1, E)) + list(range(E + 1, 2 * E))):
                pool.affine_select(out=low, in_=low, compare_op=ALU.not_equal, fill=0.0, base=-d,
                                   pattern=[[-2, NP], [-1, 2], [0, D]], channel_multiplier=1).then_inc(pool_steps, 1)
                pool.wait_ge(pool_steps, 3 + n)
            pool.nop().then_inc(sel_ready, 1)

            def weighted_input(b):
                if isinstance(b, int) and b == 0:
                    pool.wait_ge(scaled_in, 1)
                    pool.wait_ge(h0_in, NG)
                wait(pool, pe_a, b)
                wait(pool, po_ub, b)
                pool.tensor_tensor(ub_t[:], h_of(b), wide(mean_h0[:, bass.ds(b * C, C)], D), ALU.subtract)\
                    .then_inc(po_in, 1)
                pool.wait_ge(po_in, b + 1)
                pool.tensor_tensor(ub[:], ub_t[:], wide(u_scale[:, bass.ds(b * C, C)], D), ALU.mult).then_inc(po_ub, 1)

            def attn_low(b):
                pool.wait_ge(ac_ah, b + 1)
                pool.tensor_tensor(a_p[:, :, D:2 * D], an[:], a_p[:, :, 0:D], ALU.subtract).then_inc(po_al, 1)

            def centred(b):
                pool.wait_ge(dv_h, b + 1)
                wait(pool, po_xc, b)
                pool.tensor_tensor(xc_t[:], h_of(b), wide(h_mean[:], D), ALU.subtract).then_inc(po_xt, 1)
                wait(pool, po_xl, b)
                pool.wait_ge(po_xt, b + 1)
                pool.tensor_tensor(xc[:], xc_t[:], wide(h_scale[:], D), ALU.mult).then_inc(po_xc, 1)

            def centred_low(b):
                pool.wait_ge(ac_xh, b + 1)
                pool.tensor_tensor(x_p[:, :, D:2 * D], xc[:], x_p[:, :, 0:D], ALU.subtract).then_inc(po_xl, 1)

            def add_pairs(b, n):
                pool.wait_ge(dv_tm, NP * b + 2 * n + 2)
                wait(pool, po_acc, b)
                pool.tensor_tensor(half[:, n, :], tm[:, 2 * n, :], tm[:, 2 * n + 1, :], ALU.add).then_inc(po_half, 1)

            def add_halves(b):
                pool.wait_ge(po_half, 2 * b + 2)
                wait(pool, pe_fold, b)
                pool.tensor_tensor(acc[:], half[:, 0, :], half[:, 1, :], ALU.add).then_inc(po_acc, 1)

            def turn(i, att, mlp, ahead):
                if att:
                    attn_low(i)
                if ahead:
                    weighted_input(i + 1)
                if mlp:
                    add_pairs(i - 1, 0)
                if att:
                    centred(i)
                    centred_low(i)
                if mlp:
                    add_pairs(i - 1, 1)
                    add_halves(i - 1)

            weighted_input(0)
            turn(0, True, False, True)
            turn(1, True, True, True)
            with pool.Fori(2, B - 1) as i:
                turn(i, True, True, True)
            turn(B - 1, True, True, False)
            turn(B, False, True, False)

        @block.scalar
        def _(act):
            def group(g):
                act.wait_ge(pe_h0, g + 1)
                act.activation(h_all[:, bass.ds(g * GROUP * D, GROUP * D)], bank[1][:, :], ACT.Copy)\
                   .then_inc(h0_in, 1)
                for n in range(0, GROUP // 2, 2):
                    act.wait_ge(pe_g2, (GROUP // 2) * g + n + 1)
                    for k in range(2):
                        pre = bank[2 + n][:, k * NS:(k + 1) * NS]
                        act.activation(pre, pre, ACT.Relu,
                                       accum_out=upd_sum[:, bass.ds(g * GROUP + 2 * n + k, 1)]).then_inc(sum_a, 1)

            with act.Fori(0, NG) as g:
                group(g)
            with act.Fori(0, NG // 2) as g:
                act.wait_ge(pe_scT, 2 * g + 1)
                act.activation(rows_or_scaled[:, bass.ds(g * 2 * GROUP * P, GROUP * P)], bank[0][:, :].bitcast(BF16),
                               ACT.Copy).then_inc(scT_in, 1)

            def relu(b):
                act.wait_ge(pe_pre, b + 1)
                wait(act, dv_x, NK * b)
                for k in range(NK):
                    act.activation(relu_b[:, k, :], n_bank[k][:, :], ACT.Relu).then_inc(ac_relu, 1)

            def off_diagonal(b, sc):
                act.wait_ge(dv_diag, C * b + sc + 1)
                wait(act, pe_a, b)
                act.activation(pm[:, OFF[sc] + P:OFF[sc] + WIDE[sc]], n_bank[sc % 2][:, P:WIDE[sc]], ACT.Copy)\
                   .then_inc(ac_off, 1)

            def attn_high(b):
                act.wait_ge(dv_an, b + 1)
                wait(act, pe_aT, b)
                act.activation(a_p[:, :, 0:D], an[:], ACT.Copy).then_inc(ac_ah, 1)

            def attn_T(b):
                act.wait_ge(pe_aT, b + 1)
                wait(act, pe_y, NK * b)
                act.activation(aT[:], tp_h[:, S:2 * S], ACT.Copy).then_inc(ac_aT, 1)

            def centred_high(b):
                act.wait_ge(po_xc, b + 1)
                wait(act, pe_xT, b)
                act.activation(x_p[:, :, 0:D], xc[:], ACT.Copy).then_inc(ac_xh, 1)

            def centred_T(b):
                act.wait_ge(pe_xT, b + 1)
                wait(act, pe_hid, E * b)
                wait(act, pe_lg, b)
                act.activation(xT[:], tp_h[:, 0:S], ACT.Copy).then_inc(ac_xT, 1)

            def gelu(b, e):
                act.wait_ge(pe_hid, E * b + e + 1)
                wait(act, pe_zz, NP * b)
                act.activation(hid[:, e, :], h_bank[e % 2][:, :], ACT.Gelu, bias=b1T[:, e:e + 1],
                               scale=w1_scale[:, e:e + 1]).then_inc(ac_gelu, 1)

            def tanh(b):
                act.wait_ge(dv_gap, b + 1)
                act.activation(tanh_g[:], gap[:], ACT.Tanh, scale=0.5).then_inc(ac_tanh, 1)

            def weights_T(b):
                act.wait_ge(pe_wT2, b + 1)
                wait(act, pe_wb, NP * b)
                act.activation(wT[:], ly_w[0:2 * E, :], ACT.Copy).then_inc(ac_wT, 1)

            def weights_wide(b, q):
                act.wait_ge(pe_wb, NP * b + q + 1)
                wait(act, dv_tm, NP * b - NP + q + 1)
                act.activation(wb[:, q, :], tp[:, :], ACT.Copy).then_inc(ac_wb, 1)

            def turn(i, att, mlp, ahead):
                k = i - 1
                if att:
                    for sc in range(C - 1):
                        off_diagonal(i, sc)
                if mlp:
                    centred_T(k)
                    gelu(k, 0)
                    gelu(k, 1)
                if att:
                    attn_high(i)
                if mlp:
                    tanh(k)
                if att:
                    attn_T(i)
                if mlp:
                    gelu(k, 2)
                    gelu(k, 3)
                    weights_T(k)
                    weights_wide(k, 0)
                    gelu(k, 4)
                    gelu(k, 5)
                    weights_wide(k, 1)
                if ahead:
                    relu(i + 1)
                if mlp:
                    gelu(k, 6)
                    gelu(k, 7)
                    weights_wide(k, 2)
                    weights_wide(k, 3)
                if att:
                    centred_high(i)

            relu(0)
            act.wait_ge(weights_in, 1)
            turn(0, True, False, True)
            turn(1, True, True, True)
            with act.Fori(2, B - 1) as i:
                turn(i, True, True, True)
            turn(B - 1, True, True, False)
            turn(B, False, True, False)

        @block.vector
        def _(dve):
            s = Steps(dve, dve_set)

            def op(instruction):
                s.done(instruction)
                s.last()

            def rsqrt(y, v, t, chain):
                chain.done(dve.tensor_scalar(y.bitcast(I32), v.bitcast(I32), -0.5, RSQRT_SEED, ALU.mult, ALU.add))
                for _ in range(3):
                    chain.last()
                    chain.done(dve.tensor_tensor(t, y, y, ALU.mult))
                    chain.last()
                    chain.done(dve.scalar_tensor_tensor(t, t, -0.5, v, ALU.mult, ALU.mult))
                    chain.last()
                    chain.done(dve.scalar_tensor_tensor(y, t, 1.5, y, ALU.add, ALU.mult))

            def variance(st, var, t, chain):
                chain.done(dve.tensor_tensor(t, st[:, :, 1], st[:, :, 4], ALU.subtract))
                chain.done(dve.tensor_tensor(var, st[:, :, 2], st[:, :, 5], ALU.add))
                chain.last()
                chain.done(dve.scalar_tensor_tensor(t, t, 0.25, t, ALU.mult, ALU.mult))
                chain.last()
                chain.done(dve.scalar_tensor_tensor(var, var, 1.0 / D, t, ALU.mult, ALU.add))

            def mean(st, m, t, chain):
                chain.done(dve.tensor_tensor(t, st[:, :, 1], st[:, :, 4], ALU.add))
                chain.last()
                chain.done(dve.tensor_scalar(m, t, 0.5, None, ALU.mult))

            dve.wait_ge(ld_x, 32)
            dve.tensor_copy(xf[:], xi[:]).then_inc(ints_f, 1)
            dve.tensor_copy(rf[:], ri[:]).then_inc(ints_f, 1)
            dve.wait_ge(ints_f, 2)
            dve.tensor_scalar(skill_row[:], xf[:], float(SKILLS), -1.0, ALU.min, ALU.max).then_inc(rows_ready, 1)
            dve.wait_ge(ld_c, 48)
            dve.tensor_copy(ident_h[:], ident_f[:]).then_inc(ids_ready, 1)
            dve.tensor_copy(ident_b[:], ident_f[:]).then_inc(ids_ready, 1)
            op(dve.tensor_copy(upto_b[:], mask_sb[:, 0:P]))
            op(dve.tensor_copy(fold_f[0:D, :], ident_f[0:D, 0:D]))
            op(dve.tensor_copy(fold_f[D:P, :], ident_f[D:P, D:P]))
            op(dve.memset(ones_row[:], 0.0))
            dve.memset(ones_row[:, NF - 1:NF], 1.0).then_inc(ids_ready, 1)
            dve.memset(feat_parts[:].rearrange("p j n -> p (j n)").bitcast(U32), 0).then_inc(ids_ready, 1)
            dve.memset(table_k[:], 0.0).then_inc(table_zeroed, 1)

            dve.wait_ge(pe_tok_T, 1)
            op(dve.tensor_copy(skill_T[:], bank[1][:, 0:P]))
            op(dve.tensor_copy(right_T[:], bank[1][:, P:2 * P]))
            op(dve.memset(right_parts[:], 1.0))
            op(dve.tensor_copy(right_parts[:, :, 1], right_T[:]))
            op(dve.tensor_tensor(feat_t[:], right_T[:], right_parts[:, :, 1], ALU.subtract))
            op(dve.tensor_copy(right_parts[:, :, 2], feat_t[:]))
            dve.tensor_tensor(right_parts[:, :, 3], feat_t[:], right_parts[:, :, 2], ALU.subtract).then_inc(tok_in, 1)

            def equal(b, side):
                wait(dve, pe_counts, b - 1)
                for sc in range(C):
                    row = bass.ds(b * S + sc * P, P)
                    mine = skill_T[:, bass.ds(b * C + sc, 1)]
                    last = dve.scalar_tensor_tensor(same[:, side, OFF[sc]:OFF[sc] + P], rows_or_scaled[:, row], mine,
                                                    upto_b[:], ALU.is_equal, ALU.mult)
                    if sc < C - 1:
                        rest = bass.ds(b * S + (sc + 1) * P, WIDE[sc] - P)
                        last.then_inc(same_in, 1)
                        last = dve.tensor_scalar(same[:, side, OFF[sc] + P:OFF[sc] + WIDE[sc]],
                                                 rows_or_scaled[:, rest], mine, None, ALU.is_equal)
                    last.then_inc(same_in, 1)

            for q in range(4):
                dve.wait_ge(ld_rows[q], 16)
                n = B // 8
                if q == 0:
                    equal(0, 0)
                    equal(1, 1)
                with dve.Fori(max(1, n * q), n * (q + 1)) as pair:
                    equal(2 * pair, 0)
                    equal(2 * pair + 1, 1)

            op(dve.tensor_scalar(valid[:], skill_T[:], 0.0, None, ALU.is_ge))
            op(dve.scalar_tensor_tensor(valid[:], skill_T[:], float(SKILLS), valid[:], ALU.is_lt, ALU.mult))
            dve.wait_ge(pe_counts, B)
            op(dve.tensor_copy(attempts[:], counts[:, :, 0]))
            op(dve.tensor_scalar(feat_t[:], attempts[:], 1.0, None, ALU.max))
            op(dve.reciprocal(feat_t[:], feat_t[:]))
            op(dve.tensor_reduce(newton[:], counts[:, :, 1:4], AX_X, ALU.add))
            op(dve.tensor_tensor(feat_t[:], feat_t[:], newton[:], ALU.mult))
            op(dve.tensor_tensor(feat[:, 0, :], skill_T[:], valid[:], ALU.mult))
            op(dve.tensor_tensor(feat[:, 1, :], attempts[:], valid[:], ALU.mult))
            op(dve.tensor_tensor(feat[:, 2, :], feat_t[:], valid[:], ALU.mult))
            op(dve.tensor_copy(feat[:, 3, :], valid[:]))

            def cut(source):
                for piece in range(PIECES):
                    at = feat_parts[:, :, NF * piece:NF * (piece + 1)].rearrange("p j f -> p f j")
                    op(dve.tensor_copy(at, source))
                    if piece < PIECES - 1:
                        op(dve.tensor_tensor(feat_r[:], source, at, ALU.subtract))
                        source = feat_r[:]
                n = NF * PIECES
                op(dve.tensor_copy(feat_parts[:, :, n:2 * n], feat_parts[:, :, 0:n]))
                op(dve.tensor_copy(feat_parts[:, :, 2 * n:3 * n], feat_parts[:, :, 0:n]))

            cut(feat[:])
            dve.nop().then_inc(feats_in, 1)

            dve.wait_ge(pe_wT, 1)
            dve.tensor_copy(projT[:], bank[2][0:D, 0:D]).then_inc(projT_in, 1)
            op(dve.tensor_copy(dxT[:], bank[2][0:D, D:D + NS]))
            dve.wait_ge(pe_tab, 1)
            op(dve.tensor_copy(table[:, 0:D], bank[3][0:NF, 0:D]))
            op(dve.tensor_reduce(table_m[:], table[:, 0:D], AX_X, ALU.add))
            op(dve.tensor_scalar(table_m[:], table_m[:], 1.0 / D, None, ALU.mult))
            dve.tensor_scalar(table_c[:], table[:, 0:D], table_m[:, 0:1], None, ALU.subtract).then_inc(tab_c_in, 1)
            dve.wait_ge(pe_tabT, 1)
            dve.tensor_copy(table_cT[:], bank[3][0:D, D:D + NF]).then_inc(tabT_in, 1)
            dve.wait_ge(pe_g, 1)
            op(dve.tensor_copy(table[:, D:D + NS], bank[3][0:NF, P:P + NS]))
            op(dve.tensor_copy(table_p[:, 0, :], table[:]))
            op(dve.tensor_tensor(table_r[:], table[:], table_p[:, 0, :], ALU.subtract))
            op(dve.tensor_copy(table_p[:, 1, :], table_r[:]))
            op(dve.tensor_tensor(table_r[:], table_r[:], table_p[:, 1, :], ALU.subtract))
            dve.tensor_copy(table_p[:, 2, :], table_r[:]).then_inc(table_ready, 1)

            dve.wait_ge(ld_w2, 16 * 12)
            dve.tensor_scalar(w1g[:], w1_sb[:], gam2[0:D, 0:1], None, ALU.mult).then_inc(gammas_in, 1)
            op(dve.memset(bet_wide[:], 0.0))
            dve.tensor_scalar(bet_wide[:], bet_wide[:], bet[:, 0:1], None, ALU.add).then_inc(wide_beta, 1)
            op(dve.tensor_scalar(wr_g[:], wr_sb[:], gam2[:, 0:1], None, ALU.mult))
            op(dve.tensor_copy(wr_p[:, 0, :], wr_g[:]))
            op(dve.tensor_tensor(wr_r[:], wr_g[:], wr_p[:, 0, :], ALU.subtract))
            op(dve.tensor_copy(wr_p[:, 1, :], wr_r[:]))
            op(dve.tensor_tensor(wr_p[:, 2, :], wr_r[:], wr_p[:, 1, :], ALU.subtract))
            dve.wait_ge(pe_bias, 1)
            op(dve.tensor_copy(b1T[:], bank[5][:, 16:24]))
            op(dve.tensor_copy(b2_pair[:], bank[5][:, 24:24 + NP]))
            op(dve.tensor_tensor(b1T[:], b1T[:], bank[5][:, 0:E], ALU.add))
            op(dve.tensor_tensor(br_sb[:], br_sb[:], bank[5][:, E:2 * E], ALU.add))

            def power_of_two(scale, inverse):
                op(dve.tensor_scalar(scale, scale, 1e-30, None, ALU.max))
                op(dve.tensor_scalar(scale.bitcast(I32), scale.bitcast(I32), EXP_MASK, None, ALU.bitwise_and))
                op(dve.reciprocal(inverse, scale))

            w1T_ps = bank[6][:, :].rearrange("h (e d) -> h e d", e=E)
            op(dve.tensor_reduce(w1_scale[:], w1T_ps, AX_X, ALU.max, apply_absolute_value=True))
            power_of_two(w1_scale[:], w1_inv[:])
            op(dve.tensor_tensor(w1T[:], w1T_ps, wide(w1_inv[:], D), ALU.mult))
            op(dve.tensor_copy(w1_p[:, 0, :, 0, :], w1T[:]))
            op(dve.tensor_copy(w1_p[:, 0, :, 1, :], w1T[:]))
            op(dve.tensor_tensor(w1_p[:, 1, :, 0, :], w1T[:], w1_p[:, 0, :, 0, :], ALU.subtract))
            op(dve.tensor_copy(w1_p[:, 1, :, 1, :], w1_p[:, 1, :, 0, :]))
            op(dve.tensor_reduce(dy_scale[:, 0:NK], dy_sb[:], AX_X, ALU.max, apply_absolute_value=True))
            power_of_two(dy_scale[:, 0:NK], dy_scale[:, NK:2 * NK])
            op(dve.tensor_tensor(dy_sb[:], dy_sb[:], wide(dy_scale[:, NK:2 * NK], D), ALU.mult))
            op(dve.tensor_copy(dy_p[:, 0, :, 0, :], dy_sb[:]))
            op(dve.tensor_copy(dy_p[:, 0, :, 1, :], dy_sb[:]))
            op(dve.tensor_tensor(dy_p[:, 1, :, 0, :], dy_sb[:], dy_p[:, 0, :, 0, :], ALU.subtract))
            dve.tensor_copy(dy_p[:, 1, :, 1, :], dy_p[:, 1, :, 0, :]).then_inc(parts_in, 1)
            op(dve.tensor_copy(eT[:].rearrange("p k d -> p (k d)"), bank[5][:, P:2 * P]))
            op(dve.tensor_reduce(e_mean[:], eT[:], AX_X, ALU.add))
            op(dve.tensor_scalar(e_mean[:], e_mean[:], 1.0 / D, None, ALU.mult))
            op(dve.tensor_tensor(eT[:], eT[:], wide(e_mean[:], D), ALU.subtract))
            op(dve.tensor_tensor(eT[:], eT[:], wide(dy_scale[:, 0:NK], D), ALU.mult))
            dve.wait_ge(pe_parts, 1)
            op(dve.tensor_copy(w1k[:, 0].rearrange("p e h -> p (e h)"), bank[2][:, :].bitcast(F16)))
            op(dve.tensor_copy(w1k[:, 1].rearrange("p e h -> p (e h)"), bank[3][:, :].bitcast(F16)))
            dve.tensor_copy(dyT[:].rearrange("p k n -> p (k n)"), bank[4][:, 0:NS].bitcast(F16)).then_inc(weights_in, 1)

            def group(g):
                dve.wait_ge(pe_featT, g + 1)
                dve.tensor_copy(feat_k[:, bass.ds(g * GROUP * P, GROUP * P)], bank[0][:, :].bitcast(BF16))\
                   .then_inc(featT_in, 1)
                dve.wait_ge(h0_in, g + 1)
                for n in range(GROUP):
                    at = stat_h0[:, bass.ds(g * GROUP + n, 1), :].rearrange("p o k -> p (o k)")
                    dve.bn_stats(at, h_all[:, bass.ds((g * GROUP + n) * D, D)]).then_inc(h0_stats, 1)
                for n in range(1, GROUP // 2, 2):
                    dve.wait_ge(pe_g2, (GROUP // 2) * g + n + 1)
                    for k in range(2):
                        pre = bank[2 + n][:, k * NS:(k + 1) * NS]
                        dve.tensor_scalar(pre, pre, 0.0, None, ALU.max, ALU.add,
                                          accum_out=upd_sum[:, bass.ds(g * GROUP + 2 * n + k, 1)]).then_inc(sum_v, 1)

            with dve.Fori(0, NG) as g:
                group(g)
            dve.wait_ge(h0_stats, J)
            dve.wait_ge(sum_v, J // 2)
            dve.wait_ge(sum_a, J // 2)
            mean(stat_h0, mean_h0[:], feat_t[:], s)
            s.last()
            variance(stat_h0, var_h0[:], feat_t[:], s)
            s.last()
            op(dve.tensor_scalar(feat_t[:], var_h0[:], EPS, None, ALU.add))
            rsqrt(rstd[:], feat_t[:], newton[:], s)
            s.last()
            dve.tensor_tensor(upd_sum[:], upd_sum[:], rstd[:], ALU.mult).then_inc(upd_in, 1)
            op(dve.tensor_scalar(feat_t[:], var_h0[:], 1.0 + EPS, EPS * EPS, ALU.mult, ALU.add))
            rsqrt(u_scale[:], feat_t[:], newton[:], s)
            s.last()
            op(dve.tensor_tensor(u_scale[:].rearrange("p (b c) -> p b c", c=C),
                                 u_scale[:].rearrange("p (b c) -> p b c", c=C),
                                 dec[:, 0:C].unsqueeze(1).to_broadcast([P, B, C]), ALU.mult))
            dve.wait_ge(pe_updT, 1)
            dve.tensor_copy(upd_sum_T[:], bank[1][:, 0:P]).then_inc(updT_in, 1)

            grow = DECAY / L1_EPS
            dve.wait_ge(ld_row_u, 16)
            op(dve.tensor_scalar(row_w, row_u, 1.0 / L1_EPS, 1.0, ALU.mult, ALU.min))
            op(dve.tensor_scalar(row_nz, row_u, 0.0, None, ALU.is_gt))
            op(dve.memset(row_one, 0.0))
            op(dve.tensor_tensor_scan(row_any, row_nz, row_one, 0.0, ALU.max, ALU.add))
            op(dve.tensor_copy(row_one[:, 3:S], row_any[:, 0:S - 3]))
            op(dve.tensor_tensor(row_w, row_w, row_one, ALU.max))
            op(dve.tensor_scalar(row_one, row_one, -grow, grow, ALU.mult, ALU.add))
            op(dve.tensor_tensor_scan(row_any, row_one, row_w, 0.0, ALU.mult, ALU.add))
            op(dve.memset(row_d, 0.0))
            op(dve.tensor_scalar(row_d[:, 1:S], row_any[:, 0:S - 1], 1.0, DECAY, ALU.min, ALU.mult))
            op(dve.tensor_tensor(row_d, row_d, row_u, ALU.add))
            op(dve.tensor_scalar(row_d, row_d, L1_EPS, None, ALU.max))
            op(dve.reciprocal(row_w, row_d))
            dve.tensor_scalar(row_nz, row_w, DECAY, None, ALU.mult).then_inc(scalars_in, 1)
            dve.wait_ge(pe_recT, 1)
            op(dve.tensor_tensor(recip_T[:], rstd[:], bank[1][:, P:2 * P], ALU.mult))
            for f in range(NF):
                op(dve.tensor_tensor(feat[:, f, :], feat[:, f, :], recip_T[:], ALU.mult))
            cut(feat[:])
            dve.nop().then_inc(scaled_in, 1)
            with dve.Fori(0, NG // 2) as g:
                dve.wait_ge(pe_scT, 2 * g + 2)
                dve.tensor_copy(rows_or_scaled[:, bass.ds((2 * g + 1) * GROUP * P, GROUP * P)],
                                bank[1][:, :].bitcast(BF16)).then_inc(scT_in, 1)

            def scan(b):
                dve.wait_ge(ac_relu, NK * (b + 1))
                dve.wait_ge(ld_factor, 16 * (b + 1))
                wait(dve, pe_s, C * b)
                wait(dve, dv_y, NK * b)
                for k in range(NK):
                    dve.tensor_tensor_scan(xs[:, k, :], factor[:], relu_b[:, k, :], 0.0, ALU.mult, ALU.add)\
                       .then_inc(dv_x, 1)

            def diagonal(b, sc):
                dve.wait_ge(pe_s, C * b + sc + 1)
                wait(dve, pe_a, b)
                dve.tensor_tensor(pm[:, OFF[sc]:OFF[sc] + P], n_bank[sc % 2][:, 0:P], causal_f, ALU.mult)\
                   .then_inc(dv_diag, 1)

            def finish(b):
                dve.wait_ge(pe_fold, b + 1)
                wait(dve, st_out, 16 * b)
                dve.tensor_tensor(o_sb[:], ly_y.rearrange("p (c d) -> p c d", c=C), h_of(b), ALU.add)\
                   .then_inc(dv_out, 1)

            def attn_scale(b, s):
                dve.wait_ge(pe_a, b + 1)
                for c in range(C):
                    s.done(dve.bn_stats(st_a[:, c, :], az_a[:, c, :]))
                s.last()
                t, v, q = t_a[:, 0, :], t_a[:, 1, :], t_a[:, 2, :]
                variance(st_a, v, t, s)
                s.last()
                s.done(dve.tensor_tensor(v, v, dec[:, C:2 * C], ALU.add))
                s.last()
                s.done(dve.tensor_scalar(q.bitcast(I32), v.bitcast(I32), -0.5, RSQRT_SEED, ALU.mult, ALU.add))
                s.last()
                wait(dve, po_al, b)
                dve.tensor_tensor(an[:], az_a, wide(q, D), ALU.mult).then_inc(dv_an, 1)
                s.done(dve.tensor_tensor(t, q, q, ALU.mult))
                s.last()
                s.done(dve.scalar_tensor_tensor(v, t, EPS, v, ALU.mult, ALU.mult))

            def gate(b, k):
                dve.wait_ge(pe_y, NK * b + k + 1)
                wait(dve, pe_z, b)
                dve.scalar_tensor_tensor(ys[:, k, :], n_bank[k][:, :], 0.0, xs[:, k, :], ALU.max, ALU.mult)\
                   .then_inc(dv_y, 1)

            def residual(b, s):
                dve.wait_ge(pe_z, b + 1)
                for c in range(C):
                    s.done(dve.bn_stats(st_z[:, c, :], az_z[:, c, :]))
                s.last()
                var, t, y = t_z[:, 0, :], t_z[:, 1, :], t_z[:, 2, :]
                variance(st_z, var, t, s)
                s.last()
                s.done(dve.tensor_tensor(var, var, t_a[:, 1, :], ALU.add))
                s.last()
                rsqrt(y, var, t, s)
                s.last()
                for c in range(C):
                    h = h_all[:, bass.ds(b * C * D + c * D, D)]
                    s.done(dve.scalar_tensor_tensor(h, az_z[:, c, :], y[:, c:c + 1], h, ALU.mult, ALU.add))
                s.last()
                dve.nop().then_inc(dv_passed, 1)
                for c in range(C):
                    s.done(dve.bn_stats(st_h[:, c, :], h_all[:, bass.ds(b * C * D + c * D, D)]))
                s.last()
                wait(dve, po_xc, b)
                mean(st_h, h_mean[:], t_h[:, 0, :], s)
                s.last()
                var, t = t_h[:, 1, :], t_h[:, 0, :]
                variance(st_h, var, t, s)
                s.last()
                s.done(dve.tensor_scalar(var, var, 1.0 + EPS, EPS * EPS, ALU.mult, ALU.add))
                s.last()
                rsqrt(h_scale[:], var, t, s)
                s.last()
                dve.nop().then_inc(dv_h, 1)

            def route(b, s):
                dve.wait_ge(pe_lg, b + 1)
                dve.tensor_reduce(lg[:], ly_lg.rearrange("p (c k e) -> p c e k", c=C, k=PIECES), AX_X, ALU.add)\
                   .then_inc(dv_lg, 1)
                dve.wait_ge(dv_lg, b + 1)
                s.done(dve.tensor_tensor(lg[:], lg[:], br_sb[:].unsqueeze(1).to_broadcast([P, C, E]), ALU.add))
                s.last()
                dve.nop().then_inc(dv_passed, 1)
                for c in range(C):
                    s.done(dve.max(top[:, c, :], lg[:, c, :]))
                s.last()
                dve.tensor_tensor(gap[:], top[:, :, 0], top[:, :, 1], ALU.subtract).then_inc(dv_gap, 1)
                for c in range(C):
                    s.done(dve.max_index(top_i[:, c, :], top[:, c, :], lg[:, c, :]))
                s.last()
                iota = dec[:, 2 * C:2 * C + E].unsqueeze(1).to_broadcast([P, C, E])
                for k in range(2):
                    s.done(dve.tensor_tensor(pick[:, k], iota, wide(top_i[:, :, k], E), ALU.is_equal))

            def mix(b, s):
                dve.wait_ge(ac_tanh, b + 1)
                s.done(dve.tensor_scalar(wgt[:, 0, :], tanh_g[:], 0.5, 0.5, ALU.mult, ALU.add))
                s.done(dve.tensor_scalar(wgt[:, 1, :], tanh_g[:], -0.5, 0.5, ALU.mult, ALU.add))
                s.last()
                s.done(dve.tensor_tensor(pick[:].rearrange("p k c e -> p (k c) e"),
                                         pick[:].rearrange("p k c e -> p (k c) e"),
                                         wide(wgt[:].rearrange("p k c -> p (k c)"), E), ALU.mult))
                s.last()
                s.done(dve.tensor_tensor(pick[:, 0], pick[:, 0], pick[:, 1], ALU.add))
                s.last()
                wait(dve, pe_wT2, b)
                s.done(dve.tensor_copy(w_p[:, :, 0:E], pick[:, 0]))
                s.last()
                dve.tensor_tensor(w_p[:, :, E:2 * E], pick[:, 0], w_p[:, :, 0:E], ALU.subtract).then_inc(dv_w, 1)

            def weigh(b, q):
                dve.wait_ge(pe_zz, NP * b + q + 1)
                dve.wait_ge(ac_wb, NP * b + q + 1)
                wait(dve, po_acc, b)
                dve.scalar_tensor_tensor(tm[:, q, :], zb[:, :], b2_pair[:, q:q + 1], wb[:, q, :], ALU.add, ALU.mult)\
                   .then_inc(dv_tm, 1)

            def turn(i, att, mlp, done, ahead):
                k = i - 1
                a = Steps(dve, att_steps, N_ATT * i)
                m = Steps(dve, mlp_steps, N_MLP * k)
                if att:
                    for sc in range(C):
                        diagonal(i, sc)
                if done:
                    finish(i - 2)
                if att:
                    attn_scale(i, a)
                if mlp:
                    route(k, m)
                    mix(k, m)
                if att:
                    gate(i, 0)
                    gate(i, 1)
                if mlp:
                    weigh(k, 0)
                    weigh(k, 1)
                if ahead:
                    scan(i + 1)
                if mlp:
                    weigh(k, 2)
                if att:
                    residual(i, a)
                if mlp:
                    weigh(k, 3)
                assert a.n in (0, N_ATT) and m.n in (0, N_MLP), (a.n, m.n)

            scan(0)
            turn(0, True, False, False, True)
            turn(1, True, True, False, True)
            with dve.Fori(2, B - 1) as i:
                turn(i, True, True, True, True)
            turn(B - 1, True, True, True, False)
            turn(B, False, True, True, False)
            finish(B - 1)

        @block.tensor
        def _(pe):
            pe.wait_ge(ld_c, 48)
            pe.wait_ge(ints_f, 2)
            pe.transpose(bank[1][:, 0:P], xf[:], ident_f[:])
            pe.transpose(bank[1][:, P:2 * P], rf[:], ident_f[:]).then_inc(pe_tok_T, 1)
            pe.wait_ge(ld_w, 16 * 9)
            pe.transpose(bank[2][0:D, 0:D], proj_sb[:], ident_f[0:D, 0:D])
            for k in range(NK):
                last = pe.transpose(bank[2][0:D, D + k * P:D + (k + 1) * P], dx_sb[:, k, :], ident_f[:])
            last.then_inc(pe_wT, 1)

            def count(b, side):
                pe.wait_ge(same_in, (2 * C - 1) * (b + 1))
                for tc in range(C):
                    for sc in range(tc + 1):
                        at = OFF[sc] + P * (tc - sc)
                        last = pe.matmul(bank[0][:, bass.ds((b * C + tc) * 4, 4)], same[:, side, at:at + P],
                                         right_parts[:, bass.ds(b * C + sc, 1), :].rearrange("p o k -> p (o k)"),
                                         start=(sc == 0), stop=(sc == tc))
                last.then_inc(pe_counts, 1)

            pe.wait_ge(tok_in, 1)
            with pe.Fori(0, B // 2) as pair:
                count(2 * pair, 0)
                count(2 * pair + 1, 1)

            pe.wait_ge(projT_in, 1)
            pe.wait_ge(ids_ready, 4)
            pe.matmul(bank[3][0:NF, 0:D], s4[:], projT[:], start=True, stop=False)
            pe.matmul(bank[3][0:NF, 0:D], ones_row[:], projb[:], start=False, stop=True).then_inc(pe_tab, 1)
            pe.wait_ge(tab_c_in, 1)
            pe.transpose(bank[3][0:D, D:D + NF], table_c[:], ident_f[0:NF, 0:NF]).then_inc(pe_tabT, 1)
            pe.wait_ge(tabT_in, 1)
            pe.matmul(bank[3][0:NF, P:P + NS], table_cT[:], dxT[:], start=True, stop=True).then_inc(pe_g, 1)
            pe.wait_ge(ld_w2, 16 * 12)
            pe.wait_ge(wide_beta, 1)
            for e in range(E):
                pe.matmul(bank[5][:, e:e + 1], w1_sb[:, e, :], bet[:], start=True, stop=True)
            pe.matmul(bank[5][:, E:2 * E], bet_wide[:], wr_sb[0:D, :], start=True, stop=True)
            pe.transpose(bank[5][:, 16:24], b1_sb[:], ident_f[0:E, 0:E])
            pe.transpose(bank[5][:, 24:24 + NP], b2_sb[:], ident_f[0:NP, 0:NP])
            for k in range(NK):
                pe.transpose(bank[5][:, P + k * D:P + (k + 1) * D], e_sb[:, k * P:(k + 1) * P], ident_f[0:D, 0:D])
            pe.wait_ge(gammas_in, 1)
            for e in range(E):
                last = pe.transpose(bank[6][:, e * D:(e + 1) * D], w1g[:, e, :], ident_f[0:D, 0:D])
            last.then_inc(pe_bias, 1)
            pe.wait_ge(parts_in, 1)
            for part in range(2):
                for e in range(E):
                    pe.transpose(bank[2 + part][:, :].bitcast(F16)[:, e * P:(e + 1) * P],
                                 w1_p[:, part, e].rearrange("h u d -> h (u d)"), ident_h[:])
                for k in range(NK):
                    at = (part * NK + k) * P
                    last = pe.transpose(bank[4][:, :].bitcast(F16)[:, at:at + P],
                                        dy_p[:, part, k].rearrange("n u d -> n (u d)"), ident_h[:])
            last.then_inc(pe_parts, 1)

            def group(g, first):
                if first:
                    pe.wait_ge(feats_in, 1)
                    pe.wait_ge(weights_in, 1)
                for n in range(GROUP):
                    last = pe.transpose(bank[0][:, :].bitcast(BF16)[:, n * P:(n + 1) * P],
                                        feat_parts[:, bass.ds(g * GROUP + n, 1), :].rearrange("p o k -> p (o k)"),
                                        ident_b[:])
                last.then_inc(pe_featT, 1)
                pe.wait_ge(featT_in, g + 1)
                if first:
                    pe.wait_ge(ld_table, 16 * PIECES * PIECES)
                else:
                    pe.wait_ge(h0_in, g)
                for n in range(GROUP):
                    last = pe.matmul(bank[1][:, n * D:(n + 1) * D], feat_k[:, bass.ds((g * GROUP + n) * P, P)],
                                     table_k[:, 0:D], start=True, stop=True)
                last.then_inc(pe_h0, 1)
                for n in range(GROUP // 2):
                    if not first:
                        pe.wait_ge([sum_a, sum_v][n % 2], (GROUP // 2) * (g - 1) + 2 * (n // 2) + 2)
                    for k in range(2):
                        last = pe.matmul(bank[2 + n][:, k * NS:(k + 1) * NS],
                                         feat_k[:, bass.ds((g * GROUP + 2 * n + k) * P, P)],
                                         table_k[:, D:D + NS], start=True, stop=True)
                    last.then_inc(pe_g2, 1)

            group(0, True)
            with pe.Fori(1, NG) as g:
                group(g, False)
            pe.wait_ge(upd_in, 1)
            pe.transpose(bank[1][:, 0:P], upd_sum[:], ident_f[:]).then_inc(pe_updT, 1)
            pe.wait_ge(ld_recip, 16)
            pe.transpose(bank[1][:, P:2 * P], recip_j[:], ident_f[:]).then_inc(pe_recT, 1)
            pe.wait_ge(scaled_in, 1)

            def scaled(g, side, first):
                if not first:
                    pe.wait_ge(scT_in, 2 * g)
                for n in range(GROUP):
                    last = pe.transpose(bank[side][:, :].bitcast(BF16)[:, n * P:(n + 1) * P],
                                        feat_parts[:, bass.ds((2 * g + side) * GROUP + n, 1), :]
                                        .rearrange("p o k -> p (o k)"), ident_b[:])
                last.then_inc(pe_scT, 1)

            scaled(0, 0, True)
            scaled(0, 1, True)
            with pe.Fori(1, NG // 2) as g:
                scaled(g, 0, False)
                scaled(g, 1, False)
            pe.wait_ge(scT_in, NG)

            def update(b):
                wait(pe, dv_y, NK * b)
                for k in range(NK):
                    last = pe.matmul(n_bank[k][:, :], table_k[:, D + k * P:D + (k + 1) * P],
                                     rows_or_scaled[:, bass.ds(b * S, S)], start=True, stop=True)
                last.then_inc(pe_pre, 1)

            def scores(b):
                pe.wait_ge(dv_x, NK * (b + 1))
                for sc in range(C):
                    if sc >= 2:
                        pe.wait_ge(dv_diag, C * b + sc - 1)
                        pe.wait_ge(ac_off, (C - 1) * b + sc - 1)
                    for k in range(NK):
                        last = pe.matmul(n_bank[sc % 2][:, 0:WIDE[sc]], xs[:, k, sc * P:(sc + 1) * P],
                                         xs[:, k, sc * P:S], start=(k == 0), stop=(k == NK - 1))
                    last.then_inc(pe_s, 1)

            def values(b):
                pe.wait_ge(dv_diag, C * (b + 1))
                pe.wait_ge(ac_off, (C - 1) * (b + 1))
                pe.wait_ge(po_ub, b + 1)
                wait(pe, dv_h, b)
                for tc in range(C):
                    for sc in range(tc + 1):
                        at = OFF[sc] + P * (tc - sc)
                        last = pe.matmul(az[:, tc * D:(tc + 1) * D], pm[:, at:at + P], ub[:, sc, :],
                                         start=(sc == 0), stop=(sc == tc))
                last.then_inc(pe_a, 1)

            def attn_T(b, k):
                pe.wait_ge(po_al, b + 1)
                pe.wait_ge(ac_ah, b + 1)
                wait(pe, ac_wb, NP * k)
                for c in range(C):
                    last = pe.transpose(tp_h[:, S + c * P:S + (c + 1) * P], a_p[:, c, :], ident_h[:])
                last.then_inc(pe_aT, 1)

            def y_core(b):
                pe.wait_ge(ac_aT, b + 1)
                for k in range(NK):
                    pe.matmul(n_bank[k][:, :], dyT[:, 0, k * P:(k + 1) * P], aT[:], start=True, stop=False)
                    pe.matmul(n_bank[k][:, :], dyT[:, 1, k * P:(k + 1) * P], aT[:], start=False, stop=True)\
                      .then_inc(pe_y, 1)

            def z_out(b):
                pe.wait_ge(dv_y, NK * (b + 1))
                for c in range(C):
                    for k in range(NK):
                        last = pe.matmul(az[:, (C + c) * D:(C + c + 1) * D], ys[:, k, c * P:(c + 1) * P], eT[:, k, :],
                                         start=(k == 0), stop=(k == NK - 1))
                last.then_inc(pe_z, 1)

            def centred_T(b):
                pe.wait_ge(po_xl, b + 1)
                wait(pe, ac_wb, NP * b)
                for c in range(C):
                    last = pe.transpose(tp_h[:, c * P:(c + 1) * P], x_p[:, c, :], ident_h[:])
                last.then_inc(pe_xT, 1)

            def logits(b):
                pe.wait_ge(ac_xT, b + 1)
                wait(pe, dv_out, b)
                n = PIECES * E
                for c in range(C):
                    last = pe.matmul(ly[:, c * n:(c + 1) * n], xT[:, c * P:(c + 1) * P],
                                     wr_p[:].rearrange("p k e -> p (k e)"), start=True, stop=True)
                last.then_inc(pe_lg, 1)

            def hidden(b, e):
                pe.wait_ge(ac_xT, b + 1)
                wait(pe, ac_gelu, E * b + e - 1)
                pe.matmul(h_bank[e % 2][:, :], w1k[:, 0, e, :], xT[:], start=True, stop=False)
                pe.matmul(h_bank[e % 2][:, :], w1k[:, 1, e, :], xT[:], start=False, stop=True).then_inc(pe_hid, 1)

            def expert_out(b, q):
                pe.wait_ge(ac_gelu, E * b + 2 * q + 2)
                wait(pe, dv_tm, NP * b + q)
                pe.matmul(zb[0:D, :], w2_sb[:, 2 * q, :], hid[:, 2 * q, :], start=True, stop=True)
                pe.matmul(zb[D:P, :], w2_sb[:, 2 * q + 1, :], hid[:, 2 * q + 1, :], start=True, stop=True)\
                  .then_inc(pe_zz, 1)

            def weights_T(b):
                pe.wait_ge(dv_w, b + 1)
                wait(pe, dv_out, b)
                for c in range(C):
                    last = pe.transpose(ly_w[0:2 * E, c * P:(c + 1) * P], w_p[:, c, :], ident_h[:])
                last.then_inc(pe_wT2, 1)

            def weights_wide(b, q):
                if q == 0:
                    pe.wait_ge(ac_wT, b + 1)
                wait(pe, ac_wb, NP * b + q)
                pe.matmul(tp[:, :], sel[:, q, :], wT[:], start=True, stop=True).then_inc(pe_wb, 1)

            def fold(b):
                pe.wait_ge(po_acc, b + 1)
                for c in range(C):
                    last = pe.matmul(ly[:, 256 + c * D:256 + (c + 1) * D], acc[:, c * P:(c + 1) * P], fold_f[:],
                                     start=True, stop=True)
                last.then_inc(pe_fold, 1)

            def turn(i, att, mlp, done, ahead):
                k = i - 1
                if att:
                    scores(i)
                if done:
                    fold(i - 2)
                if mlp:
                    centred_T(k)
                if att:
                    values(i)
                if mlp:
                    logits(k)
                    hidden(k, 0)
                    hidden(k, 1)
                if att:
                    attn_T(i, k)
                if mlp:
                    hidden(k, 2)
                if att:
                    y_core(i)
                if mlp:
                    hidden(k, 3)
                    expert_out(k, 0)
                    weights_T(k)
                    weights_wide(k, 0)
                    hidden(k, 4)
                    hidden(k, 5)
                    expert_out(k, 1)
                    weights_wide(k, 1)
                if att:
                    z_out(i)
                if ahead:
                    update(i + 1)
                if mlp:
                    hidden(k, 6)
                    hidden(k, 7)
                    expert_out(k, 2)
                    weights_wide(k, 2)
                    weights_wide(k, 3)
                    expert_out(k, 3)

            pe.wait_ge(sel_ready, 1)
            update(0)
            turn(0, True, False, False, True)
            turn(1, True, True, False, True)
            with pe.Fori(2, B - 1) as i:
                turn(i, True, True, True, True)
            turn(B - 1, True, True, True, False)
            turn(B, False, True, True, False)
            fold(B - 1)


_INS = ["x", "mask_BS_i0_1", "L0_tok_skill_w", "L0_tok_skill_b", "L0_tok_att_w", "L0_tok_att_b", "L0_tok_mast_w",
        "L0_tok_mast_b", "L0_tok_proj_w", "L0_tok_proj_b", "L0_attn_E", "L0_attn_Dx", "L0_attn_Dy", "L0_ffn_gamma",
        "L0_ffn_beta", "L0_ffn_Wr", "L0_ffn_br", "L0_ffn_W1", "L0_ffn_b1", "L0_ffn_W2", "L0_ffn_b2"]


def constants():
    row, col = np.arange(P)[:, None], np.arange(P)[None, :]
    t = (np.arange(P)[:, None] + P * np.arange(C)[None, :]).astype(np.float64)
    decays = np.concatenate([DECAY ** (-1.0 - t), EPS * DECAY ** (-2.0 * t), np.tile(np.arange(E), (P, 1))], axis=1)
    return {
        "ident": np.eye(P, dtype=np.float32),
        "masks": np.concatenate([row <= col, row < col], axis=1).astype(np.float32),
        "decays": decays.astype(np.float32),
    }


def kernel(**inputs):
    import concourse.bacc as _bacc
    from concourse.bass_utils import run_bass_kernel_spmd as _run

    nc = _bacc.Bacc("TRN2", target_bir_lowering=False, num_devices=1)
    arrays, args = {}, []
    named = [(name, np.ascontiguousarray(inputs[name])) for name in _INS] + list(constants().items())
    for name, a in named:
        arrays[f"in_{name}"] = a
        args.append(nc.dram_tensor(f"in_{name}", a.shape, mybir.dt.from_np(a.dtype), kind="ExternalInput").ap())
    args.append(nc.dram_tensor("out_0", (B, S, D), F32, kind="ExternalOutput").ap())
    program(nc, *args)
    r = _run(nc, [arrays], core_ids=[0])
    return r.results[0]["out_0"]
```

```python
from contextlib import ExitStack

import numpy as np

import concourse.bass as bass
from concourse import mybir

F32 = mybir.dt.float32
F16 = mybir.dt.float16
BF16 = mybir.dt.bfloat16
I32 = mybir.dt.int32
U32 = mybir.dt.uint32
ALU = mybir.AluOpType
ACT = mybir.ActivationFunctionType
AX_X = mybir.AxisListType.X

P = 128
B, S = 32, 512
C = S // P
J = B * C
D = 64
NS = 256
NK = NS // P
E = 8
HID = 128
NP = E // 2
SKILLS = 75
D3 = 21
NF = 4
PIECES = 3
KF = NF * PIECES * PIECES
DECAY = 0.97
EPS = 1e-5
L1_EPS = 1e-12
RSQRT_SEED = float(0x5F3759DF)
OFF = [0, 512, 896, 1152]
WIDE = [S - P * sc for sc in range(C)]
CAUSAL = OFF[-1] + WIDE[-1]
GROUP = 8
NG = J // GROUP
EXP_MASK = 0x7F800000

N_ATT = 12
N_RES = 22
N_MLP = 16


class Steps:

    def __init__(self, eng, sem, base=0):
        self.eng, self.sem, self.base, self.n = eng, sem, base, 0

    def done(self, instruction):
        instruction.then_inc(self.sem, 1)
        self.n += 1

    def last(self):
        self.eng.wait_ge(self.sem, self.base + self.n)


def wait(eng, sem, value):
    if not isinstance(value, int) or value > 0:
        eng.wait_ge(sem, value)


def program(nc, x, r, skill_w, skill_b, att_w, att_b, mast_w, mast_b, proj_w, proj_b, Ea, Dx, Dy, gamma, beta,
            Wr, br, W1, b1, W2, b2, ident, masks, decays, out):
    with ExitStack() as ctx:
        def sb(name, shape, dt=F32):
            return ctx.enter_context(nc.sbuf_tensor(name, shape, dt))

        def sem(name):
            return ctx.enter_context(nc.semaphore(name))

        def scratch(name, shape, dt):
            return nc.dram_tensor(name, shape, dt, kind="Internal").ap()

        bank = [ctx.enter_context(nc.psum_tensor(f"bank{n}", [P, 512], F32)) for n in range(8)]

        skill_row_d = scratch("skill_row_d", (J, P), BF16)
        upd_sum_d = scratch("upd_sum_d", (J, P), F32)
        recip_d = scratch("recip_d", (B, S), F32)
        factor_d = scratch("factor_d", (B, S), F32)
        table_d = scratch("table_d", (NF, PIECES, D + NS), BF16)

        xi, ri = sb("xi", [J, P], I32), sb("ri", [J, P], I32)
        xf, rf = sb("xf", [J, P]), sb("rf", [J, P])
        ident_f, mask_sb = sb("ident_f", [P, P]), sb("mask_sb", [P, 2 * P])
        causal_f = mask_sb[:, P:2 * P]
        ident_h, ident_b = sb("ident_h", [P, P], F16), sb("ident_b", [P, P], BF16)
        upto_b = sb("upto_b", [P, P], BF16)
        dec = sb("dec", [P, 2 * C + E])
        fold_f = sb("fold_f", [P, D])
        skill_T, right_T = sb("skill_T", [P, J]), sb("right_T", [P, J])
        skill_row = sb("skill_row", [J, P], BF16)
        right_parts = sb("right_parts", [P, J, 4], BF16)
        ones_row = sb("ones_row", [1, NF])
        s4, proj_sb, projT = sb("s4", [D, NF]), sb("proj_sb", [D, D]), sb("projT", [D, D])
        projb = sb("projb", [1, D])
        table = sb("table", [NF, D + NS])
        table_c, table_cT = sb("table_c", [NF, D]), sb("table_cT", [D, NF])
        table_m = sb("table_m", [NF, 1])
        table_p = sb("table_p", [NF, PIECES, D + NS], BF16)
        table_r = sb("table_r", [NF, D + NS])
        table_k = sb("table_k", [P, D + NS], BF16)
        dx_sb, dxT = sb("dx_sb", [P, NK, D]), sb("dxT", [D, NS])
        dy_sb, dy_scale = sb("dy_sb", [P, NK, D]), sb("dy_scale", [P, 2 * NK])
        dy_p = sb("dy_p", [P, 2, NK, 2, D], F16)
        dyT = sb("dyT", [P, 2, NS], F16)
        e_sb, eT, e_mean = sb("e_sb", [D, NS]), sb("eT", [P, NK, D]), sb("e_mean", [P, NK])
        gam2, bet = sb("gam2", [P, 1]), sb("bet", [D, 1])
        bet_wide = sb("bet_wide", [D, P])
        w1_sb, w1g = sb("w1_sb", [D, E, HID]), sb("w1g", [D, E, HID])
        w1T = sb("w1T", [HID, E, D])
        w1_scale, w1_inv = sb("w1_scale", [HID, E]), sb("w1_inv", [HID, E])
        w1_p = sb("w1_p", [HID, 2, E, 2, D], F16)
        w1k = sb("w1k", [P, 2, E, HID], F16)
        b1_sb, b1T = sb("b1_sb", [E, HID]), sb("b1T", [HID, E])
        w2_sb = sb("w2_sb", [HID, E, D])
        b2_sb, b2_pair = sb("b2_sb", [NP, P]), sb("b2_pair", [P, NP])
        wr_sb, wr_g, wr_r = sb("wr_sb", [P, E]), sb("wr_g", [P, E]), sb("wr_r", [P, E])
        wr_p = sb("wr_p", [P, PIECES, E], BF16)
        br_sb = sb("br_sb", [P, E])
        sel = sb("sel", [2 * E, NP, P], F16)

        attempts = sb("attempts", [P, J])
        valid, feat_t = sb("valid", [P, J]), sb("feat_t", [P, J])
        feat = sb("feat", [P, NF, J])
        feat_r = sb("feat_r", [P, NF, J])
        stat_h0 = sb("stat_h0", [P, J, 6])
        mean_h0, var_h0 = sb("mean_h0", [P, J]), sb("var_h0", [P, J])
        rstd, u_scale = sb("rstd", [P, J]), sb("u_scale", [P, J])
        newton = sb("newton", [P, J])
        upd_sum, recip_T = sb("upd_sum", [P, J]), sb("recip_T", [P, J])
        upd_sum_T, recip_j = sb("upd_sum_T", [J, P]), sb("recip_j", [J, P])

        h_all = sb("h_all", [P, J * D])
        rows_or_scaled = sb("rows_or_scaled", [P, J * P], BF16)
        feat_parts = sb("feat_parts", [P, J, P], BF16)
        feat_k = sb("feat_k", [P, J * P], BF16)
        same = sb("same", [P, 2, CAUSAL], BF16)

        def over(array, at, *shape):
            n = int(np.prod(shape))
            flat = array.bitcast(F32)[:, at:at + n]
            return flat.rearrange("p (a b) -> p a b", a=shape[0]) if len(shape) == 2 else flat

        row_u, row_w, row_nz, row_any, row_one, row_d = [over(feat_k[0:B, :], n * S, S) for n in range(6)]
        parts_flat = feat_parts[:].rearrange("p j n -> p (j n)")
        relu_b = over(parts_flat, 0, NK, S)
        factor = sb("factor", [P, S])
        xs = over(parts_flat, 2 * S, NK, S)
        pm = over(parts_flat, 9 * S, CAUSAL)
        ub, ub_t = sb("ub", [P, C, D]), sb("ub_t", [P, C, D])
        st_a, t_a = sb("st_a", [P, C, 6]), sb("t_a", [P, 4, C])
        an = sb("an", [P, C, D])
        a_p, aT = sb("a_p", [P, C, 2 * D], F16), sb("aT", [P, S], F16)
        ys = over(parts_flat, 4 * S, NK, S)
        power = sb("power", [P, C])
        z_sb = sb("z_sb", [P, C, D])
        st_z, t_z = sb("st_z", [P, C, 6]), sb("t_z", [P, 4, C])
        st_h, t_h = sb("st_h", [P, C, 6]), sb("t_h", [P, 4, C])
        h_mean, h_scale = sb("h_mean", [P, C]), sb("h_scale", [P, C])
        xc, xc_t = sb("xc", [P, C, D]), sb("xc_t", [P, C, D])
        x_p, xT = sb("x_p", [P, C, 2 * D], F16), sb("xT", [P, S], F16)
        lg, top, top_i = sb("lg", [P, C, E]), sb("top", [P, C, E]), sb("top_i", [P, C, E], U32)
        gap, tanh_g, wgt = sb("gap", [P, C]), sb("tanh_g", [P, C]), sb("wgt", [P, 2, C])
        pick = sb("pick", [P, 2, C, E])
        w_p, wT = sb("w_p", [P, C, 2 * E], F16), sb("wT", [2 * E, S], F16)
        wb = over(feat_k[:], E * S, NP, S)
        hid = over(feat_k[:], 0, E, S)
        tm = over(feat_k[:], (E + NP) * S, NP, S)
        half, acc = over(parts_flat, 6 * S, 2, S), over(parts_flat, 8 * S, S)
        o_sb = sb("o_sb", [P, C, D])

        ld_x, ld_c, ld_w, ld_w2 = sem("ld_x"), sem("ld_c"), sem("ld_w"), sem("ld_w2")
        ld_rows = [sem(f"ld_rows{n}") for n in range(4)]
        ld_table, ld_row_u, ld_recip, ld_factor = sem("ld_table"), sem("ld_row_u"), sem("ld_recip"), sem("ld_factor")
        st_rows, st_table, st_upd, st_recip, st_out = (sem("st_rows"), sem("st_table"), sem("st_upd"),
                                                       sem("st_recip"), sem("st_out"))
        zeroed, table_zeroed = sem("zeroed"), sem("table_zeroed")
        ints_f, rows_ready, sel_ready = sem("ints_f"), sem("rows_ready"), sem("sel_ready")
        ids_ready, gammas_in, wide_beta = sem("ids_ready"), sem("gammas_in"), sem("wide_beta")
        pe_tok_T, pe_wT, pe_bias = sem("pe_tok_T"), sem("pe_wT"), sem("pe_bias")
        projT_in, pe_tab, tab_c_in, pe_tabT, tabT_in, pe_g, table_ready = (
            sem("projT_in"), sem("pe_tab"), sem("tab_c_in"), sem("pe_tabT"), sem("tabT_in"), sem("pe_g"),
            sem("table_ready"))
        parts_in, pe_parts, weights_in = sem("parts_in"), sem("pe_parts"), sem("weights_in")
        dve_set = sem("dve_set")
        tok_in = sem("tok_in")
        same_in, pe_counts = sem("same_in"), sem("pe_counts")
        feats_in, pe_featT, featT_in = sem("feats_in"), sem("pe_featT"), sem("featT_in")
        pe_h0, pe_g2 = sem("pe_h0"), sem("pe_g2")
        h0_in, sum_a, sum_v, h0_stats = sem("h0_in"), sem("sum_a"), sem("sum_v"), sem("h0_stats")
        upd_in, pe_updT, updT_in, pe_recT = sem("upd_in"), sem("pe_updT"), sem("updT_in"), sem("pe_recT")
        scalars_in, recip_ready = sem("scalars_in"), sem("recip_ready")
        scaled_in, pe_scT, scT_in = sem("scaled_in"), sem("pe_scT"), sem("scT_in")
        pe_pre, pe_s, pe_a, pe_aT, pe_y, pe_z = (sem("pe_pre"), sem("pe_s"), sem("pe_a"), sem("pe_aT"), sem("pe_y"),
                                                 sem("pe_z"))
        pe_xT, pe_lg, pe_hid, pe_zz, pe_wT2, pe_wb, pe_fold = (
            sem("pe_xT"), sem("pe_lg"), sem("pe_hid"), sem("pe_zz"), sem("pe_wT2"), sem("pe_wb"), sem("pe_fold"))
        ac_relu, ac_off, ac_ah, ac_aT, ac_xh, ac_xT = (sem("ac_relu"), sem("ac_off"), sem("ac_ah"), sem("ac_aT"),
                                                       sem("ac_xh"), sem("ac_xT"))
        ac_gelu, ac_tanh, ac_wT, ac_wb = sem("ac_gelu"), sem("ac_tanh"), sem("ac_wT"), sem("ac_wb")
        ac_z = sem("ac_z")
        dv_x, dv_diag, dv_an, dv_y, dv_h = sem("dv_x"), sem("dv_diag"), sem("dv_an"), sem("dv_y"), sem("dv_h")
        dv_gap, dv_w, dv_tm, dv_out, dv_lg = sem("dv_gap"), sem("dv_w"), sem("dv_tm"), sem("dv_out"), sem("dv_lg")
        dv_var_z = sem("dv_var_z")
        att_steps, res_steps, mlp_steps = sem("att_steps"), sem("res_steps"), sem("mlp_steps")
        pool_steps = sem("pool_steps")
        dv_passed = sem("dv_passed")
        po_in, po_ub, po_al, po_xt, po_xc = sem("po_in"), sem("po_ub"), sem("po_al"), sem("po_xt"), sem("po_xc")
        po_xl, po_half, po_acc = sem("po_xl"), sem("po_half"), sem("po_acc")
        po_z_scale, po_h_scale = sem("po_z_scale"), sem("po_h_scale")

        mA, mB, tp, az, hA, hB, zb, ly = bank
        n_bank, h_bank = [mA, mB], [hA, hB]
        tp_h = tp[:, :].bitcast(F16)
        ly_lg = ly[:, 0:C * PIECES * E]
        ly_w = ly[:, 256:512].bitcast(F16)
        ly_y = ly[:, 256:512]
        az_a = az[:, 0:C * D].rearrange("p (c d) -> p c d", c=C)
        az_z = az[:, C * D:2 * C * D].rearrange("p (c d) -> p c d", c=C)
        counts = bank[0][:, :].rearrange("p (j k) -> p j k", k=4)

        def wide(ap, n):
            return ap.unsqueeze(2).to_broadcast([ap.shape[0], ap.shape[1], n])

        def h_of(b):
            return h_all[:, bass.ds(b * C * D, C * D)].rearrange("p (c d) -> p c d", c=C)

        block = ctx.enter_context(nc.Block())

        @block.sync
        def _(sp):
            sp.dma_start(xi[:], x.rearrange("b (c p) -> (b c) p", p=P)).then_inc(ld_x, 16)
            sp.dma_start(ri[:], r.rearrange("b (c p) -> (b c) p", p=P)).then_inc(ld_x, 16)
            sp.dma_start(ident_f[:], ident).then_inc(ld_c, 16)
            sp.dma_start(mask_sb[:], masks).then_inc(ld_c, 16)
            sp.dma_start(dec[:], decays).then_inc(ld_c, 16)
            sp.dma_start(proj_sb[:], proj_w).then_inc(ld_w, 16)
            sp.dma_start(projb[:], proj_b.unsqueeze(0)).then_inc(ld_w, 16)
            sp.wait_ge(zeroed, 1)
            sp.dma_start(s4[0:D3, 0:1], skill_w.unsqueeze(1)).then_inc(ld_w, 16)
            sp.dma_start(s4[D3:2 * D3, 1:2], att_w.unsqueeze(1)).then_inc(ld_w, 16)
            sp.dma_start(s4[2 * D3:D, 2:3], mast_w.unsqueeze(1)).then_inc(ld_w, 16)
            sp.dma_start(s4[0:D3, 3:4], skill_b.unsqueeze(1)).then_inc(ld_w, 16)
            sp.dma_start(s4[D3:2 * D3, 3:4], att_b.unsqueeze(1)).then_inc(ld_w, 16)
            sp.dma_start(s4[2 * D3:D, 3:4], mast_b.unsqueeze(1)).then_inc(ld_w, 16)
            sp.dma_start(dx_sb[:], Dx.rearrange("(k p) d -> p k d", p=P)).then_inc(ld_w, 16)
            sp.wait_ge(rows_ready, 1)
            sp.dma_start(skill_row_d, skill_row[:]).then_inc(st_rows, 16)
            sp.wait_ge(st_rows, 16)
            rows = skill_row_d.rearrange("j p -> (j p)").unsqueeze(0)
            n = J * P // 4
            for q in range(4):
                sp.dma_start(rows_or_scaled[:, q * n:(q + 1) * n],
                             rows[:, q * n:(q + 1) * n].to_broadcast([P, n])).then_inc(ld_rows[q], 16)
            sp.wait_ge(table_ready, 1)
            sp.dma_start(table_d, table_p[:]).then_inc(st_table, 16)
            sp.wait_ge(st_table, 16)
            sp.wait_ge(table_zeroed, 1)
            for g in range(PIECES):
                for piece in range(PIECES):
                    row = NF * (PIECES * g + piece)
                    sp.dma_start(table_k[row:row + NF, :], table_d[:, g, :]).then_inc(ld_table, 16)
            sp.wait_ge(updT_in, 1)
            sp.dma_start(upd_sum_d, upd_sum_T[:]).then_inc(st_upd, 16)
            sp.wait_ge(st_upd, 16)
            sp.dma_start(row_u, upd_sum_d.rearrange("(b c) p -> b (c p)", c=C)).then_inc(ld_row_u, 16)
            sp.wait_ge(scalars_in, 1)
            sp.dma_start(recip_d, row_w).then_inc(st_recip, 16)
            sp.dma_start(factor_d, row_nz).then_inc(st_recip, 16)
            sp.wait_ge(st_recip, 32)
            sp.dma_start(recip_j[:], recip_d.rearrange("b (c p) -> (b c) p", p=P)).then_inc(ld_recip, 16)

            def load_factor(b):
                wait(sp, dv_x, 2 * b)
                sp.dma_start(factor[:], factor_d[bass.ds(b, 1), :].to_broadcast([P, S])).then_inc(ld_factor, 16)

            def store(b):
                sp.wait_ge(dv_out, b + 1)
                sp.dma_start(out[bass.ds(b, 1)].rearrange("o (c p) d -> p (o c) d", p=P), o_sb[:]).then_inc(st_out, 16)

            for b in range(4):
                load_factor(b)
            with sp.Fori(3, B - 1) as i:
                load_factor(i + 1)
                store(i - 3)
            for b in range(B - 4, B):
                store(b)
            sp.wait_ge(st_out, 16 * B)

        @block.gpsimd
        def _(pool):
            pool.memset(s4[:], 0.0).then_inc(zeroed, 1)
            pool.dma_start(gam2[0:D, :], gamma.unsqueeze(1)).then_inc(ld_w2, 16)
            pool.dma_start(gam2[D:P, :], gamma.unsqueeze(1)).then_inc(ld_w2, 16)
            pool.dma_start(bet[:], beta.unsqueeze(1)).then_inc(ld_w2, 16)
            pool.dma_start(w1_sb[:], W1.rearrange("e d h -> d e h")).then_inc(ld_w2, 16)
            pool.dma_start(b1_sb[:], b1).then_inc(ld_w2, 16)
            pool.dma_start(dy_sb[:], Dy.rearrange("(k p) d -> p k d", p=P)).then_inc(ld_w2, 16)
            pool.dma_start(e_sb[:], Ea).then_inc(ld_w2, 16)
            pool.dma_start(wr_sb[0:D, :], Wr).then_inc(ld_w2, 16)
            pool.dma_start(wr_sb[D:P, :], Wr).then_inc(ld_w2, 16)
            pool.dma_start(br_sb[:], br.unsqueeze(0).to_broadcast([P, E])).then_inc(ld_w2, 16)
            pool.dma_start(w2_sb[:], W2.rearrange("e h d -> h e d")).then_inc(ld_w2, 16)
            pool.dma_start(b2_sb[:], b2.rearrange("(q two) d -> q (two d)", two=2)).then_inc(ld_w2, 16)
            pool.memset(sel[:], 1.0).then_inc(pool_steps, 1)
            pool.wait_ge(pool_steps, 1)
            low = sel[:, :, :].rearrange("k q (two m) -> k q two m", two=2)
            pool.affine_select(out=low, in_=low, compare_op=ALU.is_ge, fill=0.0, base=0,
                               pattern=[[-2, NP], [-1, 2], [0, D]], channel_multiplier=1).then_inc(pool_steps, 1)
            pool.wait_ge(pool_steps, 2)
            for n, d in enumerate(list(range(1, E)) + list(range(E + 1, 2 * E))):
                pool.affine_select(out=low, in_=low, compare_op=ALU.not_equal, fill=0.0, base=-d,
                                   pattern=[[-2, NP], [-1, 2], [0, D]], channel_multiplier=1).then_inc(pool_steps, 1)
                pool.wait_ge(pool_steps, 3 + n)
            pool.memset(power[:], -0.5).then_inc(pool_steps, 1)
            pool.wait_ge(pool_steps, 2 * E + 1)
            pool.nop().then_inc(sel_ready, 1)

            def centred_input(b):
                if isinstance(b, int) and b == 0:
                    pool.wait_ge(scaled_in, 1)
                    pool.wait_ge(h0_in, NG)
                wait(pool, po_ub, b)
                pool.tensor_tensor(ub_t[:], h_of(b), wide(mean_h0[:, bass.ds(b * C, C)], D), ALU.subtract)\
                    .then_inc(po_in, 1)

            def weighted_input(b):
                wait(pool, pe_a, b)
                pool.wait_ge(po_in, b + 1)
                pool.tensor_tensor(ub[:], ub_t[:], wide(u_scale[:, bass.ds(b * C, C)], D), ALU.mult).then_inc(po_ub, 1)

            def attn_low(b):
                pool.wait_ge(ac_ah, b + 1)
                pool.tensor_tensor(a_p[:, :, D:2 * D], an[:], a_p[:, :, 0:D], ALU.subtract).then_inc(po_al, 1)

            def z_scale(b):
                pool.wait_ge(dv_var_z, b + 1)
                pool.tensor_tensor(t_z[:, 3, :], t_z[:, 2, :], power[:], ALU.pow).then_inc(po_z_scale, 1)

            def centred(b):
                pool.wait_ge(dv_h, b + 1)
                wait(pool, po_xc, b)
                pool.tensor_tensor(h_scale[:], t_h[:, 2, :], power[:], ALU.pow).then_inc(po_h_scale, 1)
                pool.tensor_tensor(xc_t[:], h_of(b), wide(h_mean[:], D), ALU.subtract).then_inc(po_xt, 1)
                wait(pool, po_xl, b)
                pool.wait_ge(po_h_scale, b + 1)
                pool.wait_ge(po_xt, b + 1)
                pool.tensor_tensor(xc[:], xc_t[:], wide(h_scale[:], D), ALU.mult).then_inc(po_xc, 1)

            def centred_low(b):
                pool.wait_ge(ac_xh, b + 1)
                pool.tensor_tensor(x_p[:, :, D:2 * D], xc[:], x_p[:, :, 0:D], ALU.subtract).then_inc(po_xl, 1)

            def add_pairs(b, n):
                pool.wait_ge(dv_tm, NP * b + 2 * n + 2)
                wait(pool, po_acc, b)
                pool.tensor_tensor(half[:, n, :], tm[:, 2 * n, :], tm[:, 2 * n + 1, :], ALU.add).then_inc(po_half, 1)

            def add_halves(b):
                pool.wait_ge(po_half, 2 * b + 2)
                wait(pool, pe_fold, b)
                pool.tensor_tensor(acc[:], half[:, 0, :], half[:, 1, :], ALU.add).then_inc(po_acc, 1)

            def turn(i, att, res, mlp, done, ahead):
                if done:
                    add_pairs(i - 3, 1)
                if res:
                    z_scale(i - 1)
                if done:
                    add_halves(i - 3)
                if res:
                    centred(i - 1)
                if ahead:
                    centred_input(i + 1)
                if res:
                    centred_low(i - 1)
                if ahead:
                    weighted_input(i + 1)
                if att:
                    attn_low(i)
                if mlp:
                    add_pairs(i - 2, 0)

            centred_input(0)
            weighted_input(0)
            turn(0, True, False, False, False, True)
            turn(1, True, True, False, False, True)
            turn(2, True, True, True, False, True)
            with pool.Fori(3, B - 1) as i:
                turn(i, True, True, True, True, True)
            turn(B - 1, True, True, True, True, False)
            turn(B, False, True, True, True, False)
            turn(B + 1, False, False, True, True, False)
            add_pairs(B - 1, 1)
            add_halves(B - 1)

        @block.scalar
        def _(act):
            def group(g):
                act.wait_ge(pe_h0, g + 1)
                act.activation(h_all[:, bass.ds(g * GROUP * D, GROUP * D)], bank[1][:, :], ACT.Copy)\
                   .then_inc(h0_in, 1)
                for n in range(0, GROUP // 2, 2):
                    act.wait_ge(pe_g2, (GROUP // 2) * g + n + 1)
                    for k in range(2):
                        pre = bank[2 + n][:, k * NS:(k + 1) * NS]
                        act.activation(pre, pre, ACT.Relu,
                                       accum_out=upd_sum[:, bass.ds(g * GROUP + 2 * n + k, 1)]).then_inc(sum_a, 1)

            with act.Fori(0, NG) as g:
                group(g)
            with act.Fori(0, NG // 2) as g:
                act.wait_ge(pe_scT, 2 * g + 1)
                act.activation(rows_or_scaled[:, bass.ds(g * 2 * GROUP * P, GROUP * P)], bank[0][:, :].bitcast(BF16),
                               ACT.Copy).then_inc(scT_in, 1)

            def relu(b):
                act.wait_ge(pe_pre, b + 1)
                wait(act, dv_x, NK * b)
                for k in range(NK):
                    act.activation(relu_b[:, k, :], n_bank[k][:, :], ACT.Relu).then_inc(ac_relu, 1)

            def off_diagonal(b, sc):
                act.wait_ge(dv_diag, C * b + sc + 1)
                wait(act, pe_a, b)
                act.activation(pm[:, OFF[sc] + P:OFF[sc] + WIDE[sc]], n_bank[sc % 2][:, P:WIDE[sc]], ACT.Copy)\
                   .then_inc(ac_off, 1)

            def attn_high(b):
                act.wait_ge(dv_an, b + 1)
                wait(act, pe_aT, b)
                act.activation(a_p[:, :, 0:D], an[:], ACT.Copy).then_inc(ac_ah, 1)

            def attn_T(b):
                act.wait_ge(pe_aT, b + 1)
                wait(act, pe_y, NK * b)
                act.activation(aT[:], ly_w[:, :], ACT.Copy).then_inc(ac_aT, 1)

            def centred_high(b):
                act.wait_ge(po_xc, b + 1)
                wait(act, pe_xT, b)
                act.activation(x_p[:, :, 0:D], xc[:], ACT.Copy).then_inc(ac_xh, 1)

            def centred_T(b):
                act.wait_ge(pe_xT, b + 1)
                wait(act, pe_hid, E * b)
                wait(act, pe_lg, b)
                act.activation(xT[:], tp_h[:, 0:S], ACT.Copy).then_inc(ac_xT, 1)

            def gelu(b, e):
                act.wait_ge(pe_hid, E * b + e + 1)
                wait(act, pe_zz, NP * b)
                act.activation(hid[:, e, :], h_bank[e % 2][:, :], ACT.Gelu, bias=b1T[:, e:e + 1],
                               scale=w1_scale[:, e:e + 1]).then_inc(ac_gelu, 1)

            def tanh(b):
                act.wait_ge(dv_gap, b + 1)
                act.activation(tanh_g[:], gap[:], ACT.Tanh, scale=0.5).then_inc(ac_tanh, 1)

            def weights_T(b):
                act.wait_ge(pe_wT2, b + 1)
                wait(act, pe_wb, NP * b)
                act.activation(wT[:], ly_w[0:2 * E, :], ACT.Copy).then_inc(ac_wT, 1)

            def weights_wide(b, q):
                act.wait_ge(pe_wb, NP * b + q + 1)
                wait(act, dv_tm, NP * b - NP + q + 1)
                act.activation(wb[:, q, :], tp[:, :], ACT.Copy).then_inc(ac_wb, 1)

            def z_copy(b):
                act.wait_ge(pe_z, b + 1)
                wait(act, dv_h, b)
                act.activation(z_sb[:], az_z, ACT.Copy).then_inc(ac_z, 1)

            def turn(i, att, res, mlp, done, ahead):
                r, k = i - 1, i - 2
                if att:
                    off_diagonal(i, 0)
                if mlp:
                    tanh(k)
                    gelu(k, 0)
                if att:
                    off_diagonal(i, 1)
                if mlp:
                    gelu(k, 1)
                if att:
                    off_diagonal(i, 2)
                if mlp:
                    weights_T(k)
                    gelu(k, 2)
                    weights_wide(k, 0)
                if res:
                    centred_high(r)
                if mlp:
                    gelu(k, 3)
                    weights_wide(k, 1)
                if att:
                    attn_high(i)
                if mlp:
                    gelu(k, 4)
                    gelu(k, 5)
                if att:
                    attn_T(i)
                if mlp:
                    gelu(k, 6)
                    weights_wide(k, 2)
                    gelu(k, 7)
                    weights_wide(k, 3)
                if ahead:
                    relu(i + 1)
                if res:
                    centred_T(r)
                if att:
                    z_copy(i)

            relu(0)
            act.wait_ge(weights_in, 1)
            turn(0, True, False, False, False, True)
            turn(1, True, True, False, False, True)
            turn(2, True, True, True, False, True)
            with act.Fori(3, B - 1) as i:
                turn(i, True, True, True, True, True)
            turn(B - 1, True, True, True, True, False)
            turn(B, False, True, True, True, False)
            turn(B + 1, False, False, True, True, False)

        @block.vector
        def _(dve):
            s = Steps(dve, dve_set)

            def op(instruction):
                s.done(instruction)
                s.last()

            def rsqrt(y, v, t, chain):
                chain.done(dve.tensor_scalar(y.bitcast(I32), v.bitcast(I32), -0.5, RSQRT_SEED, ALU.mult, ALU.add))
                for _ in range(3):
                    chain.last()
                    chain.done(dve.tensor_tensor(t, y, y, ALU.mult))
                    chain.last()
                    chain.done(dve.scalar_tensor_tensor(t, t, -0.5, v, ALU.mult, ALU.mult))
                    chain.last()
                    chain.done(dve.scalar_tensor_tensor(y, t, 1.5, y, ALU.add, ALU.mult))

            def variance(st, var, t, chain):
                chain.done(dve.tensor_tensor(t, st[:, :, 1], st[:, :, 4], ALU.subtract))
                chain.done(dve.tensor_tensor(var, st[:, :, 2], st[:, :, 5], ALU.add))
                chain.last()
                chain.done(dve.scalar_tensor_tensor(t, t, 0.25, t, ALU.mult, ALU.mult))
                chain.last()
                chain.done(dve.scalar_tensor_tensor(var, var, 1.0 / D, t, ALU.mult, ALU.add))

            def mean(st, m, t, chain):
                chain.done(dve.tensor_tensor(t, st[:, :, 1], st[:, :, 4], ALU.add))
                chain.last()
                chain.done(dve.tensor_scalar(m, t, 0.5, None, ALU.mult))

            dve.wait_ge(ld_x, 32)
            dve.tensor_copy(xf[:], xi[:]).then_inc(ints_f, 1)
            dve.tensor_copy(rf[:], ri[:]).then_inc(ints_f, 1)
            dve.wait_ge(ints_f, 2)
            dve.tensor_scalar(skill_row[:], xf[:], float(SKILLS), -1.0, ALU.min, ALU.max).then_inc(rows_ready, 1)
            dve.wait_ge(ld_c, 48)
            dve.tensor_copy(ident_h[:], ident_f[:]).then_inc(ids_ready, 1)
            dve.tensor_copy(ident_b[:], ident_f[:]).then_inc(ids_ready, 1)
            op(dve.tensor_copy(upto_b[:], mask_sb[:, 0:P]))
            op(dve.tensor_copy(fold_f[0:D, :], ident_f[0:D, 0:D]))
            op(dve.tensor_copy(fold_f[D:P, :], ident_f[D:P, D:P]))
            op(dve.memset(ones_row[:], 0.0))
            dve.memset(ones_row[:, NF - 1:NF], 1.0).then_inc(ids_ready, 1)
            dve.memset(feat_parts[:].rearrange("p j n -> p (j n)").bitcast(U32), 0).then_inc(ids_ready, 1)
            dve.memset(table_k[:], 0.0).then_inc(table_zeroed, 1)

            dve.wait_ge(pe_tok_T, 1)
            op(dve.tensor_copy(skill_T[:], bank[1][:, 0:P]))
            op(dve.tensor_copy(right_T[:], bank[1][:, P:2 * P]))
            op(dve.memset(right_parts[:], 1.0))
            op(dve.tensor_copy(right_parts[:, :, 1], right_T[:]))
            op(dve.tensor_tensor(feat_t[:], right_T[:], right_parts[:, :, 1], ALU.subtract))
            op(dve.tensor_copy(right_parts[:, :, 2], feat_t[:]))
            dve.tensor_tensor(right_parts[:, :, 3], feat_t[:], right_parts[:, :, 2], ALU.subtract).then_inc(tok_in, 1)

            def equal(b, side):
                wait(dve, pe_counts, b - 1)
                for sc in range(C):
                    row = bass.ds(b * S + sc * P, P)
                    mine = skill_T[:, bass.ds(b * C + sc, 1)]
                    last = dve.scalar_tensor_tensor(same[:, side, OFF[sc]:OFF[sc] + P], rows_or_scaled[:, row], mine,
                                                    upto_b[:], ALU.is_equal, ALU.mult)
                    if sc < C - 1:
                        rest = bass.ds(b * S + (sc + 1) * P, WIDE[sc] - P)
                        last.then_inc(same_in, 1)
                        last = dve.tensor_scalar(same[:, side, OFF[sc] + P:OFF[sc] + WIDE[sc]],
                                                 rows_or_scaled[:, rest], mine, None, ALU.is_equal)
                    last.then_inc(same_in, 1)

            for q in range(4):
                dve.wait_ge(ld_rows[q], 16)
                n = B // 8
                if q == 0:
                    equal(0, 0)
                    equal(1, 1)
                with dve.Fori(max(1, n * q), n * (q + 1)) as pair:
                    equal(2 * pair, 0)
                    equal(2 * pair + 1, 1)

            op(dve.tensor_scalar(valid[:], skill_T[:], 0.0, None, ALU.is_ge))
            op(dve.scalar_tensor_tensor(valid[:], skill_T[:], float(SKILLS), valid[:], ALU.is_lt, ALU.mult))
            dve.wait_ge(pe_counts, B)
            op(dve.tensor_copy(attempts[:], counts[:, :, 0]))
            op(dve.tensor_scalar(feat_t[:], attempts[:], 1.0, None, ALU.max))
            op(dve.reciprocal(feat_t[:], feat_t[:]))
            op(dve.tensor_reduce(newton[:], counts[:, :, 1:4], AX_X, ALU.add))
            op(dve.tensor_tensor(feat_t[:], feat_t[:], newton[:], ALU.mult))
            op(dve.tensor_tensor(feat[:, 0, :], skill_T[:], valid[:], ALU.mult))
            op(dve.tensor_tensor(feat[:, 1, :], attempts[:], valid[:], ALU.mult))
            op(dve.tensor_tensor(feat[:, 2, :], feat_t[:], valid[:], ALU.mult))
            op(dve.tensor_copy(feat[:, 3, :], valid[:]))

            def cut(source):
                for piece in range(PIECES):
                    at = feat_parts[:, :, NF * piece:NF * (piece + 1)].rearrange("p j f -> p f j")
                    op(dve.tensor_copy(at, source))
                    if piece < PIECES - 1:
                        op(dve.tensor_tensor(feat_r[:], source, at, ALU.subtract))
                        source = feat_r[:]
                n = NF * PIECES
                op(dve.tensor_copy(feat_parts[:, :, n:2 * n], feat_parts[:, :, 0:n]))
                op(dve.tensor_copy(feat_parts[:, :, 2 * n:3 * n], feat_parts[:, :, 0:n]))

            cut(feat[:])
            dve.nop().then_inc(feats_in, 1)

            dve.wait_ge(pe_wT, 1)
            dve.tensor_copy(projT[:], bank[2][0:D, 0:D]).then_inc(projT_in, 1)
            op(dve.tensor_copy(dxT[:], bank[2][0:D, D:D + NS]))
            dve.wait_ge(pe_tab, 1)
            op(dve.tensor_copy(table[:, 0:D], bank[3][0:NF, 0:D]))
            op(dve.tensor_reduce(table_m[:], table[:, 0:D], AX_X, ALU.add))
            op(dve.tensor_scalar(table_m[:], table_m[:], 1.0 / D, None, ALU.mult))
            dve.tensor_scalar(table_c[:], table[:, 0:D], table_m[:, 0:1], None, ALU.subtract).then_inc(tab_c_in, 1)
            dve.wait_ge(pe_tabT, 1)
            dve.tensor_copy(table_cT[:], bank[3][0:D, D:D + NF]).then_inc(tabT_in, 1)
            dve.wait_ge(pe_g, 1)
            op(dve.tensor_copy(table[:, D:D + NS], bank[3][0:NF, P:P + NS]))
            op(dve.tensor_copy(table_p[:, 0, :], table[:]))
            op(dve.tensor_tensor(table_r[:], table[:], table_p[:, 0, :], ALU.subtract))
            op(dve.tensor_copy(table_p[:, 1, :], table_r[:]))
            op(dve.tensor_tensor(table_r[:], table_r[:], table_p[:, 1, :], ALU.subtract))
            dve.tensor_copy(table_p[:, 2, :], table_r[:]).then_inc(table_ready, 1)

            dve.wait_ge(ld_w2, 16 * 12)
            dve.tensor_scalar(w1g[:], w1_sb[:], gam2[0:D, 0:1], None, ALU.mult).then_inc(gammas_in, 1)
            op(dve.memset(bet_wide[:], 0.0))
            dve.tensor_scalar(bet_wide[:], bet_wide[:], bet[:, 0:1], None, ALU.add).then_inc(wide_beta, 1)
            op(dve.tensor_scalar(wr_g[:], wr_sb[:], gam2[:, 0:1], None, ALU.mult))
            op(dve.tensor_copy(wr_p[:, 0, :], wr_g[:]))
            op(dve.tensor_tensor(wr_r[:], wr_g[:], wr_p[:, 0, :], ALU.subtract))
            op(dve.tensor_copy(wr_p[:, 1, :], wr_r[:]))
            op(dve.tensor_tensor(wr_p[:, 2, :], wr_r[:], wr_p[:, 1, :], ALU.subtract))
            dve.wait_ge(pe_bias, 1)
            op(dve.tensor_copy(b1T[:], bank[5][:, 16:24]))
            op(dve.tensor_copy(b2_pair[:], bank[5][:, 24:24 + NP]))
            op(dve.tensor_tensor(b1T[:], b1T[:], bank[5][:, 0:E], ALU.add))
            op(dve.tensor_tensor(br_sb[:], br_sb[:], bank[5][:, E:2 * E], ALU.add))

            def power_of_two(scale, inverse):
                op(dve.tensor_scalar(scale, scale, 1e-30, None, ALU.max))
                op(dve.tensor_scalar(scale.bitcast(I32), scale.bitcast(I32), EXP_MASK, None, ALU.bitwise_and))
                op(dve.reciprocal(inverse, scale))

            w1T_ps = bank[6][:, :].rearrange("h (e d) -> h e d", e=E)
            op(dve.tensor_reduce(w1_scale[:], w1T_ps, AX_X, ALU.max, apply_absolute_value=True))
            power_of_two(w1_scale[:], w1_inv[:])
            op(dve.tensor_tensor(w1T[:], w1T_ps, wide(w1_inv[:], D), ALU.mult))
            op(dve.tensor_copy(w1_p[:, 0, :, 0, :], w1T[:]))
            op(dve.tensor_copy(w1_p[:, 0, :, 1, :], w1T[:]))
            op(dve.tensor_tensor(w1_p[:, 1, :, 0, :], w1T[:], w1_p[:, 0, :, 0, :], ALU.subtract))
            op(dve.tensor_copy(w1_p[:, 1, :, 1, :], w1_p[:, 1, :, 0, :]))
            op(dve.tensor_reduce(dy_scale[:, 0:NK], dy_sb[:], AX_X, ALU.max, apply_absolute_value=True))
            power_of_two(dy_scale[:, 0:NK], dy_scale[:, NK:2 * NK])
            op(dve.tensor_tensor(dy_sb[:], dy_sb[:], wide(dy_scale[:, NK:2 * NK], D), ALU.mult))
            op(dve.tensor_copy(dy_p[:, 0, :, 0, :], dy_sb[:]))
            op(dve.tensor_copy(dy_p[:, 0, :, 1, :], dy_sb[:]))
            op(dve.tensor_tensor(dy_p[:, 1, :, 0, :], dy_sb[:], dy_p[:, 0, :, 0, :], ALU.subtract))
            dve.tensor_copy(dy_p[:, 1, :, 1, :], dy_p[:, 1, :, 0, :]).then_inc(parts_in, 1)
            op(dve.tensor_copy(eT[:].rearrange("p k d -> p (k d)"), bank[5][:, P:2 * P]))
            op(dve.tensor_reduce(e_mean[:], eT[:], AX_X, ALU.add))
            op(dve.tensor_scalar(e_mean[:], e_mean[:], 1.0 / D, None, ALU.mult))
            op(dve.tensor_tensor(eT[:], eT[:], wide(e_mean[:], D), ALU.subtract))
            op(dve.tensor_tensor(eT[:], eT[:], wide(dy_scale[:, 0:NK], D), ALU.mult))
            dve.wait_ge(pe_parts, 1)
            op(dve.tensor_copy(w1k[:, 0].rearrange("p e h -> p (e h)"), bank[2][:, :].bitcast(F16)))
            op(dve.tensor_copy(w1k[:, 1].rearrange("p e h -> p (e h)"), bank[3][:, :].bitcast(F16)))
            dve.tensor_copy(dyT[:].rearrange("p k n -> p (k n)"), bank[4][:, 0:NS].bitcast(F16)).then_inc(weights_in, 1)

            def group(g):
                dve.wait_ge(pe_featT, g + 1)
                dve.tensor_copy(feat_k[:, bass.ds(g * GROUP * P, GROUP * P)], bank[0][:, :].bitcast(BF16))\
                   .then_inc(featT_in, 1)
                dve.wait_ge(h0_in, g + 1)
                for n in range(GROUP):
                    at = stat_h0[:, bass.ds(g * GROUP + n, 1), :].rearrange("p o k -> p (o k)")
                    dve.bn_stats(at, h_all[:, bass.ds((g * GROUP + n) * D, D)]).then_inc(h0_stats, 1)
                for n in range(1, GROUP // 2, 2):
                    dve.wait_ge(pe_g2, (GROUP // 2) * g + n + 1)
                    for k in range(2):
                        pre = bank[2 + n][:, k * NS:(k + 1) * NS]
                        dve.tensor_scalar(pre, pre, 0.0, None, ALU.max, ALU.add,
                                          accum_out=upd_sum[:, bass.ds(g * GROUP + 2 * n + k, 1)]).then_inc(sum_v, 1)

            with dve.Fori(0, NG) as g:
                group(g)
            dve.wait_ge(h0_stats, J)
            dve.wait_ge(sum_v, J // 2)
            dve.wait_ge(sum_a, J // 2)
            mean(stat_h0, mean_h0[:], feat_t[:], s)
            s.last()
            variance(stat_h0, var_h0[:], feat_t[:], s)
            s.last()
            op(dve.tensor_scalar(feat_t[:], var_h0[:], EPS, None, ALU.add))
            rsqrt(rstd[:], feat_t[:], newton[:], s)
            s.last()
            dve.tensor_tensor(upd_sum[:], upd_sum[:], rstd[:], ALU.mult).then_inc(upd_in, 1)
            op(dve.tensor_scalar(feat_t[:], var_h0[:], 1.0 + EPS, EPS * EPS, ALU.mult, ALU.add))
            rsqrt(u_scale[:], feat_t[:], newton[:], s)
            s.last()
            op(dve.tensor_tensor(u_scale[:].rearrange("p (b c) -> p b c", c=C),
                                 u_scale[:].rearrange("p (b c) -> p b c", c=C),
                                 dec[:, 0:C].unsqueeze(1).to_broadcast([P, B, C]), ALU.mult))
            dve.wait_ge(pe_updT, 1)
            dve.tensor_copy(upd_sum_T[:], bank[1][:, 0:P]).then_inc(updT_in, 1)

            grow = DECAY / L1_EPS
            dve.wait_ge(ld_row_u, 16)
            op(dve.tensor_scalar(row_w, row_u, 1.0 / L1_EPS, 1.0, ALU.mult, ALU.min))
            op(dve.tensor_scalar(row_nz, row_u, 0.0, None, ALU.is_gt))
            op(dve.memset(row_one, 0.0))
            op(dve.tensor_tensor_scan(row_any, row_nz, row_one, 0.0, ALU.max, ALU.add))
            op(dve.tensor_copy(row_one[:, 3:S], row_any[:, 0:S - 3]))
            op(dve.tensor_tensor(row_w, row_w, row_one, ALU.max))
            op(dve.tensor_scalar(row_one, row_one, -grow, grow, ALU.mult, ALU.add))
            op(dve.tensor_tensor_scan(row_any, row_one, row_w, 0.0, ALU.mult, ALU.add))
            op(dve.memset(row_d, 0.0))
            op(dve.tensor_scalar(row_d[:, 1:S], row_any[:, 0:S - 1], 1.0, DECAY, ALU.min, ALU.mult))
            op(dve.tensor_tensor(row_d, row_d, row_u, ALU.add))
            op(dve.tensor_scalar(row_d, row_d, L1_EPS, None, ALU.max))
            op(dve.reciprocal(row_w, row_d))
            dve.tensor_scalar(row_nz, row_w, DECAY, None, ALU.mult).then_inc(scalars_in, 1)
            dve.wait_ge(pe_recT, 1)
            op(dve.tensor_tensor(recip_T[:], rstd[:], bank[1][:, P:2 * P], ALU.mult))
            for f in range(NF):
                op(dve.tensor_tensor(feat[:, f, :], feat[:, f, :], recip_T[:], ALU.mult))
            cut(feat[:])
            dve.nop().then_inc(scaled_in, 1)
            with dve.Fori(0, NG // 2) as g:
                dve.wait_ge(pe_scT, 2 * g + 2)
                dve.tensor_copy(rows_or_scaled[:, bass.ds((2 * g + 1) * GROUP * P, GROUP * P)],
                                bank[1][:, :].bitcast(BF16)).then_inc(scT_in, 1)

            def scan(b):
                dve.wait_ge(ac_relu, NK * (b + 1))
                dve.wait_ge(ld_factor, 16 * (b + 1))
                wait(dve, pe_s, C * b)
                wait(dve, dv_y, NK * b)
                for k in range(NK):
                    dve.tensor_tensor_scan(xs[:, k, :], factor[:], relu_b[:, k, :], 0.0, ALU.mult, ALU.add)\
                       .then_inc(dv_x, 1)

            def diagonal(b, sc):
                dve.wait_ge(pe_s, C * b + sc + 1)
                wait(dve, pe_a, b)
                dve.tensor_tensor(pm[:, OFF[sc]:OFF[sc] + P], n_bank[sc % 2][:, 0:P], causal_f, ALU.mult)\
                   .then_inc(dv_diag, 1)

            def finish(b):
                dve.wait_ge(pe_fold, b + 1)
                wait(dve, st_out, 16 * b)
                dve.tensor_tensor(o_sb[:], ly_y.rearrange("p (c d) -> p c d", c=C), h_of(b), ALU.add)\
                   .then_inc(dv_out, 1)

            def halves(st, t, w, s):
                s.done(dve.tensor_tensor(t, st[:, :, 1], st[:, :, 4], ALU.subtract))
                s.done(dve.tensor_tensor(w, st[:, :, 2], st[:, :, 5], ALU.add))

            def attn_scale(b, s):
                t, v, q, w = t_a[:, 0, :], t_a[:, 1, :], t_a[:, 2, :], t_a[:, 3, :]
                dve.wait_ge(pe_a, b + 1)
                for c in range(C):
                    s.done(dve.bn_stats(st_a[:, c, :], az_a[:, c, :]))
                s.last()
                halves(st_a, t, w, s)
                s.last()
                s.done(dve.scalar_tensor_tensor(t, t, 0.25, t, ALU.mult, ALU.mult))
                s.done(dve.scalar_tensor_tensor(w, w, 1.0 / D, dec[:, C:2 * C], ALU.mult, ALU.add))
                s.last()
                s.done(dve.tensor_tensor(v, t, w, ALU.add))
                s.last()
                s.done(dve.tensor_scalar(q.bitcast(I32), v.bitcast(I32), -0.5, RSQRT_SEED, ALU.mult, ALU.add))
                s.last()
                wait(dve, po_al, b)
                dve.tensor_tensor(an[:], az_a, wide(q, D), ALU.mult).then_inc(dv_an, 1)
                s.done(dve.tensor_tensor(t, q, q, ALU.mult))
                s.last()
                s.done(dve.scalar_tensor_tensor(v, t, EPS, v, ALU.mult, ALU.mult))

            def gate(b, k):
                dve.wait_ge(pe_y, NK * b + k + 1)
                wait(dve, pe_z, b)
                dve.scalar_tensor_tensor(ys[:, k, :], n_bank[k][:, :], 0.0, xs[:, k, :], ALU.max, ALU.mult)\
                   .then_inc(dv_y, 1)

            def z_stats(b, s):
                dve.wait_ge(ac_z, b + 1)
                for c in range(C):
                    s.done(dve.bn_stats(st_z[:, c, :], z_sb[:, c, :]))

            def z_halves(b, s):
                s.last()
                halves(st_z, t_z[:, 0, :], t_z[:, 1, :], s)

            def z_parts(b, s):
                s.last()
                dve.wait_ge(att_steps, N_ATT * (b + 1))
                t, w = t_z[:, 0, :], t_z[:, 1, :]
                s.done(dve.scalar_tensor_tensor(t, t, 0.25, t, ALU.mult, ALU.mult))
                s.done(dve.scalar_tensor_tensor(w, w, 1.0 / D, t_a[:, 1, :], ALU.mult, ALU.add))

            def z_var(b, s):
                s.last()
                dve.tensor_tensor(t_z[:, 2, :], t_z[:, 0, :], t_z[:, 1, :], ALU.add).then_inc(dv_var_z, 1)

            def residual(b, s):
                dve.wait_ge(po_z_scale, b + 1)
                for c in range(C):
                    h = h_all[:, bass.ds(b * C * D + c * D, D)]
                    s.done(dve.scalar_tensor_tensor(h, z_sb[:, c, :], t_z[:, 3, c:c + 1], h, ALU.mult, ALU.add))

            def h_stats(b, s):
                s.last()
                dve.nop().then_inc(dv_passed, 1)
                for c in range(C):
                    s.done(dve.bn_stats(st_h[:, c, :], h_all[:, bass.ds(b * C * D + c * D, D)]))

            def h_halves(b, s):
                s.last()
                wait(dve, po_xc, b)
                halves(st_h, t_h[:, 0, :], t_h[:, 1, :], s)
                s.done(dve.tensor_tensor(t_h[:, 3, :], st_h[:, :, 1], st_h[:, :, 4], ALU.add))

            def h_parts(b, s):
                s.last()
                t, w = t_h[:, 0, :], t_h[:, 1, :]
                s.done(dve.scalar_tensor_tensor(t, t, 0.25, t, ALU.mult, ALU.mult))
                s.done(dve.tensor_scalar(w, w, (1.0 + EPS) / D, EPS * EPS, ALU.mult, ALU.add))
                s.done(dve.tensor_scalar(h_mean[:], t_h[:, 3, :], 0.5, None, ALU.mult))

            def h_var(b, s):
                s.last()
                dve.scalar_tensor_tensor(t_h[:, 2, :], t_h[:, 0, :], 1.0 + EPS, t_h[:, 1, :], ALU.mult, ALU.add)\
                   .then_inc(dv_h, 1)

            def logit_sum(b, s):
                dve.wait_ge(pe_lg, b + 1)
                dve.tensor_reduce(lg[:], ly_lg.rearrange("p (c k e) -> p c e k", c=C, k=PIECES), AX_X, ALU.add)\
                   .then_inc(dv_lg, 1)

            def logit_bias(b, s):
                dve.wait_ge(dv_lg, b + 1)
                s.done(dve.tensor_tensor(lg[:], lg[:], br_sb[:].unsqueeze(1).to_broadcast([P, C, E]), ALU.add))

            def largest(b, s):
                s.last()
                dve.nop().then_inc(dv_passed, 1)
                for c in range(C):
                    s.done(dve.max(top[:, c, :], lg[:, c, :]))

            def which(b, s):
                s.last()
                dve.tensor_tensor(gap[:], top[:, :, 0], top[:, :, 1], ALU.subtract).then_inc(dv_gap, 1)
                for c in range(C):
                    s.done(dve.max_index(top_i[:, c, :], top[:, c, :], lg[:, c, :]))

            def one_hot(b, s):
                s.last()
                iota = dec[:, 2 * C:2 * C + E].unsqueeze(1).to_broadcast([P, C, E])
                for k in range(2):
                    s.done(dve.tensor_tensor(pick[:, k], iota, wide(top_i[:, :, k], E), ALU.is_equal))

            def softmax(b, s):
                dve.wait_ge(ac_tanh, b + 1)
                s.done(dve.tensor_scalar(wgt[:, 0, :], tanh_g[:], 0.5, 0.5, ALU.mult, ALU.add))
                s.done(dve.tensor_scalar(wgt[:, 1, :], tanh_g[:], -0.5, 0.5, ALU.mult, ALU.add))

            def place(b, s):
                s.last()
                s.done(dve.tensor_tensor(pick[:].rearrange("p k c e -> p (k c) e"),
                                         pick[:].rearrange("p k c e -> p (k c) e"),
                                         wide(wgt[:].rearrange("p k c -> p (k c)"), E), ALU.mult))

            def merge(b, s):
                s.last()
                s.done(dve.tensor_tensor(pick[:, 0], pick[:, 0], pick[:, 1], ALU.add))

            def weight_high(b, s):
                s.last()
                wait(dve, pe_wT2, b)
                s.done(dve.tensor_copy(w_p[:, :, 0:E], pick[:, 0]))

            def weight_low(b, s):
                s.last()
                dve.tensor_tensor(w_p[:, :, E:2 * E], pick[:, 0], w_p[:, :, 0:E], ALU.subtract).then_inc(dv_w, 1)

            def weigh(b, q):
                dve.wait_ge(pe_zz, NP * b + q + 1)
                dve.wait_ge(ac_wb, NP * b + q + 1)
                wait(dve, po_acc, b)
                dve.scalar_tensor_tensor(tm[:, q, :], zb[:, :], b2_pair[:, q:q + 1], wb[:, q, :], ALU.add, ALU.mult)\
                   .then_inc(dv_tm, 1)

            def turn(i, att, res, mlp, done, ahead):
                r, k = i - 1, i - 2
                a = Steps(dve, att_steps, N_ATT * i)
                n = Steps(dve, res_steps, N_RES * r)
                m = Steps(dve, mlp_steps, N_MLP * k)
                for of_router, of_norm in ((logit_sum, z_stats), (logit_bias, z_halves), (largest, z_parts),
                                           (which, z_var), (one_hot, None)):
                    if mlp:
                        of_router(k, m)
                    if res and of_norm is not None:
                        of_norm(r, n)
                if att:
                    diagonal(i, 0)
                if mlp:
                    softmax(k, m)
                if res:
                    residual(r, n)
                if mlp:
                    place(k, m)
                if res:
                    h_stats(r, n)
                if mlp:
                    merge(k, m)
                if res:
                    h_halves(r, n)
                if mlp:
                    weight_high(k, m)
                if att:
                    diagonal(i, 1)
                if res:
                    h_parts(r, n)
                if mlp:
                    weight_low(k, m)
                if att:
                    diagonal(i, 2)
                if res:
                    h_var(r, n)
                if att:
                    diagonal(i, 3)
                if done:
                    finish(i - 3)
                if att:
                    attn_scale(i, a)
                if mlp:
                    weigh(k, 0)
                    weigh(k, 1)
                if att:
                    gate(i, 0)
                    gate(i, 1)
                if mlp:
                    weigh(k, 2)
                if ahead:
                    scan(i + 1)
                if mlp:
                    weigh(k, 3)
                assert a.n in (0, N_ATT) and n.n in (0, N_RES) and m.n in (0, N_MLP), (a.n, n.n, m.n)

            scan(0)
            turn(0, True, False, False, False, True)
            turn(1, True, True, False, False, True)
            turn(2, True, True, True, False, True)
            with dve.Fori(3, B - 1) as i:
                turn(i, True, True, True, True, True)
            turn(B - 1, True, True, True, True, False)
            turn(B, False, True, True, True, False)
            turn(B + 1, False, False, True, True, False)
            finish(B - 1)

        @block.tensor
        def _(pe):
            pe.wait_ge(ld_c, 48)
            pe.wait_ge(ints_f, 2)
            pe.transpose(bank[1][:, 0:P], xf[:], ident_f[:])
            pe.transpose(bank[1][:, P:2 * P], rf[:], ident_f[:]).then_inc(pe_tok_T, 1)
            pe.wait_ge(ld_w, 16 * 9)
            pe.transpose(bank[2][0:D, 0:D], proj_sb[:], ident_f[0:D, 0:D])
            for k in range(NK):
                last = pe.transpose(bank[2][0:D, D + k * P:D + (k + 1) * P], dx_sb[:, k, :], ident_f[:])
            last.then_inc(pe_wT, 1)

            def count(b, side):
                pe.wait_ge(same_in, (2 * C - 1) * (b + 1))
                for tc in range(C):
                    for sc in range(tc + 1):
                        at = OFF[sc] + P * (tc - sc)
                        last = pe.matmul(bank[0][:, bass.ds((b * C + tc) * 4, 4)], same[:, side, at:at + P],
                                         right_parts[:, bass.ds(b * C + sc, 1), :].rearrange("p o k -> p (o k)"),
                                         start=(sc == 0), stop=(sc == tc))
                last.then_inc(pe_counts, 1)

            pe.wait_ge(tok_in, 1)
            with pe.Fori(0, B // 2) as pair:
                count(2 * pair, 0)
                count(2 * pair + 1, 1)

            pe.wait_ge(projT_in, 1)
            pe.wait_ge(ids_ready, 4)
            pe.matmul(bank[3][0:NF, 0:D], s4[:], projT[:], start=True, stop=False)
            pe.matmul(bank[3][0:NF, 0:D], ones_row[:], projb[:], start=False, stop=True).then_inc(pe_tab, 1)
            pe.wait_ge(tab_c_in, 1)
            pe.transpose(bank[3][0:D, D:D + NF], table_c[:], ident_f[0:NF, 0:NF]).then_inc(pe_tabT, 1)
            pe.wait_ge(tabT_in, 1)
            pe.matmul(bank[3][0:NF, P:P + NS], table_cT[:], dxT[:], start=True, stop=True).then_inc(pe_g, 1)
            pe.wait_ge(ld_w2, 16 * 12)
            pe.wait_ge(wide_beta, 1)
            for e in range(E):
                pe.matmul(bank[5][:, e:e + 1], w1_sb[:, e, :], bet[:], start=True, stop=True)
            pe.matmul(bank[5][:, E:2 * E], bet_wide[:], wr_sb[0:D, :], start=True, stop=True)
            pe.transpose(bank[5][:, 16:24], b1_sb[:], ident_f[0:E, 0:E])
            pe.transpose(bank[5][:, 24:24 + NP], b2_sb[:], ident_f[0:NP, 0:NP])
            for k in range(NK):
                pe.transpose(bank[5][:, P + k * D:P + (k + 1) * D], e_sb[:, k * P:(k + 1) * P], ident_f[0:D, 0:D])
            pe.wait_ge(gammas_in, 1)
            for e in range(E):
                last = pe.transpose(bank[6][:, e * D:(e + 1) * D], w1g[:, e, :], ident_f[0:D, 0:D])
            last.then_inc(pe_bias, 1)
            pe.wait_ge(parts_in, 1)
            for part in range(2):
                for e in range(E):
                    pe.transpose(bank[2 + part][:, :].bitcast(F16)[:, e * P:(e + 1) * P],
                                 w1_p[:, part, e].rearrange("h u d -> h (u d)"), ident_h[:])
                for k in range(NK):
                    at = (part * NK + k) * P
                    last = pe.transpose(bank[4][:, :].bitcast(F16)[:, at:at + P],
                                        dy_p[:, part, k].rearrange("n u d -> n (u d)"), ident_h[:])
            last.then_inc(pe_parts, 1)

            def group(g, first):
                if first:
                    pe.wait_ge(feats_in, 1)
                    pe.wait_ge(weights_in, 1)
                for n in range(GROUP):
                    last = pe.transpose(bank[0][:, :].bitcast(BF16)[:, n * P:(n + 1) * P],
                                        feat_parts[:, bass.ds(g * GROUP + n, 1), :].rearrange("p o k -> p (o k)"),
                                        ident_b[:])
                last.then_inc(pe_featT, 1)
                pe.wait_ge(featT_in, g + 1)
                if first:
                    pe.wait_ge(ld_table, 16 * PIECES * PIECES)
                else:
                    pe.wait_ge(h0_in, g)
                for n in range(GROUP):
                    last = pe.matmul(bank[1][:, n * D:(n + 1) * D], feat_k[:, bass.ds((g * GROUP + n) * P, P)],
                                     table_k[:, 0:D], start=True, stop=True)
                last.then_inc(pe_h0, 1)
                for n in range(GROUP // 2):
                    if not first:
                        pe.wait_ge([sum_a, sum_v][n % 2], (GROUP // 2) * (g - 1) + 2 * (n // 2) + 2)
                    for k in range(2):
                        last = pe.matmul(bank[2 + n][:, k * NS:(k + 1) * NS],
                                         feat_k[:, bass.ds((g * GROUP + 2 * n + k) * P, P)],
                                         table_k[:, D:D + NS], start=True, stop=True)
                    last.then_inc(pe_g2, 1)

            group(0, True)
            with pe.Fori(1, NG) as g:
                group(g, False)
            pe.wait_ge(upd_in, 1)
            pe.transpose(bank[1][:, 0:P], upd_sum[:], ident_f[:]).then_inc(pe_updT, 1)
            pe.wait_ge(ld_recip, 16)
            pe.transpose(bank[1][:, P:2 * P], recip_j[:], ident_f[:]).then_inc(pe_recT, 1)
            pe.wait_ge(scaled_in, 1)

            def scaled(g, side, first):
                if not first:
                    pe.wait_ge(scT_in, 2 * g)
                for n in range(GROUP):
                    last = pe.transpose(bank[side][:, :].bitcast(BF16)[:, n * P:(n + 1) * P],
                                        feat_parts[:, bass.ds((2 * g + side) * GROUP + n, 1), :]
                                        .rearrange("p o k -> p (o k)"), ident_b[:])
                last.then_inc(pe_scT, 1)

            scaled(0, 0, True)
            scaled(0, 1, True)
            with pe.Fori(1, NG // 2) as g:
                scaled(g, 0, False)
                scaled(g, 1, False)
            pe.wait_ge(scT_in, NG)

            def update(b):
                wait(pe, dv_y, NK * b)
                for k in range(NK):
                    last = pe.matmul(n_bank[k][:, :], table_k[:, D + k * P:D + (k + 1) * P],
                                     rows_or_scaled[:, bass.ds(b * S, S)], start=True, stop=True)
                last.then_inc(pe_pre, 1)

            def scores(b, sc):
                if sc == 0:
                    pe.wait_ge(dv_x, NK * (b + 1))
                if sc >= 2:
                    pe.wait_ge(dv_diag, C * b + sc - 1)
                    pe.wait_ge(ac_off, (C - 1) * b + sc - 1)
                for k in range(NK):
                    last = pe.matmul(n_bank[sc % 2][:, 0:WIDE[sc]], xs[:, k, sc * P:(sc + 1) * P],
                                     xs[:, k, sc * P:S], start=(k == 0), stop=(k == NK - 1))
                last.then_inc(pe_s, 1)

            def values(b):
                pe.wait_ge(dv_diag, C * (b + 1))
                pe.wait_ge(ac_off, (C - 1) * (b + 1))
                pe.wait_ge(po_ub, b + 1)
                wait(pe, ac_z, b)
                for tc in range(C):
                    for sc in range(tc + 1):
                        at = OFF[sc] + P * (tc - sc)
                        last = pe.matmul(az[:, tc * D:(tc + 1) * D], pm[:, at:at + P], ub[:, sc, :],
                                         start=(sc == 0), stop=(sc == tc))
                last.then_inc(pe_a, 1)

            def attn_T(b):
                pe.wait_ge(po_al, b + 1)
                pe.wait_ge(ac_ah, b + 1)
                wait(pe, ac_wT, b - 1)
                for c in range(C):
                    last = pe.transpose(ly_w[:, c * P:(c + 1) * P], a_p[:, c, :], ident_h[:])
                last.then_inc(pe_aT, 1)

            def y_core(b):
                pe.wait_ge(ac_aT, b + 1)
                for k in range(NK):
                    pe.matmul(n_bank[k][:, :], dyT[:, 0, k * P:(k + 1) * P], aT[:], start=True, stop=False)
                    pe.matmul(n_bank[k][:, :], dyT[:, 1, k * P:(k + 1) * P], aT[:], start=False, stop=True)\
                      .then_inc(pe_y, 1)

            def z_out(b):
                pe.wait_ge(dv_y, NK * (b + 1))
                for c in range(C):
                    for k in range(NK):
                        last = pe.matmul(az[:, (C + c) * D:(C + c + 1) * D], ys[:, k, c * P:(c + 1) * P], eT[:, k, :],
                                         start=(k == 0), stop=(k == NK - 1))
                last.then_inc(pe_z, 1)

            def centred_T(b):
                pe.wait_ge(po_xl, b + 1)
                wait(pe, ac_wb, NP * b)
                for c in range(C):
                    last = pe.transpose(tp_h[:, c * P:(c + 1) * P], x_p[:, c, :], ident_h[:])
                last.then_inc(pe_xT, 1)

            def logits(b, att):
                pe.wait_ge(ac_xT, b + 1)
                if att:
                    pe.wait_ge(ac_aT, b + 2)
                else:
                    pe.wait_ge(ac_wT, b)
                n = PIECES * E
                for c in range(C):
                    last = pe.matmul(ly[:, c * n:(c + 1) * n], xT[:, c * P:(c + 1) * P],
                                     wr_p[:].rearrange("p k e -> p (k e)"), start=True, stop=True)
                last.then_inc(pe_lg, 1)

            def hidden(b, e):
                pe.wait_ge(ac_xT, b + 1)
                wait(pe, ac_gelu, E * b + e - 1)
                pe.matmul(h_bank[e % 2][:, :], w1k[:, 0, e, :], xT[:], start=True, stop=False)
                pe.matmul(h_bank[e % 2][:, :], w1k[:, 1, e, :], xT[:], start=False, stop=True).then_inc(pe_hid, 1)

            def expert_out(b, q):
                pe.wait_ge(ac_gelu, E * b + 2 * q + 2)
                wait(pe, dv_tm, NP * b + q)
                pe.matmul(zb[0:D, :], w2_sb[:, 2 * q, :], hid[:, 2 * q, :], start=True, stop=True)
                pe.matmul(zb[D:P, :], w2_sb[:, 2 * q + 1, :], hid[:, 2 * q + 1, :], start=True, stop=True)\
                  .then_inc(pe_zz, 1)

            def weights_T(b):
                pe.wait_ge(dv_w, b + 1)
                wait(pe, dv_out, b)
                for c in range(C):
                    last = pe.transpose(ly_w[0:2 * E, c * P:(c + 1) * P], w_p[:, c, :], ident_h[:])
                last.then_inc(pe_wT2, 1)

            def weights_wide(b, q):
                if q == 0:
                    pe.wait_ge(ac_wT, b + 1)
                wait(pe, ac_wb, NP * b + q)
                pe.matmul(tp[:, :], sel[:, q, :], wT[:], start=True, stop=True).then_inc(pe_wb, 1)

            def fold(b, more):
                pe.wait_ge(po_acc, b + 1)
                if more:
                    pe.wait_ge(dv_lg, b + 2)
                else:
                    pe.wait_ge(ac_wT, B)
                for c in range(C):
                    last = pe.matmul(ly[:, 256 + c * D:256 + (c + 1) * D], acc[:, c * P:(c + 1) * P], fold_f[:],
                                     start=True, stop=True)
                last.then_inc(pe_fold, 1)

            def turn(i, att, res, mlp, done, ahead):
                r, k = i - 1, i - 2
                if att:
                    scores(i, 0)
                if mlp:
                    hidden(k, 0)
                if att:
                    scores(i, 1)
                if mlp:
                    hidden(k, 1)
                if att:
                    scores(i, 2)
                    scores(i, 3)
                if done:
                    fold(i - 3, True)
                if mlp:
                    hidden(k, 2)
                    weights_T(k)
                if att:
                    values(i)
                if mlp:
                    weights_wide(k, 0)
                    hidden(k, 3)
                    expert_out(k, 0)
                    weights_wide(k, 1)
                    hidden(k, 4)
                    hidden(k, 5)
                    expert_out(k, 1)
                if att:
                    attn_T(i)
                if mlp:
                    hidden(k, 6)
                    weights_wide(k, 2)
                if att:
                    y_core(i)
                if mlp:
                    hidden(k, 7)
                    expert_out(k, 2)
                    weights_wide(k, 3)
                if ahead:
                    update(i + 1)
                if att:
                    z_out(i)
                if res:
                    centred_T(r)
                if mlp:
                    expert_out(k, 3)
                if res:
                    logits(r, att)

            pe.wait_ge(sel_ready, 1)
            update(0)
            turn(0, True, False, False, False, True)
            turn(1, True, True, False, False, True)
            turn(2, True, True, True, False, True)
            with pe.Fori(3, B - 1) as i:
                turn(i, True, True, True, True, True)
            turn(B - 1, True, True, True, True, False)
            turn(B, False, True, True, True, False)
            turn(B + 1, False, False, True, True, False)
            fold(B - 1, False)


_INS = ["x", "mask_BS_i0_1", "L0_tok_skill_w", "L0_tok_skill_b", "L0_tok_att_w", "L0_tok_att_b", "L0_tok_mast_w",
        "L0_tok_mast_b", "L0_tok_proj_w", "L0_tok_proj_b", "L0_attn_E", "L0_attn_Dx", "L0_attn_Dy", "L0_ffn_gamma",
        "L0_ffn_beta", "L0_ffn_Wr", "L0_ffn_br", "L0_ffn_W1", "L0_ffn_b1", "L0_ffn_W2", "L0_ffn_b2"]


def constants():
    row, col = np.arange(P)[:, None], np.arange(P)[None, :]
    t = (np.arange(P)[:, None] + P * np.arange(C)[None, :]).astype(np.float64)
    decays = np.concatenate([DECAY ** (-1.0 - t), EPS * DECAY ** (-2.0 * t), np.tile(np.arange(E), (P, 1))], axis=1)
    return {
        "ident": np.eye(P, dtype=np.float32),
        "masks": np.concatenate([row <= col, row < col], axis=1).astype(np.float32),
        "decays": decays.astype(np.float32),
    }


def kernel(**inputs):
    import concourse.bacc as _bacc
    from concourse.bass_utils import run_bass_kernel_spmd as _run

    nc = _bacc.Bacc("TRN2", target_bir_lowering=False, num_devices=1)
    arrays, args = {}, []
    named = [(name, np.ascontiguousarray(inputs[name])) for name in _INS] + list(constants().items())
    for name, a in named:
        arrays[f"in_{name}"] = a
        args.append(nc.dram_tensor(f"in_{name}", a.shape, mybir.dt.from_np(a.dtype), kind="ExternalInput").ap())
    args.append(nc.dram_tensor("out_0", (B, S, D), F32, kind="ExternalOutput").ap())
    program(nc, *args)
    r = _run(nc, [arrays], core_ids=[0])
    return r.results[0]["out_0"]
```

```python
from contextlib import ExitStack

import numpy as np

import concourse.bass as bass
from concourse import mybir

F32 = mybir.dt.float32
F16 = mybir.dt.float16
BF16 = mybir.dt.bfloat16
I32 = mybir.dt.int32
U32 = mybir.dt.uint32
ALU = mybir.AluOpType
ACT = mybir.ActivationFunctionType
AX_X = mybir.AxisListType.X

P = 128
B, S = 32, 512
C = S // P
J = B * C
D = 64
NS = 256
NK = NS // P
E = 8
HID = 128
NP = E // 2
SKILLS = 75
D3 = 21
NF = 4
PIECES = 3
KF = NF * PIECES * PIECES
DECAY = 0.97
EPS = 1e-5
L1_EPS = 1e-12
RSQRT_SEED = float(0x5F3759DF)
OFF = [0, 512, 896, 1152]
WIDE = [S - P * sc for sc in range(C)]
CAUSAL = OFF[-1] + WIDE[-1]
GROUP = 8
NG = J // GROUP
EXP_MASK = 0x7F800000

N_ATT = 12
N_RES = 22
N_MLP = 16


class Steps:

    def __init__(self, eng, sem, base=0):
        self.eng, self.sem, self.base, self.n = eng, sem, base, 0

    def done(self, instruction):
        instruction.then_inc(self.sem, 1)
        self.n += 1

    def last(self):
        self.eng.wait_ge(self.sem, self.base + self.n)


def wait(eng, sem, value):
    if not isinstance(value, int) or value > 0:
        eng.wait_ge(sem, value)


def program(nc, x, r, skill_w, skill_b, att_w, att_b, mast_w, mast_b, proj_w, proj_b, Ea, Dx, Dy, gamma, beta,
            Wr, br, W1, b1, W2, b2, ident, masks, decays, out):
    with ExitStack() as ctx:
        def sb(name, shape, dt=F32):
            return ctx.enter_context(nc.sbuf_tensor(name, shape, dt))

        def sem(name):
            return ctx.enter_context(nc.semaphore(name))

        def scratch(name, shape, dt):
            return nc.dram_tensor(name, shape, dt, kind="Internal").ap()

        bank = [ctx.enter_context(nc.psum_tensor(f"bank{n}", [P, 512], F32)) for n in range(8)]

        skill_row_d = scratch("skill_row_d", (J, P), BF16)
        upd_d = scratch("upd_d", (J, 2, P), F32)
        factor_d = scratch("factor_d", (B, 2, S), F32)
        table_d = scratch("table_d", (NF, PIECES, D + NS), BF16)

        xi, ri = sb("xi", [J, P], I32), sb("ri", [J, P], I32)
        xf, rf = sb("xf", [J, P]), sb("rf", [J, P])
        ident_f, mask_sb = sb("ident_f", [P, P]), sb("mask_sb", [P, 2 * P])
        causal_f = mask_sb[:, P:2 * P]
        ident_h, ident_b = sb("ident_h", [P, P], F16), sb("ident_b", [P, P], BF16)
        upto_b = sb("upto_b", [P, P], BF16)
        dec = sb("dec", [P, 2 * C + E])
        fold_f = sb("fold_f", [P, D])
        skill_T, right_T = sb("skill_T", [P, J]), sb("right_T", [P, J])
        skill_row = sb("skill_row", [J, P], BF16)
        right_parts = sb("right_parts", [P, J, 4], BF16)
        ones_row = sb("ones_row", [1, NF])
        s4, proj_sb, projT = sb("s4", [D, NF]), sb("proj_sb", [D, D]), sb("projT", [D, D])
        projb = sb("projb", [1, D])
        table = sb("table", [NF, D + NS])
        table_c, table_cT = sb("table_c", [NF, D]), sb("table_cT", [D, NF])
        table_m = sb("table_m", [NF, 1])
        table_p = sb("table_p", [NF, PIECES, D + NS], BF16)
        table_r = sb("table_r", [NF, D + NS])
        table_k = sb("table_k", [P, D + NS], BF16)
        dx_sb, dxT = sb("dx_sb", [P, NK, D]), sb("dxT", [D, NS])
        dy_sb, dy_scale = sb("dy_sb", [P, NK, D]), sb("dy_scale", [P, 2 * NK])
        dy_p = sb("dy_p", [P, 2, NK, 2, D], F16)
        dyT = sb("dyT", [P, 2, NS], F16)
        e_sb, eT, e_mean = sb("e_sb", [D, NS]), sb("eT", [P, NK, D]), sb("e_mean", [P, NK])
        gam2, bet = sb("gam2", [P, 1]), sb("bet", [D, 1])
        bet_wide = sb("bet_wide", [D, P])
        w1_sb, w1g = sb("w1_sb", [D, E, HID]), sb("w1g", [D, E, HID])
        w1T = sb("w1T", [HID, E, D])
        w1_scale, w1_inv = sb("w1_scale", [HID, E]), sb("w1_inv", [HID, E])
        w1_p = sb("w1_p", [HID, 2, E, 2, D], F16)
        w1k = sb("w1k", [P, 2, E, HID], F16)
        b1_sb, b1T = sb("b1_sb", [E, HID]), sb("b1T", [HID, E])
        w2_sb = sb("w2_sb", [HID, E, D])
        b2_sb, b2_pair = sb("b2_sb", [NP, P]), sb("b2_pair", [P, NP])
        wr_sb, wr_g, wr_r = sb("wr_sb", [P, E]), sb("wr_g", [P, E]), sb("wr_r", [P, E])
        wr_p = sb("wr_p", [P, PIECES, E], BF16)
        br_sb = sb("br_sb", [P, E])
        sel = sb("sel", [2 * E, NP, P], F16)

        attempts = sb("attempts", [P, J])
        valid, feat_t = sb("valid", [P, J]), sb("feat_t", [P, J])
        feat = sb("feat", [P, NF, J])
        feat_r = sb("feat_r", [P, NF, J])
        stat_h0 = sb("stat_h0", [P, J, 6])
        mean_h0, var_h0 = sb("mean_h0", [P, J]), sb("var_h0", [P, J])
        rstd, u_scale = sb("rstd", [P, J]), sb("u_scale", [P, J])
        newton = sb("newton", [P, J])
        stat_g = sb("stat_g", [P, 2, GROUP, 6])
        upd_sum, upd_T = sb("upd_sum", [P, J]), sb("upd_T", [J, 2, P])

        h_all = sb("h_all", [P, J * D])
        skill_rows = sb("skill_rows", [P, J * P], BF16)
        feat_parts = sb("feat_parts", [P, J, P], BF16)
        feat_k = sb("feat_k", [P, J * P], BF16)
        same = sb("same", [P, 2, C * (S + P)], BF16)

        def over(array, at, *shape):
            n = int(np.prod(shape))
            flat = array.bitcast(F32)[:, at:at + n]
            return flat.rearrange("p (a b) -> p a b", a=shape[0]) if len(shape) == 2 else flat

        row_u, row_w, row_nz, row_any, row_one, row_d, row_rstd, row_zero = (
            over(skill_rows[0:B, :], n * S, S) for n in range(8))
        parts_flat = feat_parts[:].rearrange("p j n -> p (j n)")
        same_flat = same[:].rearrange("p side n -> p (side n)")
        relu_b = over(parts_flat, 0, NK, S)
        factor = over(same_flat, 0, 2, S)
        xs = over(parts_flat, 2 * S, NK, S)
        pm = over(parts_flat, 9 * S, CAUSAL)
        ub, ub_t = over(same_flat, 2 * S, C, D), over(same_flat, 2 * S + C * D, C, D)
        st_a, t_a = sb("st_a", [P, C, 6]), sb("t_a", [P, 4, C])
        an = sb("an", [P, C, D])
        a_p, aT = sb("a_p", [P, C, 2 * D], F16), sb("aT", [P, S], F16)
        ys = over(parts_flat, 4 * S, NK, S)
        power = sb("power", [P, C])
        z_sb = over(same_flat, 2 * S + 2 * C * D, C, D)
        st_z, t_z = sb("st_z", [P, C, 6]), sb("t_z", [P, 4, C])
        st_h, t_h = sb("st_h", [P, C, 6]), sb("t_h", [P, 4, C])
        h_mean, h_scale = sb("h_mean", [P, C]), sb("h_scale", [P, C])
        xc, xc_t = sb("xc", [P, C, D]), sb("xc_t", [P, C, D])
        x_p, xT = sb("x_p", [P, C, 2 * D], F16), sb("xT", [P, S], F16)
        lg, top, top_i = sb("lg", [P, C, E]), sb("top", [P, C, E]), sb("top_i", [P, C, E], U32)
        gap, tanh_g, wgt = sb("gap", [P, C]), sb("tanh_g", [P, C]), sb("wgt", [P, 2, C])
        pick = sb("pick", [P, 2, C, E])
        w_p, wT = sb("w_p", [P, C, 2 * E], F16), sb("wT", [2 * E, S], F16)
        wb = over(skill_rows[:], E * S, NP, S)
        hid = over(skill_rows[:], 0, E, S)
        tm = over(skill_rows[:], (E + NP) * S, NP, S)
        half, acc = over(parts_flat, 6 * S, 2, S), over(parts_flat, 8 * S, S)
        o_sb = sb("o_sb", [P, C, D])

        ld_x, ld_c, ld_w, ld_w2 = sem("ld_x"), sem("ld_c"), sem("ld_w"), sem("ld_w2")
        ld_w3 = sem("ld_w3")
        ld_rows = [sem(f"ld_rows{n}") for n in range(4)]
        ld_table, ld_row_u, ld_factor = sem("ld_table"), sem("ld_row_u"), sem("ld_factor")
        st_rows, st_table, st_upd, st_factor, st_out = (sem("st_rows"), sem("st_table"), sem("st_upd"),
                                                        sem("st_factor"), sem("st_out"))
        zeroed, table_zeroed = sem("zeroed"), sem("table_zeroed")
        ints_f, rows_ready, sel_ready = sem("ints_f"), sem("rows_ready"), sem("sel_ready")
        ids_ready, gammas_in, wide_beta = sem("ids_ready"), sem("gammas_in"), sem("wide_beta")
        pe_tok_T, pe_wT, pe_bias = sem("pe_tok_T"), sem("pe_wT"), sem("pe_bias")
        projT_in, pe_tab, tab_c_in, pe_tabT, tabT_in, pe_g, table_ready = (
            sem("projT_in"), sem("pe_tab"), sem("tab_c_in"), sem("pe_tabT"), sem("tabT_in"), sem("pe_g"),
            sem("table_ready"))
        parts_in, pe_parts, weights_in = sem("parts_in"), sem("pe_parts"), sem("weights_in")
        dve_set = sem("dve_set")
        tok_in = sem("tok_in")
        same_raw, same_in, pe_counts = sem("same_raw"), sem("same_in"), sem("pe_counts")
        feats_in, pe_featT, featT_in = sem("feats_in"), sem("pe_featT"), sem("featT_in")
        pe_h0, pe_g2 = sem("pe_h0"), sem("pe_g2")
        h0_in, sum_a, sum_v, h0_stats = sem("h0_in"), sem("sum_a"), sem("sum_v"), sem("h0_stats")
        h0_bn, parts_zeroed = sem("h0_bn"), sem("parts_zeroed")
        upd_in, pe_updT, updT_in = sem("upd_in"), sem("pe_updT"), sem("updT_in")
        factors_in, scales_in = sem("factors_in"), sem("scales_in")
        pe_pre, pe_s, pe_a, pe_aT, pe_y, pe_z = (sem("pe_pre"), sem("pe_s"), sem("pe_a"), sem("pe_aT"), sem("pe_y"),
                                                 sem("pe_z"))
        pe_xT, pe_lg, pe_hid, pe_zz, pe_wT2, pe_wb, pe_fold = (
            sem("pe_xT"), sem("pe_lg"), sem("pe_hid"), sem("pe_zz"), sem("pe_wT2"), sem("pe_wb"), sem("pe_fold"))
        ac_off, ac_ah, ac_aT, ac_xh, ac_xT = sem("ac_off"), sem("ac_ah"), sem("ac_aT"), sem("ac_xh"), sem("ac_xT")
        ac_gelu, ac_tanh, ac_wT, ac_wb = sem("ac_gelu"), sem("ac_tanh"), sem("ac_wT"), sem("ac_wb")
        ac_z = sem("ac_z")
        dv_x, dv_diag, dv_an, dv_y, dv_h = sem("dv_x"), sem("dv_diag"), sem("dv_an"), sem("dv_y"), sem("dv_h")
        dv_relu = sem("dv_relu")
        dv_gap, dv_w, dv_tm, dv_out, dv_lg = sem("dv_gap"), sem("dv_w"), sem("dv_tm"), sem("dv_out"), sem("dv_lg")
        dv_var_z = sem("dv_var_z")
        att_steps, res_steps, mlp_steps = sem("att_steps"), sem("res_steps"), sem("mlp_steps")
        pool_steps = sem("pool_steps")
        dv_passed = sem("dv_passed")
        po_in, po_ub, po_al, po_xt, po_xc = sem("po_in"), sem("po_ub"), sem("po_al"), sem("po_xt"), sem("po_xc")
        po_xl, po_half, po_acc = sem("po_xl"), sem("po_half"), sem("po_acc")
        po_z_scale, po_h_scale = sem("po_z_scale"), sem("po_h_scale")

        mA, mB, tp, az, hA, hB, zb, ly = bank
        n_bank, h_bank = [mA, mB], [hA, hB]
        tp_h = tp[:, :].bitcast(F16)
        ly_lg = ly[:, 0:C * PIECES * E]
        ly_w = ly[:, 256:512].bitcast(F16)
        ly_y = ly[:, 256:512]
        az_a = az[:, 0:C * D].rearrange("p (c d) -> p c d", c=C)
        az_z = az[:, C * D:2 * C * D].rearrange("p (c d) -> p c d", c=C)
        feat_bank, h0_bank = [bank[0], bank[6]], [bank[1], bank[7]]
        counts = bank[0][:, :].rearrange("p (j k) -> p j k", k=4)

        def wide(ap, n):
            return ap.unsqueeze(2).to_broadcast([ap.shape[0], ap.shape[1], n])

        def h_of(b):
            return h_all[:, bass.ds(b * C * D, C * D)].rearrange("p (c d) -> p c d", c=C)

        block = ctx.enter_context(nc.Block())

        @block.sync
        def _(sp):
            sp.dma_start(xi[:], x.rearrange("b (c p) -> (b c) p", p=P)).then_inc(ld_x, 16)
            sp.dma_start(ri[:], r.rearrange("b (c p) -> (b c) p", p=P)).then_inc(ld_x, 16)
            sp.dma_start(ident_f[:], ident).then_inc(ld_c, 16)
            sp.dma_start(mask_sb[:], masks).then_inc(ld_c, 16)
            sp.dma_start(dec[:], decays).then_inc(ld_c, 16)
            sp.dma_start(proj_sb[:], proj_w).then_inc(ld_w, 16)
            sp.dma_start(projb[:], proj_b.unsqueeze(0)).then_inc(ld_w, 16)
            sp.wait_ge(zeroed, 1)
            sp.dma_start(s4[0:D3, 0:1], skill_w.unsqueeze(1)).then_inc(ld_w, 16)
            sp.dma_start(s4[D3:2 * D3, 1:2], att_w.unsqueeze(1)).then_inc(ld_w, 16)
            sp.dma_start(s4[2 * D3:D, 2:3], mast_w.unsqueeze(1)).then_inc(ld_w, 16)
            sp.dma_start(s4[0:D3, 3:4], skill_b.unsqueeze(1)).then_inc(ld_w, 16)
            sp.dma_start(s4[D3:2 * D3, 3:4], att_b.unsqueeze(1)).then_inc(ld_w, 16)
            sp.dma_start(s4[2 * D3:D, 3:4], mast_b.unsqueeze(1)).then_inc(ld_w, 16)
            sp.dma_start(dx_sb[:], Dx.rearrange("(k p) d -> p k d", p=P)).then_inc(ld_w, 16)
            sp.wait_ge(rows_ready, 1)
            sp.dma_start(skill_row_d, skill_row[:]).then_inc(st_rows, 16)
            sp.wait_ge(st_rows, 16)
            rows = skill_row_d.rearrange("j p -> (j p)").unsqueeze(0)
            n = J * P // 4
            for q in range(4):
                sp.dma_start(skill_rows[:, q * n:(q + 1) * n],
                             rows[:, q * n:(q + 1) * n].to_broadcast([P, n])).then_inc(ld_rows[q], 16)
            sp.wait_ge(table_ready, 1)
            sp.dma_start(table_d, table_p[:]).then_inc(st_table, 16)
            sp.wait_ge(st_table, 16)
            sp.wait_ge(table_zeroed, 1)
            for g in range(PIECES):
                for piece in range(PIECES):
                    row = NF * (PIECES * g + piece)
                    sp.dma_start(table_k[row:row + NF, :], table_d[:, g, :]).then_inc(ld_table, 16)
            sp.wait_ge(updT_in, 1)
            sp.dma_start(upd_d, upd_T[:]).then_inc(st_upd, 16)
            sp.wait_ge(st_upd, 16)
            for n, row in enumerate((row_u, row_rstd)):
                sp.dma_start(row.rearrange("b (c p) -> b c p", p=P),
                             upd_d[:, n, :].rearrange("(b c) p -> b c p", c=C)).then_inc(ld_row_u, 16)
            sp.wait_ge(factors_in, 1)
            sp.dma_start(factor_d[:, 0, :], row_nz).then_inc(st_factor, 16)
            sp.dma_start(factor_d[:, 1, :], row_w).then_inc(st_factor, 16)
            sp.wait_ge(st_factor, 32)

            def load_factor(b):
                wait(sp, dv_x, 2 * b)
                row = factor_d[bass.ds(b, 1)].rearrange("o two t -> o (two t)")
                sp.dma_start(factor.rearrange("p two t -> p (two t)"), row.to_broadcast([P, 2 * S]))\
                  .then_inc(ld_factor, 16)

            def store(b):
                sp.wait_ge(dv_out, b + 1)
                sp.dma_start(out[bass.ds(b, 1)].rearrange("o (c p) d -> p (o c) d", p=P), o_sb[:]).then_inc(st_out, 16)

            for b in range(4):
                load_factor(b)
            with sp.Fori(3, B - 1) as i:
                load_factor(i + 1)
                store(i - 3)
            for b in range(B - 4, B):
                store(b)
            sp.wait_ge(st_out, 16 * B)

        @block.gpsimd
        def _(pool):
            pool.memset(s4[:], 0.0).then_inc(zeroed, 1)
            pool.dma_start(gam2[0:D, :], gamma.unsqueeze(1)).then_inc(ld_w3, 16)
            pool.dma_start(gam2[D:P, :], gamma.unsqueeze(1)).then_inc(ld_w3, 16)
            pool.dma_start(bet[:], beta.unsqueeze(1)).then_inc(ld_w3, 16)
            pool.dma_start(wr_sb[0:D, :], Wr).then_inc(ld_w3, 16)
            pool.dma_start(wr_sb[D:P, :], Wr).then_inc(ld_w3, 16)
            pool.dma_start(br_sb[:], br.unsqueeze(0).to_broadcast([P, E])).then_inc(ld_w3, 16)
            pool.memset(feat_parts[:].rearrange("p j n -> p (j n)").bitcast(U32), 0).then_inc(parts_zeroed, 1)
            pool.memset(sel[:], 1.0).then_inc(pool_steps, 1)
            pool.wait_ge(pool_steps, 1)
            low = sel[:, :, :].rearrange("k q (two m) -> k q two m", two=2)
            pool.affine_select(out=low, in_=low, compare_op=ALU.is_ge, fill=0.0, base=0,
                               pattern=[[-2, NP], [-1, 2], [0, D]], channel_multiplier=1).then_inc(pool_steps, 1)
            pool.wait_ge(pool_steps, 2)
            for n, d in enumerate(list(range(1, E)) + list(range(E + 1, 2 * E))):
                pool.affine_select(out=low, in_=low, compare_op=ALU.not_equal, fill=0.0, base=-d,
                                   pattern=[[-2, NP], [-1, 2], [0, D]], channel_multiplier=1).then_inc(pool_steps, 1)
                pool.wait_ge(pool_steps, 3 + n)
            pool.memset(power[:], -0.5).then_inc(pool_steps, 1)
            pool.wait_ge(pool_steps, 2 * E + 1)
            pool.nop().then_inc(sel_ready, 1)

            def centred_input(b):
                if isinstance(b, int) and b == 0:
                    pool.wait_ge(scales_in, 1)
                    pool.wait_ge(h0_in, NG)
                wait(pool, po_ub, b)
                pool.tensor_tensor(ub_t[:], h_of(b), wide(mean_h0[:, bass.ds(b * C, C)], D), ALU.subtract)\
                    .then_inc(po_in, 1)

            def weighted_input(b):
                wait(pool, pe_a, b)
                pool.wait_ge(po_in, b + 1)
                pool.tensor_tensor(ub[:], ub_t[:], wide(u_scale[:, bass.ds(b * C, C)], D), ALU.mult).then_inc(po_ub, 1)

            def attn_low(b):
                pool.wait_ge(ac_ah, b + 1)
                pool.tensor_tensor(a_p[:, :, D:2 * D], an[:], a_p[:, :, 0:D], ALU.subtract).then_inc(po_al, 1)

            def z_scale(b):
                pool.wait_ge(dv_var_z, b + 1)
                pool.tensor_tensor(t_z[:, 3, :], t_z[:, 2, :], power[:], ALU.pow).then_inc(po_z_scale, 1)

            def centred(b):
                pool.wait_ge(dv_h, b + 1)
                wait(pool, po_xc, b)
                pool.tensor_tensor(h_scale[:], t_h[:, 2, :], power[:], ALU.pow).then_inc(po_h_scale, 1)
                pool.tensor_tensor(xc_t[:], h_of(b), wide(h_mean[:], D), ALU.subtract).then_inc(po_xt, 1)
                wait(pool, po_xl, b)
                pool.wait_ge(po_h_scale, b + 1)
                pool.wait_ge(po_xt, b + 1)
                pool.tensor_tensor(xc[:], xc_t[:], wide(h_scale[:], D), ALU.mult).then_inc(po_xc, 1)

            def centred_low(b):
                pool.wait_ge(ac_xh, b + 1)
                pool.tensor_tensor(x_p[:, :, D:2 * D], xc[:], x_p[:, :, 0:D], ALU.subtract).then_inc(po_xl, 1)

            def add_pairs(b, n):
                pool.wait_ge(dv_tm, NP * b + 2 * n + 2)
                wait(pool, po_acc, b)
                pool.tensor_tensor(half[:, n, :], tm[:, 2 * n, :], tm[:, 2 * n + 1, :], ALU.add).then_inc(po_half, 1)

            def add_halves(b):
                pool.wait_ge(po_half, 2 * b + 2)
                wait(pool, pe_fold, b)
                pool.tensor_tensor(acc[:], half[:, 0, :], half[:, 1, :], ALU.add).then_inc(po_acc, 1)

            def turn(i, att, res, mlp, done, ahead):
                if done:
                    add_pairs(i - 3, 1)
                if res:
                    z_scale(i - 1)
                if done:
                    add_halves(i - 3)
                if res:
                    centred(i - 1)
                if ahead:
                    centred_input(i + 1)
                if att:
                    attn_low(i)
                if res:
                    centred_low(i - 1)
                if ahead:
                    weighted_input(i + 1)
                if mlp:
                    add_pairs(i - 2, 0)

            centred_input(0)
            weighted_input(0)
            turn(0, True, False, False, False, True)
            turn(1, True, True, False, False, True)
            turn(2, True, True, True, False, True)
            with pool.Fori(0, B // 2 - 2) as two:
                turn(2 * two + 3, True, True, True, True, True)
                turn(2 * two + 4, True, True, True, True, True)
            turn(B - 1, True, True, True, True, False)
            turn(B, False, True, True, True, False)
            turn(B + 1, False, False, True, True, False)
            add_pairs(B - 1, 1)
            add_halves(B - 1)

        @block.scalar
        def _(act):
            act.dma_start(w1_sb[:], W1.rearrange("e d h -> d e h")).then_inc(ld_w2, 16)
            act.dma_start(b1_sb[:], b1).then_inc(ld_w2, 16)
            act.dma_start(dy_sb[:], Dy.rearrange("(k p) d -> p k d", p=P)).then_inc(ld_w2, 16)
            act.dma_start(e_sb[:], Ea).then_inc(ld_w2, 16)
            act.dma_start(w2_sb[:], W2.rearrange("e h d -> h e d")).then_inc(ld_w2, 16)
            act.dma_start(b2_sb[:], b2.rearrange("(q two) d -> q (two d)", two=2)).then_inc(ld_w2, 16)
            act.wait_ge(ld_c, 48)
            act.activation(tanh_g[:], dec[:, 0:C], ACT.Gelu)

            def group(g, side):
                act.wait_ge(pe_h0, g + 1)
                act.activation(h_all[:, bass.ds(g * GROUP * D, GROUP * D)], h0_bank[side][:, :], ACT.Copy)\
                   .then_inc(h0_in, 1)
                for n in range(GROUP // 2 - 1):
                    act.wait_ge(pe_g2, (GROUP // 2) * g + n + 1)
                    for k in range(2):
                        pre = bank[2 + n][:, k * NS:(k + 1) * NS]
                        act.activation(pre, pre, ACT.Relu,
                                       accum_out=upd_sum[:, bass.ds(g * GROUP + 2 * n + k, 1)]).then_inc(sum_a, 1)

            with act.Fori(0, NG // 2) as pair:
                group(2 * pair, 0)
                group(2 * pair + 1, 1)

            def off_diagonal(b, sc):
                act.wait_ge(dv_diag, C * b + sc + 1)
                wait(act, pe_a, b)
                act.activation(pm[:, OFF[sc] + P:OFF[sc] + WIDE[sc]], n_bank[sc % 2][:, P:WIDE[sc]], ACT.Copy)\
                   .then_inc(ac_off, 1)

            def attn_high(b):
                act.wait_ge(dv_an, b + 1)
                wait(act, pe_aT, b)
                act.activation(a_p[:, :, 0:D], an[:], ACT.Copy).then_inc(ac_ah, 1)

            def attn_T(b):
                act.wait_ge(pe_aT, b + 1)
                wait(act, pe_y, NK * b)
                act.activation(aT[:], ly_w[:, :], ACT.Copy).then_inc(ac_aT, 1)

            def centred_high(b):
                act.wait_ge(po_xc, b + 1)
                wait(act, pe_xT, b)
                act.activation(x_p[:, :, 0:D], xc[:], ACT.Copy).then_inc(ac_xh, 1)

            def centred_T(b):
                act.wait_ge(pe_xT, b + 1)
                wait(act, pe_hid, E * b)
                wait(act, pe_lg, b)
                act.activation(xT[:], tp_h[:, 0:S], ACT.Copy).then_inc(ac_xT, 1)

            def gelu(b, e):
                act.wait_ge(pe_hid, E * b + e + 1)
                wait(act, pe_zz, NP * b)
                act.activation(hid[:, e, :], h_bank[e % 2][:, :], ACT.Gelu, bias=b1T[:, e:e + 1],
                               scale=w1_scale[:, e:e + 1]).then_inc(ac_gelu, 1)

            def tanh(b):
                act.wait_ge(dv_gap, b + 1)
                act.activation(tanh_g[:], gap[:], ACT.Tanh, scale=0.5).then_inc(ac_tanh, 1)

            def weights_T(b):
                act.wait_ge(pe_wT2, b + 1)
                wait(act, pe_wb, NP * b)
                act.activation(wT[:], ly_w[0:2 * E, :], ACT.Copy).then_inc(ac_wT, 1)

            def weights_wide(b, q):
                act.wait_ge(pe_wb, NP * b + q + 1)
                wait(act, dv_tm, NP * b - NP + q + 1)
                act.activation(wb[:, q, :], tp[:, :], ACT.Copy).then_inc(ac_wb, 1)

            def z_copy(b):
                act.wait_ge(pe_z, b + 1)
                wait(act, dv_h, b)
                act.activation(z_sb[:], az_z, ACT.Copy).then_inc(ac_z, 1)

            def turn(i, att, res, mlp, done, ahead):
                r, k = i - 1, i - 2
                if att:
                    off_diagonal(i, 0)
                if mlp:
                    tanh(k)
                if att:
                    off_diagonal(i, 1)
                if mlp:
                    gelu(k, 0)
                if mlp:
                    gelu(k, 1)
                if att:
                    off_diagonal(i, 2)
                if mlp:
                    gelu(k, 2)
                    weights_T(k)
                    gelu(k, 3)
                    weights_wide(k, 0)
                if att:
                    attn_high(i)
                if res:
                    centred_high(r)
                if mlp:
                    weights_wide(k, 1)
                    gelu(k, 4)
                if att:
                    attn_T(i)
                if mlp:
                    gelu(k, 5)
                    gelu(k, 6)
                    weights_wide(k, 2)
                    gelu(k, 7)
                    weights_wide(k, 3)
                if res:
                    centred_T(r)
                if att:
                    z_copy(i)

            act.wait_ge(weights_in, 1)
            turn(0, True, False, False, False, True)
            turn(1, True, True, False, False, True)
            turn(2, True, True, True, False, True)
            with act.Fori(0, B // 2 - 2) as two:
                turn(2 * two + 3, True, True, True, True, True)
                turn(2 * two + 4, True, True, True, True, True)
            turn(B - 1, True, True, True, True, False)
            turn(B, False, True, True, True, False)
            turn(B + 1, False, False, True, True, False)

        @block.vector
        def _(dve):
            s = Steps(dve, dve_set)

            def op(instruction):
                s.done(instruction)
                s.last()

            def rsqrt(y, v, t, chain):
                chain.done(dve.tensor_scalar(y.bitcast(I32), v.bitcast(I32), -0.5, RSQRT_SEED, ALU.mult, ALU.add))
                for _ in range(3):
                    chain.last()
                    chain.done(dve.tensor_tensor(t, y, y, ALU.mult))
                    chain.last()
                    chain.done(dve.scalar_tensor_tensor(t, t, -0.5, v, ALU.mult, ALU.mult))
                    chain.last()
                    chain.done(dve.scalar_tensor_tensor(y, t, 1.5, y, ALU.add, ALU.mult))

            def variance(st, var, t, chain):
                chain.done(dve.tensor_tensor(t, st[:, :, 1], st[:, :, 4], ALU.subtract))
                chain.done(dve.tensor_tensor(var, st[:, :, 2], st[:, :, 5], ALU.add))
                chain.last()
                chain.done(dve.scalar_tensor_tensor(t, t, 0.25, t, ALU.mult, ALU.mult))
                chain.last()
                chain.done(dve.scalar_tensor_tensor(var, var, 1.0 / D, t, ALU.mult, ALU.add))

            def mean(st, m, t, chain):
                chain.done(dve.tensor_tensor(t, st[:, :, 1], st[:, :, 4], ALU.add))
                chain.last()
                chain.done(dve.tensor_scalar(m, t, 0.5, None, ALU.mult))

            dve.wait_ge(ld_x, 32)
            dve.tensor_copy(xf[:], xi[:]).then_inc(ints_f, 1)
            dve.tensor_copy(rf[:], ri[:]).then_inc(ints_f, 1)
            dve.wait_ge(ints_f, 2)
            dve.tensor_scalar(skill_row[:], xf[:], float(SKILLS), -1.0, ALU.min, ALU.max).then_inc(rows_ready, 1)
            dve.wait_ge(ld_c, 48)
            dve.tensor_copy(ident_h[:], ident_f[:]).then_inc(ids_ready, 1)
            dve.tensor_copy(ident_b[:], ident_f[:]).then_inc(ids_ready, 1)
            op(dve.tensor_copy(upto_b[:], mask_sb[:, 0:P]))
            op(dve.tensor_copy(fold_f[0:D, :], ident_f[0:D, 0:D]))
            op(dve.tensor_copy(fold_f[D:P, :], ident_f[D:P, D:P]))
            op(dve.memset(ones_row[:], 0.0))
            dve.memset(ones_row[:, NF - 1:NF], 1.0).then_inc(ids_ready, 1)
            dve.memset(table_k[:], 0.0).then_inc(table_zeroed, 1)

            dve.wait_ge(pe_tok_T, 1)
            op(dve.tensor_copy(skill_T[:], bank[1][:, 0:P]))
            op(dve.tensor_copy(right_T[:], bank[1][:, P:2 * P]))
            op(dve.memset(right_parts[:], 1.0))
            op(dve.tensor_copy(right_parts[:, :, 1], right_T[:]))
            op(dve.tensor_tensor(feat_t[:], right_T[:], right_parts[:, :, 1], ALU.subtract))
            op(dve.tensor_copy(right_parts[:, :, 2], feat_t[:]))
            dve.tensor_tensor(right_parts[:, :, 3], feat_t[:], right_parts[:, :, 2], ALU.subtract).then_inc(tok_in, 1)

            dve.wait_ge(pe_wT, 1)
            dve.tensor_copy(projT[:], bank[2][0:D, 0:D]).then_inc(projT_in, 1)
            op(dve.tensor_copy(dxT[:], bank[2][0:D, D:D + NS]))
            dve.wait_ge(pe_tab, 1)
            op(dve.tensor_copy(table[:, 0:D], bank[3][0:NF, 0:D]))
            op(dve.tensor_reduce(table_m[:], table[:, 0:D], AX_X, ALU.add))
            op(dve.tensor_scalar(table_m[:], table_m[:], 1.0 / D, None, ALU.mult))
            dve.tensor_scalar(table_c[:], table[:, 0:D], table_m[:, 0:1], None, ALU.subtract).then_inc(tab_c_in, 1)
            dve.wait_ge(pe_tabT, 1)
            dve.tensor_copy(table_cT[:], bank[3][0:D, D:D + NF]).then_inc(tabT_in, 1)
            dve.wait_ge(pe_g, 1)
            op(dve.tensor_copy(table[:, D:D + NS], bank[3][0:NF, P:P + NS]))
            op(dve.tensor_copy(table_p[:, 0, :], table[:]))
            op(dve.tensor_tensor(table_r[:], table[:], table_p[:, 0, :], ALU.subtract))
            op(dve.tensor_copy(table_p[:, 1, :], table_r[:]))
            op(dve.tensor_tensor(table_r[:], table_r[:], table_p[:, 1, :], ALU.subtract))
            dve.tensor_copy(table_p[:, 2, :], table_r[:]).then_inc(table_ready, 1)

            dve.wait_ge(ld_w2, 16 * 6)
            dve.wait_ge(ld_w3, 16 * 6)
            dve.tensor_scalar(w1g[:], w1_sb[:], gam2[0:D, 0:1], None, ALU.mult).then_inc(gammas_in, 1)
            op(dve.memset(bet_wide[:], 0.0))
            dve.tensor_scalar(bet_wide[:], bet_wide[:], bet[:, 0:1], None, ALU.add).then_inc(wide_beta, 1)
            op(dve.tensor_scalar(wr_g[:], wr_sb[:], gam2[:, 0:1], None, ALU.mult))
            op(dve.tensor_copy(wr_p[:, 0, :], wr_g[:]))
            op(dve.tensor_tensor(wr_r[:], wr_g[:], wr_p[:, 0, :], ALU.subtract))
            op(dve.tensor_copy(wr_p[:, 1, :], wr_r[:]))
            op(dve.tensor_tensor(wr_p[:, 2, :], wr_r[:], wr_p[:, 1, :], ALU.subtract))
            def power_of_two(scale, inverse):
                op(dve.tensor_scalar(scale, scale, 1e-30, None, ALU.max))
                op(dve.tensor_scalar(scale.bitcast(I32), scale.bitcast(I32), EXP_MASK, None, ALU.bitwise_and))
                op(dve.reciprocal(inverse, scale))

            op(dve.tensor_reduce(dy_scale[:, 0:NK], dy_sb[:], AX_X, ALU.max, apply_absolute_value=True))
            power_of_two(dy_scale[:, 0:NK], dy_scale[:, NK:2 * NK])
            op(dve.tensor_tensor(dy_sb[:], dy_sb[:], wide(dy_scale[:, NK:2 * NK], D), ALU.mult))
            op(dve.tensor_copy(dy_p[:, 0, :, 0, :], dy_sb[:]))
            op(dve.tensor_copy(dy_p[:, 0, :, 1, :], dy_sb[:]))
            op(dve.tensor_tensor(dy_p[:, 1, :, 0, :], dy_sb[:], dy_p[:, 0, :, 0, :], ALU.subtract))
            op(dve.tensor_copy(dy_p[:, 1, :, 1, :], dy_p[:, 1, :, 0, :]))
            dve.wait_ge(pe_bias, 1)
            op(dve.tensor_copy(b1T[:], bank[5][:, 16:24]))
            op(dve.tensor_copy(b2_pair[:], bank[5][:, 24:24 + NP]))
            op(dve.tensor_tensor(b1T[:], b1T[:], bank[5][:, 0:E], ALU.add))
            op(dve.tensor_tensor(br_sb[:], br_sb[:], bank[5][:, E:2 * E], ALU.add))

            w1T_ps = bank[6][:, :].rearrange("h (e d) -> h e d", e=E)
            op(dve.tensor_reduce(w1_scale[:], w1T_ps, AX_X, ALU.max, apply_absolute_value=True))
            power_of_two(w1_scale[:], w1_inv[:])
            op(dve.tensor_tensor(w1T[:], w1T_ps, wide(w1_inv[:], D), ALU.mult))
            op(dve.tensor_copy(w1_p[:, 0, :, 0, :], w1T[:]))
            op(dve.tensor_copy(w1_p[:, 0, :, 1, :], w1T[:]))
            op(dve.tensor_tensor(w1_p[:, 1, :, 0, :], w1T[:], w1_p[:, 0, :, 0, :], ALU.subtract))
            dve.tensor_copy(w1_p[:, 1, :, 1, :], w1_p[:, 1, :, 0, :]).then_inc(parts_in, 1)
            op(dve.tensor_copy(eT[:].rearrange("p k d -> p (k d)"), bank[5][:, P:2 * P]))
            op(dve.tensor_reduce(e_mean[:], eT[:], AX_X, ALU.add))
            op(dve.tensor_scalar(e_mean[:], e_mean[:], 1.0 / D, None, ALU.mult))
            op(dve.tensor_tensor(eT[:], eT[:], wide(e_mean[:], D), ALU.subtract))
            op(dve.tensor_tensor(eT[:], eT[:], wide(dy_scale[:, 0:NK], D), ALU.mult))
            dve.wait_ge(pe_parts, 1)
            op(dve.tensor_copy(w1k[:, 0].rearrange("p e h -> p (e h)"), bank[2][:, :].bitcast(F16)))
            op(dve.tensor_copy(w1k[:, 1].rearrange("p e h -> p (e h)"), bank[3][:, :].bitcast(F16)))
            dve.tensor_copy(dyT[:].rearrange("p k n -> p (k n)"), bank[4][:, 0:NS].bitcast(F16)).then_inc(weights_in, 1)

            def equal(b, side):
                wait(dve, pe_counts, b - 1)
                for sc in range(C):
                    dve.tensor_scalar(same[:, side, sc * (S + P):(sc + 1) * S],
                                      skill_rows[:, bass.ds(b * S + sc * P, WIDE[sc])],
                                      skill_T[:, bass.ds(b * C + sc, 1)], None, ALU.is_equal).then_inc(same_raw, 1)
                dve.wait_ge(same_raw, C * (b + 1))
                own = same[:, side, :].rearrange("p (c w) -> p c w", c=C)[:, :, 0:P]
                dve.tensor_tensor(own, own, upto_b[:].unsqueeze(1).to_broadcast([P, C, P]), ALU.mult)\
                   .then_inc(same_in, 1)

            for q in range(4):
                dve.wait_ge(ld_rows[q], 16)
                n = B // 8
                if q == 0:
                    equal(0, 0)
                    equal(1, 1)
                with dve.Fori(max(1, n * q), n * (q + 1)) as pair:
                    equal(2 * pair, 0)
                    equal(2 * pair + 1, 1)

            op(dve.tensor_scalar(valid[:], skill_T[:], 0.0, None, ALU.is_ge))
            op(dve.scalar_tensor_tensor(valid[:], skill_T[:], float(SKILLS), valid[:], ALU.is_lt, ALU.mult))
            op(dve.tensor_tensor(feat[:, 0, :], skill_T[:], valid[:], ALU.mult))
            op(dve.tensor_copy(feat[:, 3, :], valid[:]))
            dve.wait_ge(pe_counts, B)
            op(dve.tensor_copy(attempts[:], counts[:, :, 0]))
            op(dve.tensor_scalar(feat_t[:], attempts[:], 1.0, None, ALU.max))
            op(dve.reciprocal(feat_t[:], feat_t[:]))
            op(dve.tensor_reduce(newton[:], counts[:, :, 1:4], AX_X, ALU.add))
            op(dve.tensor_tensor(feat_t[:], feat_t[:], newton[:], ALU.mult))
            op(dve.tensor_tensor(feat[:, 1, :], attempts[:], valid[:], ALU.mult))
            op(dve.tensor_tensor(feat[:, 2, :], feat_t[:], valid[:], ALU.mult))

            def cut(source):
                for piece in range(PIECES):
                    at = feat_parts[:, :, NF * piece:NF * (piece + 1)].rearrange("p j f -> p f j")
                    op(dve.tensor_copy(at, source))
                    if piece < PIECES - 1:
                        op(dve.tensor_tensor(feat_r[:], source, at, ALU.subtract))
                        source = feat_r[:]
                n = NF * PIECES
                op(dve.tensor_copy(feat_parts[:, :, n:2 * n], feat_parts[:, :, 0:n]))
                op(dve.tensor_copy(feat_parts[:, :, 2 * n:3 * n], feat_parts[:, :, 0:n]))

            dve.wait_ge(parts_zeroed, 1)
            cut(feat[:])
            dve.nop().then_inc(feats_in, 1)

            def features(g, side):
                dve.wait_ge(pe_featT, g + 1)
                dve.tensor_copy(feat_k[:, bass.ds(g * GROUP * P, GROUP * P)], feat_bank[side][:, :].bitcast(BF16))\
                   .then_inc(featT_in, 1)

            def group(g, side):
                dve.wait_ge(h0_in, g + 1)
                wait(dve, h0_stats, g - 1)
                for n in range(GROUP):
                    dve.bn_stats(stat_g[:, side, n, :], h0_bank[side][:, n * D:(n + 1) * D]).then_inc(h0_bn, 1)
                dve.wait_ge(pe_g2, (GROUP // 2) * (g + 1))
                for k in range(2):
                    at = g * GROUP + GROUP - 2 + k
                    pre = bank[5][:, k * NS:(k + 1) * NS]
                    dve.tensor_scalar(pre, pre, 0.0, None, ALU.max, ALU.add,
                                      accum_out=upd_sum[:, bass.ds(at, 1)]).then_inc(sum_v, 1)
                dve.wait_ge(h0_bn, GROUP * (g + 1))
                dve.tensor_copy(stat_h0[:, bass.ds(g * GROUP, GROUP), :], stat_g[:, side]).then_inc(h0_stats, 1)

            features(0, 0)
            features(1, 1)
            group(0, 0)
            features(2, 0)
            group(1, 1)
            with dve.Fori(1, NG // 2 - 1) as pair:
                features(2 * pair + 1, 1)
                group(2 * pair, 0)
                features(2 * pair + 2, 0)
                group(2 * pair + 1, 1)
            features(NG - 1, 1)
            group(NG - 2, 0)
            group(NG - 1, 1)
            dve.wait_ge(h0_stats, NG)
            dve.wait_ge(sum_v, 2 * NG)
            dve.wait_ge(sum_a, (GROUP - 2) * NG)
            mean(stat_h0, mean_h0[:], feat_t[:], s)
            s.last()
            variance(stat_h0, var_h0[:], feat_t[:], s)
            s.last()
            op(dve.tensor_scalar(feat_t[:], var_h0[:], EPS, None, ALU.add))
            rsqrt(rstd[:], feat_t[:], newton[:], s)
            s.last()
            dve.tensor_tensor(upd_sum[:], upd_sum[:], rstd[:], ALU.mult).then_inc(upd_in, 1)
            op(dve.tensor_scalar(feat_t[:], var_h0[:], 1.0 + EPS, EPS * EPS, ALU.mult, ALU.add))
            dve.wait_ge(pe_updT, 1)
            dve.tensor_copy(upd_T[:].rearrange("j two p -> j (two p)"), bank[1][:, 0:2 * P]).then_inc(updT_in, 1)
            rsqrt(u_scale[:], feat_t[:], newton[:], s)
            s.last()
            op(dve.tensor_tensor(u_scale[:].rearrange("p (b c) -> p b c", c=C),
                                 u_scale[:].rearrange("p (b c) -> p b c", c=C),
                                 dec[:, 0:C].unsqueeze(1).to_broadcast([P, B, C]), ALU.mult))
            dve.nop().then_inc(scales_in, 1)

            grow = DECAY / L1_EPS
            op(dve.memset(row_zero, 0.0))
            op(dve.memset(row_one, 0.0))
            op(dve.memset(row_d[:, 0:1], 0.0))
            dve.wait_ge(ld_row_u, 32)
            op(dve.tensor_scalar(row_w, row_u, 1.0 / L1_EPS, 1.0, ALU.mult, ALU.min))
            op(dve.tensor_scalar(row_nz, row_u, 0.0, None, ALU.is_gt))
            op(dve.tensor_tensor_scan(row_any, row_nz, row_zero, 0.0, ALU.max, ALU.add))
            op(dve.tensor_copy(row_one[:, 3:S], row_any[:, 0:S - 3]))
            op(dve.tensor_tensor(row_w, row_w, row_one, ALU.max))
            op(dve.tensor_scalar(row_one, row_one, -grow, grow, ALU.mult, ALU.add))
            op(dve.tensor_tensor_scan(row_any, row_one, row_w, 0.0, ALU.mult, ALU.add))
            op(dve.tensor_scalar(row_d[:, 1:S], row_any[:, 0:S - 1], 1.0, DECAY, ALU.min, ALU.mult))
            op(dve.tensor_tensor(row_d, row_d, row_u, ALU.add))
            op(dve.tensor_scalar(row_d, row_d, L1_EPS, None, ALU.max))
            op(dve.reciprocal(row_w, row_d))
            op(dve.tensor_scalar(row_nz, row_w, DECAY, None, ALU.mult))
            dve.tensor_tensor(row_w, row_w, row_rstd, ALU.mult).then_inc(factors_in, 1)

            def scan(b):
                dve.wait_ge(ld_factor, 16 * (b + 1))
                wait(dve, pe_s, C * b)
                wait(dve, dv_y, NK * b)
                for k in range(NK):
                    dve.wait_ge(pe_pre, NK * b + k + 1)
                    dve.scalar_tensor_tensor(relu_b[:, k, :], n_bank[k][:, :], 0.0, factor[:, 1, :], ALU.max, ALU.mult)\
                       .then_inc(dv_relu, 1)
                for k in range(NK):
                    dve.wait_ge(dv_relu, NK * b + k + 1)
                    dve.tensor_tensor_scan(xs[:, k, :], factor[:, 0, :], relu_b[:, k, :], 0.0, ALU.mult, ALU.add)\
                       .then_inc(dv_x, 1)

            def diagonal(b, sc):
                dve.wait_ge(pe_s, C * b + sc + 1)
                wait(dve, pe_a, b)
                dve.tensor_tensor(pm[:, OFF[sc]:OFF[sc] + P], n_bank[sc % 2][:, 0:P], causal_f, ALU.mult)\
                   .then_inc(dv_diag, 1)

            def finish(b):
                dve.wait_ge(pe_fold, b + 1)
                wait(dve, st_out, 16 * b)
                dve.tensor_tensor(o_sb[:], ly_y.rearrange("p (c d) -> p c d", c=C), h_of(b), ALU.add)\
                   .then_inc(dv_out, 1)

            def halves(st, t, w, s):
                s.done(dve.tensor_tensor(t, st[:, :, 1], st[:, :, 4], ALU.subtract))
                s.done(dve.tensor_tensor(w, st[:, :, 2], st[:, :, 5], ALU.add))

            def attn_scale(b, s):
                t, v, q, w = t_a[:, 0, :], t_a[:, 1, :], t_a[:, 2, :], t_a[:, 3, :]
                dve.wait_ge(pe_a, b + 1)
                for c in range(C):
                    s.done(dve.bn_stats(st_a[:, c, :], az_a[:, c, :]))
                s.last()
                halves(st_a, t, w, s)
                s.last()
                s.done(dve.scalar_tensor_tensor(t, t, 0.25, t, ALU.mult, ALU.mult))
                s.done(dve.scalar_tensor_tensor(w, w, 1.0 / D, dec[:, C:2 * C], ALU.mult, ALU.add))
                s.last()
                s.done(dve.tensor_tensor(v, t, w, ALU.add))
                s.last()
                s.done(dve.tensor_scalar(q.bitcast(I32), v.bitcast(I32), -0.5, RSQRT_SEED, ALU.mult, ALU.add))
                s.last()
                wait(dve, po_al, b)
                dve.tensor_tensor(an[:], az_a, wide(q, D), ALU.mult).then_inc(dv_an, 1)
                s.done(dve.tensor_tensor(t, q, q, ALU.mult))
                s.last()
                s.done(dve.scalar_tensor_tensor(v, t, EPS, v, ALU.mult, ALU.mult))

            def gate(b, k):
                dve.wait_ge(pe_y, NK * b + k + 1)
                wait(dve, pe_z, b)
                dve.scalar_tensor_tensor(ys[:, k, :], n_bank[k][:, :], 0.0, xs[:, k, :], ALU.max, ALU.mult)\
                   .then_inc(dv_y, 1)

            def z_stats(b, s):
                dve.wait_ge(ac_z, b + 1)
                for c in range(C):
                    s.done(dve.bn_stats(st_z[:, c, :], z_sb[:, c, :]))

            def z_halves(b, s):
                s.last()
                halves(st_z, t_z[:, 0, :], t_z[:, 1, :], s)

            def z_parts(b, s):
                s.last()
                dve.wait_ge(att_steps, N_ATT * (b + 1))
                t, w = t_z[:, 0, :], t_z[:, 1, :]
                s.done(dve.scalar_tensor_tensor(t, t, 0.25, t, ALU.mult, ALU.mult))
                s.done(dve.scalar_tensor_tensor(w, w, 1.0 / D, t_a[:, 1, :], ALU.mult, ALU.add))

            def z_var(b, s):
                s.last()
                dve.tensor_tensor(t_z[:, 2, :], t_z[:, 0, :], t_z[:, 1, :], ALU.add).then_inc(dv_var_z, 1)

            def residual(b, s):
                dve.wait_ge(po_z_scale, b + 1)
                for c in range(C):
                    h = h_all[:, bass.ds(b * C * D + c * D, D)]
                    s.done(dve.scalar_tensor_tensor(h, z_sb[:, c, :], t_z[:, 3, c:c + 1], h, ALU.mult, ALU.add))

            def h_stats(b, s):
                s.last()
                dve.nop().then_inc(dv_passed, 1)
                for c in range(C):
                    s.done(dve.bn_stats(st_h[:, c, :], h_all[:, bass.ds(b * C * D + c * D, D)]))

            def h_halves(b, s):
                s.last()
                wait(dve, po_xc, b)
                halves(st_h, t_h[:, 0, :], t_h[:, 1, :], s)
                s.done(dve.tensor_tensor(t_h[:, 3, :], st_h[:, :, 1], st_h[:, :, 4], ALU.add))

            def h_parts(b, s):
                s.last()
                t, w = t_h[:, 0, :], t_h[:, 1, :]
                s.done(dve.scalar_tensor_tensor(t, t, 0.25, t, ALU.mult, ALU.mult))
                s.done(dve.tensor_scalar(w, w, (1.0 + EPS) / D, EPS * EPS, ALU.mult, ALU.add))
                s.done(dve.tensor_scalar(h_mean[:], t_h[:, 3, :], 0.5, None, ALU.mult))

            def h_var(b, s):
                s.last()
                dve.scalar_tensor_tensor(t_h[:, 2, :], t_h[:, 0, :], 1.0 + EPS, t_h[:, 1, :], ALU.mult, ALU.add)\
                   .then_inc(dv_h, 1)

            def logit_sum(b, s):
                dve.wait_ge(pe_lg, b + 1)
                dve.tensor_reduce(lg[:], ly_lg.rearrange("p (c k e) -> p c e k", c=C, k=PIECES), AX_X, ALU.add)\
                   .then_inc(dv_lg, 1)

            def logit_bias(b, s):
                dve.wait_ge(dv_lg, b + 1)
                s.done(dve.tensor_tensor(lg[:], lg[:], br_sb[:].unsqueeze(1).to_broadcast([P, C, E]), ALU.add))

            def largest(b, s):
                s.last()
                dve.nop().then_inc(dv_passed, 1)
                for c in range(C):
                    s.done(dve.max(top[:, c, :], lg[:, c, :]))

            def which(b, s):
                s.last()
                dve.tensor_tensor(gap[:], top[:, :, 0], top[:, :, 1], ALU.subtract).then_inc(dv_gap, 1)
                for c in range(C):
                    s.done(dve.max_index(top_i[:, c, :], top[:, c, :], lg[:, c, :]))

            def one_hot(b, s):
                s.last()
                iota = dec[:, 2 * C:2 * C + E].unsqueeze(1).to_broadcast([P, C, E])
                for k in range(2):
                    s.done(dve.tensor_tensor(pick[:, k], iota, wide(top_i[:, :, k], E), ALU.is_equal))

            def softmax(b, s):
                dve.wait_ge(ac_tanh, b + 1)
                s.done(dve.tensor_scalar(wgt[:, 0, :], tanh_g[:], 0.5, 0.5, ALU.mult, ALU.add))
                s.done(dve.tensor_scalar(wgt[:, 1, :], tanh_g[:], -0.5, 0.5, ALU.mult, ALU.add))

            def place(b, s):
                s.last()
                s.done(dve.tensor_tensor(pick[:].rearrange("p k c e -> p (k c) e"),
                                         pick[:].rearrange("p k c e -> p (k c) e"),
                                         wide(wgt[:].rearrange("p k c -> p (k c)"), E), ALU.mult))

            def merge(b, s):
                s.last()
                s.done(dve.tensor_tensor(pick[:, 0], pick[:, 0], pick[:, 1], ALU.add))

            def weight_high(b, s):
                s.last()
                wait(dve, pe_wT2, b)
                s.done(dve.tensor_copy(w_p[:, :, 0:E], pick[:, 0]))

            def weight_low(b, s):
                s.last()
                dve.tensor_tensor(w_p[:, :, E:2 * E], pick[:, 0], w_p[:, :, 0:E], ALU.subtract).then_inc(dv_w, 1)

            def weigh(b, q):
                dve.wait_ge(pe_zz, NP * b + q + 1)
                dve.wait_ge(ac_wb, NP * b + q + 1)
                wait(dve, po_acc, b)
                dve.scalar_tensor_tensor(tm[:, q, :], zb[:, :], b2_pair[:, q:q + 1], wb[:, q, :], ALU.add, ALU.mult)\
                   .then_inc(dv_tm, 1)

            def turn(i, att, res, mlp, done, ahead):
                r, k = i - 1, i - 2
                a = Steps(dve, att_steps, N_ATT * i)
                n = Steps(dve, res_steps, N_RES * r)
                m = Steps(dve, mlp_steps, N_MLP * k)
                for of_router, of_norm in ((logit_sum, z_stats), (logit_bias, z_halves), (largest, z_parts)):
                    if mlp:
                        of_router(k, m)
                    if res:
                        of_norm(r, n)
                if att:
                    diagonal(i, 0)
                if mlp:
                    which(k, m)
                if res:
                    z_var(r, n)
                if mlp:
                    one_hot(k, m)
                if att:
                    diagonal(i, 1)
                if mlp:
                    softmax(k, m)
                if res:
                    residual(r, n)
                if mlp:
                    place(k, m)
                if att:
                    diagonal(i, 2)
                if res:
                    h_stats(r, n)
                if mlp:
                    merge(k, m)
                if att:
                    diagonal(i, 3)
                if res:
                    h_halves(r, n)
                if mlp:
                    weight_high(k, m)
                if res:
                    h_parts(r, n)
                if mlp:
                    weight_low(k, m)
                if res:
                    h_var(r, n)
                if att:
                    attn_scale(i, a)
                if mlp:
                    weigh(k, 0)
                if done:
                    finish(i - 3)
                if mlp:
                    weigh(k, 1)
                if att:
                    gate(i, 0)
                    gate(i, 1)
                if mlp:
                    weigh(k, 2)
                if ahead:
                    scan(i + 1)
                if mlp:
                    weigh(k, 3)
                assert a.n in (0, N_ATT) and n.n in (0, N_RES) and m.n in (0, N_MLP), (a.n, n.n, m.n)

            scan(0)
            turn(0, True, False, False, False, True)
            turn(1, True, True, False, False, True)
            turn(2, True, True, True, False, True)
            with dve.Fori(0, B // 2 - 2) as two:
                turn(2 * two + 3, True, True, True, True, True)
                turn(2 * two + 4, True, True, True, True, True)
            turn(B - 1, True, True, True, True, False)
            turn(B, False, True, True, True, False)
            turn(B + 1, False, False, True, True, False)
            finish(B - 1)

        @block.tensor
        def _(pe):
            pe.wait_ge(ld_c, 48)
            pe.wait_ge(ints_f, 2)
            pe.transpose(bank[1][:, 0:P], xf[:], ident_f[:])
            pe.transpose(bank[1][:, P:2 * P], rf[:], ident_f[:]).then_inc(pe_tok_T, 1)
            pe.wait_ge(ld_w, 16 * 9)
            pe.transpose(bank[2][0:D, 0:D], proj_sb[:], ident_f[0:D, 0:D])
            for k in range(NK):
                last = pe.transpose(bank[2][0:D, D + k * P:D + (k + 1) * P], dx_sb[:, k, :], ident_f[:])
            last.then_inc(pe_wT, 1)

            pe.wait_ge(projT_in, 1)
            pe.wait_ge(ids_ready, 3)
            pe.matmul(bank[3][0:NF, 0:D], s4[:], projT[:], start=True, stop=False)
            pe.matmul(bank[3][0:NF, 0:D], ones_row[:], projb[:], start=False, stop=True).then_inc(pe_tab, 1)
            pe.wait_ge(tab_c_in, 1)
            pe.transpose(bank[3][0:D, D:D + NF], table_c[:], ident_f[0:NF, 0:NF]).then_inc(pe_tabT, 1)
            pe.wait_ge(tabT_in, 1)
            pe.matmul(bank[3][0:NF, P:P + NS], table_cT[:], dxT[:], start=True, stop=True).then_inc(pe_g, 1)
            pe.wait_ge(ld_w2, 16 * 6)
            pe.wait_ge(ld_w3, 16 * 6)
            pe.wait_ge(wide_beta, 1)
            for e in range(E):
                pe.matmul(bank[5][:, e:e + 1], w1_sb[:, e, :], bet[:], start=True, stop=True)
            pe.matmul(bank[5][:, E:2 * E], bet_wide[:], wr_sb[0:D, :], start=True, stop=True)
            pe.transpose(bank[5][:, 16:24], b1_sb[:], ident_f[0:E, 0:E])
            pe.transpose(bank[5][:, 24:24 + NP], b2_sb[:], ident_f[0:NP, 0:NP])
            for k in range(NK):
                pe.transpose(bank[5][:, P + k * D:P + (k + 1) * D], e_sb[:, k * P:(k + 1) * P], ident_f[0:D, 0:D])
            pe.wait_ge(gammas_in, 1)
            for e in range(E):
                last = pe.transpose(bank[6][:, e * D:(e + 1) * D], w1g[:, e, :], ident_f[0:D, 0:D])
            last.then_inc(pe_bias, 1)
            pe.wait_ge(parts_in, 1)
            for part in range(2):
                for e in range(E):
                    pe.transpose(bank[2 + part][:, :].bitcast(F16)[:, e * P:(e + 1) * P],
                                 w1_p[:, part, e].rearrange("h u d -> h (u d)"), ident_h[:])
                for k in range(NK):
                    at = (part * NK + k) * P
                    last = pe.transpose(bank[4][:, :].bitcast(F16)[:, at:at + P],
                                        dy_p[:, part, k].rearrange("n u d -> n (u d)"), ident_h[:])
            last.then_inc(pe_parts, 1)

            def count(b, side):
                pe.wait_ge(same_in, b + 1)
                for tc in range(C):
                    for sc in range(tc + 1):
                        at = sc * S + P * tc
                        last = pe.matmul(bank[0][:, bass.ds((b * C + tc) * 4, 4)], same[:, side, at:at + P],
                                         right_parts[:, bass.ds(b * C + sc, 1), :].rearrange("p o k -> p (o k)"),
                                         start=(sc == 0), stop=(sc == tc))
                last.then_inc(pe_counts, 1)

            pe.wait_ge(tok_in, 1)
            with pe.Fori(0, B // 2) as pair:
                count(2 * pair, 0)
                count(2 * pair + 1, 1)

            def features(g, side):
                wait(pe, featT_in, g - 1)
                for n in range(GROUP):
                    last = pe.transpose(feat_bank[side][:, :].bitcast(BF16)[:, n * P:(n + 1) * P],
                                        feat_parts[:, bass.ds(g * GROUP + n, 1), :].rearrange("p o k -> p (o k)"),
                                        ident_b[:])
                last.then_inc(pe_featT, 1)

            def group(g, side):
                pe.wait_ge(featT_in, g + 1)
                wait(pe, h0_bn, GROUP * (g - 1))
                for n in range(GROUP):
                    last = pe.matmul(h0_bank[side][:, n * D:(n + 1) * D], feat_k[:, bass.ds((g * GROUP + n) * P, P)],
                                     table_k[:, 0:D], start=True, stop=True)
                last.then_inc(pe_h0, 1)
                for n in range(GROUP // 2):
                    if n < GROUP // 2 - 1:
                        wait(pe, sum_a, (GROUP - 2) * g + (2 * n + 2 - (GROUP - 2)) if not isinstance(g, int) or g
                             else 0)
                    else:
                        wait(pe, sum_v, 2 * g)
                    for k in range(2):
                        last = pe.matmul(bank[2 + n][:, k * NS:(k + 1) * NS],
                                         feat_k[:, bass.ds((g * GROUP + 2 * n + k) * P, P)],
                                         table_k[:, D:D + NS], start=True, stop=True)
                    last.then_inc(pe_g2, 1)

            pe.wait_ge(feats_in, 1)
            pe.wait_ge(weights_in, 1)
            pe.wait_ge(ld_table, 16 * PIECES * PIECES)
            features(0, 0)
            features(1, 1)
            group(0, 0)
            features(2, 0)
            group(1, 1)
            with pe.Fori(1, NG // 2 - 1) as pair:
                features(2 * pair + 1, 1)
                group(2 * pair, 0)
                features(2 * pair + 2, 0)
                group(2 * pair + 1, 1)
            features(NG - 1, 1)
            group(NG - 2, 0)
            group(NG - 1, 1)
            pe.wait_ge(upd_in, 1)
            pe.transpose(bank[1][:, 0:P], upd_sum[:], ident_f[:])
            pe.transpose(bank[1][:, P:2 * P], rstd[:], ident_f[:]).then_inc(pe_updT, 1)
            def update(b):
                for k in range(NK):
                    wait(pe, dv_y, NK * b + (k + 1 - NK))
                    pe.matmul(n_bank[k][:, :], table_k[:, D + k * P:D + (k + 1) * P],
                              feat_k[:, bass.ds(b * S, S)], start=True, stop=True).then_inc(pe_pre, 1)

            def scores(b, sc):
                if sc == 0:
                    pe.wait_ge(dv_x, NK * (b + 1))
                if sc >= 2:
                    pe.wait_ge(dv_diag, C * b + sc - 1)
                    pe.wait_ge(ac_off, (C - 1) * b + sc - 1)
                for k in range(NK):
                    last = pe.matmul(n_bank[sc % 2][:, 0:WIDE[sc]], xs[:, k, sc * P:(sc + 1) * P],
                                     xs[:, k, sc * P:S], start=(k == 0), stop=(k == NK - 1))
                last.then_inc(pe_s, 1)

            def values(b):
                pe.wait_ge(po_ub, b + 1)
                wait(pe, ac_z, b)
                for tc in range(C):
                    pe.wait_ge(dv_diag, C * b + tc + 1)
                    if tc:
                        pe.wait_ge(ac_off, (C - 1) * b + tc)
                    for sc in range(tc + 1):
                        at = OFF[sc] + P * (tc - sc)
                        last = pe.matmul(az[:, tc * D:(tc + 1) * D], pm[:, at:at + P], ub[:, sc, :],
                                         start=(sc == 0), stop=(sc == tc))
                last.then_inc(pe_a, 1)

            def attn_T(b):
                pe.wait_ge(po_al, b + 1)
                pe.wait_ge(ac_ah, b + 1)
                wait(pe, ac_wT, b - 1)
                wait(pe, dv_out, b - 2)
                for c in range(C):
                    last = pe.transpose(ly_w[:, c * P:(c + 1) * P], a_p[:, c, :], ident_h[:])
                last.then_inc(pe_aT, 1)

            def y_core(b):
                pe.wait_ge(ac_aT, b + 1)
                for k in range(NK):
                    pe.matmul(n_bank[k][:, :], dyT[:, 0, k * P:(k + 1) * P], aT[:], start=True, stop=False)
                    pe.matmul(n_bank[k][:, :], dyT[:, 1, k * P:(k + 1) * P], aT[:], start=False, stop=True)\
                      .then_inc(pe_y, 1)

            def z_out(b, chunks):
                pe.wait_ge(dv_y, NK * (b + 1))
                for c in chunks:
                    for k in range(NK):
                        last = pe.matmul(az[:, (C + c) * D:(C + c + 1) * D], ys[:, k, c * P:(c + 1) * P], eT[:, k, :],
                                         start=(k == 0), stop=(k == NK - 1))
                if c == C - 1:
                    last.then_inc(pe_z, 1)

            def centred_T(b):
                pe.wait_ge(po_xl, b + 1)
                wait(pe, ac_wb, NP * b)
                for c in range(C):
                    last = pe.transpose(tp_h[:, c * P:(c + 1) * P], x_p[:, c, :], ident_h[:])
                last.then_inc(pe_xT, 1)

            def logits(b, att):
                pe.wait_ge(ac_xT, b + 1)
                if att:
                    pe.wait_ge(ac_aT, b + 2)
                else:
                    pe.wait_ge(ac_wT, b)
                    pe.wait_ge(dv_out, b - 1)
                n = PIECES * E
                for c in range(C):
                    last = pe.matmul(ly[:, c * n:(c + 1) * n], xT[:, c * P:(c + 1) * P],
                                     wr_p[:].rearrange("p k e -> p (k e)"), start=True, stop=True)
                last.then_inc(pe_lg, 1)

            def hidden(b, e):
                pe.wait_ge(ac_xT, b + 1)
                wait(pe, ac_gelu, E * b + e - 1)
                pe.matmul(h_bank[e % 2][:, :], w1k[:, 0, e, :], xT[:], start=True, stop=False)
                pe.matmul(h_bank[e % 2][:, :], w1k[:, 1, e, :], xT[:], start=False, stop=True).then_inc(pe_hid, 1)

            def expert_out(b, q):
                pe.wait_ge(ac_gelu, E * b + 2 * q + 2)
                wait(pe, dv_tm, NP * b + q)
                pe.matmul(zb[0:D, :], w2_sb[:, 2 * q, :], hid[:, 2 * q, :], start=True, stop=True)
                pe.matmul(zb[D:P, :], w2_sb[:, 2 * q + 1, :], hid[:, 2 * q + 1, :], start=True, stop=True)\
                  .then_inc(pe_zz, 1)

            def weights_T(b):
                pe.wait_ge(dv_w, b + 1)
                wait(pe, dv_out, b - 1)
                for c in range(C):
                    last = pe.transpose(ly_w[0:2 * E, c * P:(c + 1) * P], w_p[:, c, :], ident_h[:])
                last.then_inc(pe_wT2, 1)

            def weights_wide(b, q):
                if q == 0:
                    pe.wait_ge(ac_wT, b + 1)
                wait(pe, ac_wb, NP * b + q)
                pe.matmul(tp[:, :], sel[:, q, :], wT[:], start=True, stop=True).then_inc(pe_wb, 1)

            def fold(b):
                pe.wait_ge(po_acc, b + 1)
                if isinstance(b, int):
                    pe.wait_ge(ac_wT, min(b + 2, B))
                else:
                    pe.wait_ge(ac_wT, b + 2)
                for c in range(C):
                    last = pe.matmul(ly[:, 256 + c * D:256 + (c + 1) * D], acc[:, c * P:(c + 1) * P], fold_f[:],
                                     start=True, stop=True)
                last.then_inc(pe_fold, 1)

            def turn(i, att, res, mlp, done, ahead):
                r, k = i - 1, i - 2
                if att:
                    scores(i, 0)
                if mlp:
                    hidden(k, 0)
                if att:
                    scores(i, 1)
                if mlp:
                    hidden(k, 1)
                if att:
                    scores(i, 2)
                    scores(i, 3)
                if mlp:
                    hidden(k, 2)
                if att:
                    values(i)
                if mlp:
                    weights_T(k)
                    hidden(k, 3)
                    expert_out(k, 0)
                    weights_wide(k, 0)
                if done:
                    fold(i - 3)
                if mlp:
                    hidden(k, 4)
                    weights_wide(k, 1)
                    hidden(k, 5)
                if att:
                    attn_T(i)
                if mlp:
                    expert_out(k, 1)
                    hidden(k, 6)
                if att:
                    y_core(i)
                if mlp:
                    weights_wide(k, 2)
                    hidden(k, 7)
                    expert_out(k, 2)
                    weights_wide(k, 3)
                if ahead:
                    update(i + 1)
                if att:
                    z_out(i, range(0, C // 2))
                if res:
                    centred_T(r)
                if att:
                    z_out(i, range(C // 2, C))
                if mlp:
                    expert_out(k, 3)
                if res:
                    logits(r, att)

            pe.wait_ge(sel_ready, 1)
            pe.wait_ge(updT_in, 1)
            update(0)
            turn(0, True, False, False, False, True)
            turn(1, True, True, False, False, True)
            turn(2, True, True, True, False, True)
            with pe.Fori(0, B // 2 - 2) as two:
                turn(2 * two + 3, True, True, True, True, True)
                turn(2 * two + 4, True, True, True, True, True)
            turn(B - 1, True, True, True, True, False)
            turn(B, False, True, True, True, False)
            turn(B + 1, False, False, True, True, False)
            fold(B - 1)


_INS = ["x", "mask_BS_i0_1", "L0_tok_skill_w", "L0_tok_skill_b", "L0_tok_att_w", "L0_tok_att_b", "L0_tok_mast_w",
        "L0_tok_mast_b", "L0_tok_proj_w", "L0_tok_proj_b", "L0_attn_E", "L0_attn_Dx", "L0_attn_Dy", "L0_ffn_gamma",
        "L0_ffn_beta", "L0_ffn_Wr", "L0_ffn_br", "L0_ffn_W1", "L0_ffn_b1", "L0_ffn_W2", "L0_ffn_b2"]


def constants():
    row, col = np.arange(P)[:, None], np.arange(P)[None, :]
    t = (np.arange(P)[:, None] + P * np.arange(C)[None, :]).astype(np.float64)
    decays = np.concatenate([DECAY ** (-1.0 - t), EPS * DECAY ** (-2.0 * t), np.tile(np.arange(E), (P, 1))], axis=1)
    return {
        "ident": np.eye(P, dtype=np.float32),
        "masks": np.concatenate([row <= col, row < col], axis=1).astype(np.float32),
        "decays": decays.astype(np.float32),
    }


def kernel(**inputs):
    import concourse.bacc as _bacc
    from concourse.bass_utils import run_bass_kernel_spmd as _run

    nc = _bacc.Bacc("TRN2", target_bir_lowering=False, num_devices=1)
    arrays, args = {}, []
    named = [(name, np.ascontiguousarray(inputs[name])) for name in _INS] + list(constants().items())
    for name, a in named:
        arrays[f"in_{name}"] = a
        args.append(nc.dram_tensor(f"in_{name}", a.shape, mybir.dt.from_np(a.dtype), kind="ExternalInput").ap())
    args.append(nc.dram_tensor("out_0", (B, S, D), F32, kind="ExternalOutput").ap())
    program(nc, *args)
    r = _run(nc, [arrays], core_ids=[0])
    return r.results[0]["out_0"]
```
